# Optimizing a Trainium2 kernel written in Bass

```python
import numpy as np
import jax
import jax.numpy as jnp

def _softmax(x, axis=-1):
    return jax.nn.softmax(x, axis=axis)

def _gelu(x):
    return jax.nn.gelu(x, approximate=True)

def _silu(x):
    return jax.nn.silu(x)

def _sigmoid(x):
    return jax.nn.sigmoid(x)

def _layernorm(x, axis=-1, eps=1e-05):
    m = jnp.mean(x, axis=axis, keepdims=True)
    v = jnp.var(x, axis=axis, keepdims=True)
    return (x - m) / jnp.sqrt(v + eps)

def _scatter_add(tgt, idx, src, axis=0):
    return tgt.at[idx].add(src)

def _segment_sum(src, seg, n):
    return jax.ops.segment_sum(src, seg, n)
kernel_name = 'mk_decoder_postln_d2_seqx_r4_a71d5a'

def setup_inputs(seed: int=0):
    np.random.seed(seed)
    _w = jnp.asarray

    def _rec_inputs():
        import jax
        import jax.numpy as jnp
        _rk = jax.random.key(seed)
        x = 7.22e-05 + 1 * jax.random.normal(jax.random.fold_in(_rk, 1), (32, 128, 512), jnp.float32)
        _lenS = 128 - jax.random.randint(jax.random.fold_in(_rk, 7), (32,), 0, max(1, 128 // 4) + 1, jnp.int32)
        _lenS2 = 128 - jax.random.randint(jax.random.fold_in(_rk, 8), (32,), 0, max(1, 128 // 4) + 1, jnp.int32)
        _ctx_512P = jax.random.normal(jax.random.fold_in(_rk, 11), (32, 16, 128), jnp.float32)
        _ctx_512c = jax.random.dirichlet(jax.random.fold_in(_rk, 511), 0.3 * jnp.ones((16,), jnp.float32), (32, 128))
        _ctx_512t = jnp.einsum('bsk,bkd->bsd', _ctx_512c, _ctx_512P)
        _ctx_512t = _ctx_512t * jax.lax.rsqrt(jnp.mean(jnp.square(_ctx_512t)) + 1e-12) * 0.953939
        ctx_512 = -0.000514642 + 1.00011 * (_ctx_512t + 0.3 * jax.random.normal(jax.random.fold_in(_rk, 611), (32, 128, 128), jnp.float32))
        return (x, ctx_512)
    x, ctx_512 = _rec_inputs()

    def _L0_attn_setup():
        import jax, jax.numpy as jnp
        import numpy as np
        D_MODEL = 512
        B, L = (4, 512)

        def _dwconv(x, w, b):
            y = jax.lax.conv_general_dilated(x, w, window_strides=(1,), padding=[(2, 0)], feature_group_count=x.shape[1], dimension_numbers=('NCH', 'OIH', 'NCH'))
            return y + b[None, :, None]
        key = jax.random.key(seed)
        ks = jax.random.split(key, 12)
        D = D_MODEL
        s = 0.02
        inp = {'u': jax.random.normal(ks[0], (B, L, D), jnp.float32), 'Wq': jax.random.normal(ks[1], (D, D), jnp.float32) * s, 'bq': jnp.zeros((D,), jnp.float32), 'Wk': jax.random.normal(ks[2], (D, D), jnp.float32) * s, 'bk': jnp.zeros((D,), jnp.float32), 'Wv': jax.random.normal(ks[3], (D, D), jnp.float32) * s, 'bv': jnp.zeros((D,), jnp.float32), 'convq_w': jax.random.normal(ks[4], (D, 1, 3), jnp.float32) * 0.5, 'convq_b': jnp.zeros((D,), jnp.float32), 'convk_w': jax.random.normal(ks[5], (D, 1, 3), jnp.float32) * 0.5, 'convk_b': jnp.zeros((D,), jnp.float32), 'ssm_kernel': jax.random.normal(ks[6], (D, L), jnp.float32) * 0.01, 'D_skip': jax.random.normal(ks[7], (D,), jnp.float32), 'Wo': jax.random.normal(ks[8], (D, D), jnp.float32) * s, 'bo': jnp.zeros((D,), jnp.float32)}
        return inp
    _L0_attn_all = _L0_attn_setup()
    _L0_attn_in = {k: v for k, v in _L0_attn_all.items() if k in ('Wq', 'bq', 'Wk', 'bk', 'Wv', 'bv', 'convq_w', 'convq_b', 'convk_w', 'convk_b', 'ssm_kernel', 'D_skip', 'Wo', 'bo')}
    del _L0_attn_all

    def _L0_xattn_setup():
        import jax, jax.numpy as jnp
        import numpy as np
        import math
        NUM_Q_HEADS = 32
        NUM_KV_HEADS = 8
        key = jax.random.key(seed)
        k1, k2, k3 = jax.random.split(key, 3)
        B, S, E = (2, 512, 512)
        kv_E = NUM_KV_HEADS * (E // NUM_Q_HEADS)
        q = jax.random.normal(k1, (B, S, E), dtype=jnp.float32)
        k = jax.random.normal(k2, (B, S, kv_E), dtype=jnp.float32)
        v = jax.random.normal(k3, (B, S, kv_E), dtype=jnp.float32)
        return {'q': q, 'k': k, 'v': v}
    _L0_xattn_all = _L0_xattn_setup()
    _L0_xattn_in = {k: v for k, v in _L0_xattn_all.items() if k in ()}
    del _L0_xattn_all

    def _L0_ffn_setup():
        import jax, jax.numpy as jnp
        import numpy as np
        key = jax.random.key(seed)
        k1, k2, k3, k4, k5 = jax.random.split(key, 5)
        B, L, H, N = (2, 512, 512, 2048)
        x = jax.random.normal(k1, (B, L, H), dtype=jnp.float32)
        W0 = jax.random.normal(k2, (N, H), dtype=jnp.float32) * (1.0 / np.sqrt(H))
        bias0 = jax.random.normal(k3, (N,), dtype=jnp.float32) * 0.02
        W1 = jax.random.normal(k4, (H, N), dtype=jnp.float32) * (1.0 / np.sqrt(N))
        bias1 = jax.random.normal(k5, (H,), dtype=jnp.float32) * 0.02
        return {'x': x, 'W0': W0, 'bias0': bias0, 'W1': W1, 'bias1': bias1}
    _L0_ffn_all = _L0_ffn_setup()
    _L0_ffn_in = {k: v for k, v in _L0_ffn_all.items() if k in ('W0', 'bias0', 'W1', 'bias1')}
    del _L0_ffn_all

    def _L1_attn_setup():
        import jax, jax.numpy as jnp
        import numpy as np
        B, T, D_MODEL = (4, 1024, 512)
        D_LATENT = 128
        D_COMP = 64
        THETA = 10000.0
        LN_EPS = 1e-05

        def _rope_tables(seq_len: int, dim: int):
            inv_freq = 1.0 / THETA ** (jnp.arange(0, dim, 2, dtype=jnp.float32) / dim)
            freqs = jnp.arange(seq_len, dtype=jnp.float32)[:, None] * inv_freq[None, :]
            cos = jnp.concatenate([jnp.cos(freqs), jnp.cos(freqs)], axis=-1)
            sin = jnp.concatenate([jnp.sin(freqs), jnp.sin(freqs)], axis=-1)
            return (cos, sin)

        def _rotate_half(x):
            x1, x2 = jnp.split(x, 2, axis=-1)
            return jnp.concatenate([-x2, x1], axis=-1)
        key = jax.random.key(seed)
        ks = jax.random.split(key, 8)
        s = 0.02
        return {'x': jax.random.normal(ks[0], (B, T, D_MODEL), dtype=jnp.float32), 'W_to_kv': jax.random.normal(ks[1], (D_LATENT, D_MODEL), dtype=jnp.float32) * s, 'W_compress': jax.random.normal(ks[2], (D_COMP, D_LATENT), dtype=jnp.float32) * s, 'ln_gamma': jnp.ones((D_COMP,), dtype=jnp.float32), 'ln_beta': jnp.zeros((D_COMP,), dtype=jnp.float32), 'W_q_comp': jax.random.normal(ks[3], (D_COMP, D_COMP), dtype=jnp.float32) * s, 'W_kv_comp': jax.random.normal(ks[4], (2 * D_COMP, D_COMP), dtype=jnp.float32) * s, 'W_comp2lat': jax.random.normal(ks[5], (D_LATENT, D_COMP), dtype=jnp.float32) * s, 'W_out_res': jnp.zeros((D_MODEL, D_LATENT), dtype=jnp.float32), 'b_out_res': jnp.zeros((D_MODEL,), dtype=jnp.float32)}
    _L1_attn_all = _L1_attn_setup()
    _L1_attn_in = {k: v for k, v in _L1_attn_all.items() if k in ('W_to_kv', 'W_compress', 'ln_gamma', 'ln_beta', 'W_q_comp', 'W_kv_comp', 'W_comp2lat', 'W_out_res', 'b_out_res')}
    del _L1_attn_all

    def _L1_xattn_setup():
        import jax, jax.numpy as jnp
        import numpy as np
        B, S, E = (2, 512, 512)
        QH, KVH = (32, 8)
        D = E // QH
        G = QH // KVH
        DROPOUT = 1.0
        key = jax.random.key(seed)
        k1, k2, k3 = jax.random.split(key, 3)
        q = jax.random.normal(k1, (B, S, E), dtype=jnp.float32)
        k = jax.random.normal(k2, (B, S, E // G), dtype=jnp.float32)
        v = jax.random.normal(k3, (B, S, E // G), dtype=jnp.float32)
        return {'q': q, 'k': k, 'v': v}
    _L1_xattn_all = _L1_xattn_setup()
    _L1_xattn_in = {k: v for k, v in _L1_xattn_all.items() if k in ()}
    del _L1_xattn_all

    def _L1_ffn_setup():
        import jax, jax.numpy as jnp
        import numpy as np
        N_EXPERTS = 8
        TOP_K = 2
        D_MODEL = 512
        D_FF = 256
        BATCH, SEQ = (2, 512)

        def _trunc_normal(key, shape, fan_in):
            std = jnp.sqrt(1.0 / 3.0) / jnp.sqrt(float(fan_in))
            return jax.random.truncated_normal(key, -2.0, 2.0, shape, dtype=jnp.float32) * std
        key = jax.random.key(seed)
        kx, kr, k1, k2, k3 = jax.random.split(key, 5)
        x = jax.random.normal(kx, (BATCH, SEQ, D_MODEL), dtype=jnp.float32)
        router_w = jax.random.uniform(kr, (N_EXPERTS, D_MODEL), dtype=jnp.float32, minval=-1.0, maxval=1.0) / jnp.sqrt(float(D_MODEL))
        w1 = _trunc_normal(k1, (N_EXPERTS, D_MODEL, D_FF), D_MODEL)
        w2 = _trunc_normal(k2, (N_EXPERTS, D_MODEL, D_FF), D_MODEL)
        w3 = _trunc_normal(k3, (N_EXPERTS, D_FF, D_MODEL), D_FF)
        return {'x': x, 'router_w': router_w, 'w1': w1, 'w2': w2, 'w3': w3}
    _L1_ffn_all = _L1_ffn_setup()
    _L1_ffn_in = {k: v for k, v in _L1_ffn_all.items() if k in ('router_w', 'w1', 'w2', 'w3')}
    del _L1_ffn_all
    return {'x': x, 'ctx_512': ctx_512, 'L0_attn_Wq': _L0_attn_in['Wq'], 'L0_attn_bq': _L0_attn_in['bq'], 'L0_attn_Wk': _L0_attn_in['Wk'], 'L0_attn_bk': _L0_attn_in['bk'], 'L0_attn_Wv': _L0_attn_in['Wv'], 'L0_attn_bv': _L0_attn_in['bv'], 'L0_attn_convq_w': _L0_attn_in['convq_w'], 'L0_attn_convq_b': _L0_attn_in['convq_b'], 'L0_attn_convk_w': _L0_attn_in['convk_w'], 'L0_attn_convk_b': _L0_attn_in['convk_b'], 'L0_attn_ssm_kernel': _L0_attn_in['ssm_kernel'], 'L0_attn_D_skip': _L0_attn_in['D_skip'], 'L0_attn_Wo': _L0_attn_in['Wo'], 'L0_attn_bo': _L0_attn_in['bo'], 'L0_ffn_W0': _L0_ffn_in['W0'], 'L0_ffn_bias0': _L0_ffn_in['bias0'], 'L0_ffn_W1': _L0_ffn_in['W1'], 'L0_ffn_bias1': _L0_ffn_in['bias1'], 'L1_attn_W_to_kv': _L1_attn_in['W_to_kv'], 'L1_attn_W_compress': _L1_attn_in['W_compress'], 'L1_attn_ln_gamma': _L1_attn_in['ln_gamma'], 'L1_attn_ln_beta': _L1_attn_in['ln_beta'], 'L1_attn_W_q_comp': _L1_attn_in['W_q_comp'], 'L1_attn_W_kv_comp': _L1_attn_in['W_kv_comp'], 'L1_attn_W_comp2lat': _L1_attn_in['W_comp2lat'], 'L1_attn_W_out_res': _L1_attn_in['W_out_res'], 'L1_attn_b_out_res': _L1_attn_in['b_out_res'], 'L1_ffn_router_w': _L1_ffn_in['router_w'], 'L1_ffn_w1': _L1_ffn_in['w1'], 'L1_ffn_w2': _L1_ffn_in['w2'], 'L1_ffn_w3': _L1_ffn_in['w3']}

def reference(x, ctx_512, L0_attn_Wq, L0_attn_bq, L0_attn_Wk, L0_attn_bk, L0_attn_Wv, L0_attn_bv, L0_attn_convq_w, L0_attn_convq_b, L0_attn_convk_w, L0_attn_convk_b, L0_attn_ssm_kernel, L0_attn_D_skip, L0_attn_Wo, L0_attn_bo, L0_ffn_W0, L0_ffn_bias0, L0_ffn_W1, L0_ffn_bias1, L1_attn_W_to_kv, L1_attn_W_compress, L1_attn_ln_gamma, L1_attn_ln_beta, L1_attn_W_q_comp, L1_attn_W_kv_comp, L1_attn_W_comp2lat, L1_attn_W_out_res, L1_attn_b_out_res, L1_ffn_router_w, L1_ffn_w1, L1_ffn_w2, L1_ffn_w3):
    import jax
    import jax.numpy as jnp

    def _L0_attn_ref(u, Wq, bq, Wk, bk, Wv, bv, convq_w, convq_b, convk_w, convk_b, ssm_kernel, D_skip, Wo, bo):
        import jax, jax.numpy as jnp
        import numpy as np
        D_MODEL = 512
        B, L = (4, 512)

        def _dwconv(x, w, b):
            y = jax.lax.conv_general_dilated(x, w, window_strides=(1,), padding=[(2, 0)], feature_group_count=x.shape[1], dimension_numbers=('NCH', 'OIH', 'NCH'))
            return y + b[None, :, None]
        Lq = u.shape[1]
        fft_size = 2 * Lq
        q = jnp.einsum('blh,eh->ble', u, Wq) + bq
        k = jnp.einsum('blh,eh->ble', u, Wk) + bk
        v = jnp.einsum('blh,eh->ble', u, Wv) + bv
        q = jnp.transpose(q, (0, 2, 1))
        k = jnp.transpose(k, (0, 2, 1))
        v = jnp.transpose(v, (0, 2, 1))
        q = _dwconv(q, convq_w, convq_b)
        k = _dwconv(k, convk_w, convk_b)
        kv = k * v
        kv_f = jnp.fft.rfft(kv, n=fft_size)
        kernel_f = jnp.fft.rfft(ssm_kernel, n=fft_size)
        y = jnp.fft.irfft(kv_f * kernel_f, n=fft_size)[..., :Lq]
        y = (y + kv * D_skip[None, :, None]) * q
        y = jnp.transpose(y, (0, 2, 1))
        return jnp.einsum('blh,eh->ble', y, Wo) + bo

    def _L0_xattn_ref(q, k, v):
        import jax, jax.numpy as jnp
        import numpy as np
        import math
        NUM_Q_HEADS = 32
        NUM_KV_HEADS = 8
        B, S, E = q.shape
        H, KV = (NUM_Q_HEADS, NUM_KV_HEADS)
        D = E // H
        G = H // KV
        scale = math.sqrt(D)
        qh = q.reshape(B, S, KV, G, D).transpose(0, 2, 3, 1, 4)
        kh = k.reshape(B, S, KV, D).transpose(0, 2, 1, 3)
        vh = v.reshape(B, S, KV, D).transpose(0, 2, 1, 3)
        scores = jnp.einsum('bkgsd,bktd->bkgst', qh, kh) / scale
        weights = jax.nn.softmax(scores, axis=-1)
        out = jnp.einsum('bkgst,bktd->bkgsd', weights, vh)
        return out.transpose(0, 3, 1, 2, 4).reshape(B, S, E)

    def _L0_ffn_ref(x, W0, bias0, W1, bias1):
        import jax, jax.numpy as jnp
        import numpy as np
        B, L, H = x.shape
        X = x.reshape(-1, H).astype(jnp.float16)
        D = jnp.dot(X.astype(jnp.float32), W0.T) + bias0
        D = jax.nn.gelu(D, approximate=False).astype(jnp.float16)
        E = jnp.dot(D.astype(jnp.float32), W1.T) + bias1
        return E.astype(jnp.float16).reshape(B, L, H)

    def _L1_attn_ref(x, W_to_kv, W_compress, ln_gamma, ln_beta, W_q_comp, W_kv_comp, W_comp2lat, W_out_res, b_out_res):
        import jax, jax.numpy as jnp
        import numpy as np
        B, T, D_MODEL = (4, 1024, 512)
        D_LATENT = 128
        D_COMP = 64
        THETA = 10000.0
        LN_EPS = 1e-05

        def _rope_tables(seq_len: int, dim: int):
            inv_freq = 1.0 / THETA ** (jnp.arange(0, dim, 2, dtype=jnp.float32) / dim)
            freqs = jnp.arange(seq_len, dtype=jnp.float32)[:, None] * inv_freq[None, :]
            cos = jnp.concatenate([jnp.cos(freqs), jnp.cos(freqs)], axis=-1)
            sin = jnp.concatenate([jnp.sin(freqs), jnp.sin(freqs)], axis=-1)
            return (cos, sin)

        def _rotate_half(x):
            x1, x2 = jnp.split(x, 2, axis=-1)
            return jnp.concatenate([-x2, x1], axis=-1)
        Bx, Tx, _ = x.shape
        dc = W_compress.shape[0]
        kv_latent = x @ W_to_kv.T
        c = kv_latent @ W_compress.T
        mu = jnp.mean(c, axis=-1, keepdims=True)
        var = jnp.mean((c - mu) ** 2, axis=-1, keepdims=True)
        ch = (c - mu) * jax.lax.rsqrt(var + LN_EPS) * ln_gamma + ln_beta
        q = ch @ W_q_comp.T
        kv = ch @ W_kv_comp.T
        k, v = jnp.split(kv, 2, axis=-1)
        cos, sin = _rope_tables(Tx, dc)
        q = q * cos + _rotate_half(q) * sin
        k = k * cos + _rotate_half(k) * sin
        scale = 1.0 / jnp.sqrt(jnp.float32(dc))
        scores = jnp.einsum('btd,bsd->bts', q, k) * scale
        causal = jnp.tril(jnp.ones((Tx, Tx), dtype=bool))
        scores = jnp.where(causal[None], scores, jnp.float32(-1e+30))
        attn = jax.nn.softmax(scores, axis=-1)
        o = jnp.einsum('bts,bsd->btd', attn, v)
        z = o @ W_comp2lat.T
        out = z @ W_to_kv + z @ W_out_res.T + b_out_res
        return out

    def _L1_xattn_ref(q, k, v):
        import jax, jax.numpy as jnp
        import numpy as np
        B, S, E = (2, 512, 512)
        QH, KVH = (32, 8)
        D = E // QH
        G = QH // KVH
        DROPOUT = 1.0
        b, s, _ = q.shape
        qh = q.reshape(b, s, KVH, G, D).transpose(0, 2, 3, 1, 4)
        kh = k.reshape(b, s, KVH, D).transpose(0, 2, 1, 3)
        vh = v.reshape(b, s, KVH, D).transpose(0, 2, 1, 3)
        scale = 1.0 / jnp.sqrt(jnp.float32(D))
        scores = jnp.einsum('bkgsd,bktd->bkgst', qh, kh) * scale
        attn = jax.nn.softmax(scores, axis=-1) / DROPOUT
        out = jnp.einsum('bkgst,bktd->bkgsd', attn, vh)
        return out.transpose(0, 3, 1, 2, 4).reshape(b, s, E)

    def _L1_ffn_ref(x, router_w, w1, w2, w3):
        import jax, jax.numpy as jnp
        import numpy as np
        N_EXPERTS = 8
        TOP_K = 2
        D_MODEL = 512
        D_FF = 256
        BATCH, SEQ = (2, 512)

        def _trunc_normal(key, shape, fan_in):
            std = jnp.sqrt(1.0 / 3.0) / jnp.sqrt(float(fan_in))
            return jax.random.truncated_normal(key, -2.0, 2.0, shape, dtype=jnp.float32) * std
        B, S, D = x.shape
        xf = x.reshape(-1, D)
        n_tokens = xf.shape[0]
        logits = xf @ router_w.T
        topk_vals, topk_idx = jax.lax.top_k(logits, TOP_K)
        topk_weights = jax.nn.softmax(topk_vals, axis=-1)
        gate = jax.nn.silu(jnp.einsum('nd,edf->enf', xf, w1))
        value = jnp.einsum('nd,edf->enf', xf, w2)
        expert_out = jnp.einsum('enf,efd->end', gate * value, w3)
        tok = jnp.arange(n_tokens)[:, None]
        selected = expert_out[topk_idx, tok]
        out = jnp.sum(selected * topk_weights[..., None], axis=1)
        return out.reshape(B, S, D)
    x = _layernorm(x + _L0_attn_ref(x, L0_attn_Wq, L0_attn_bq, L0_attn_Wk, L0_attn_bk, L0_attn_Wv, L0_attn_bv, L0_attn_convq_w, L0_attn_convq_b, L0_attn_convk_w, L0_attn_convk_b, L0_attn_ssm_kernel, L0_attn_D_skip, L0_attn_Wo, L0_attn_bo), axis=-1)
    x = _layernorm(x + _L0_xattn_ref(x, ctx_512, ctx_512), axis=-1)
    x = _layernorm(x + _L0_ffn_ref(x, L0_ffn_W0, L0_ffn_bias0, L0_ffn_W1, L0_ffn_bias1), axis=-1)
    x = _layernorm(x + _L1_attn_ref(x, L1_attn_W_to_kv, L1_attn_W_compress, L1_attn_ln_gamma, L1_attn_ln_beta, L1_attn_W_q_comp, L1_attn_W_kv_comp, L1_attn_W_comp2lat, L1_attn_W_out_res, L1_attn_b_out_res), axis=-1)
    x = _layernorm(x + _L1_xattn_ref(x, ctx_512, ctx_512), axis=-1)
    x = _layernorm(x + _L1_ffn_ref(x, L1_ffn_router_w, L1_ffn_w1, L1_ffn_w2, L1_ffn_w3), axis=-1)
    return x

_drawn_inputs = setup_inputs


def setup_inputs(seed=0):
    import zlib

    import numpy as np

    out = dict(_drawn_inputs(seed))
    spreads = {'L0_attn_bq': (0.0, 0.8),
     'L0_attn_bk': (0.0, 0.8),
     'L0_attn_bv': (0.0, 0.8),
     'L0_attn_convq_b': (0.0, 0.8),
     'L0_attn_convk_b': (0.0, 0.8),
     'L0_attn_bo': (0.0, 0.1),
     'L1_attn_ln_gamma': (1.0, 0.6),
     'L1_attn_ln_beta': (0.0, 0.8),
     'L1_attn_W_out_res': (0.0, 0.664),
     'L1_attn_b_out_res': (0.0, 0.358)}
    factors = {'L0_attn_ssm_kernel': 8.0,
     'L0_ffn_bias0': 5.713,
     'L0_ffn_bias1': 4.158,
     'L1_attn_W_to_kv': 4.69,
     'L1_attn_W_compress': 5.088,
     'L1_attn_W_q_comp': 8.0,
     'L1_attn_W_kv_comp': 4.728,
     'L1_attn_W_comp2lat': 4.477}
    for name, (base, spread) in spreads.items():
        noise = np.random.default_rng([zlib.crc32(name.encode()), seed]).standard_normal(out[name].shape)
        drawn = base * np.exp(spread * noise) if base else spread * noise
        out[name] = jnp.asarray(drawn.astype(out[name].dtype))
    for name, factor in factors.items():
        out[name] = (out[name] * factor).astype(out[name].dtype)
    return out
```

```python
from contextlib import ExitStack

import concourse.bass as bass
from concourse import mybir

F32 = mybir.dt.float32
F16 = mybir.dt.float16
U32 = mybir.dt.uint32
ALU = mybir.AluOpType
ACT = mybir.ActivationFunctionType
AX = mybir.AxisListType

P = 128
B = 32
D = 512
DC = D // P
GS = 4
GT = GS * P
NG = B // GS
FF = 2048
FC = FF // P
NE = 8
FE = 256
WS = 256.0
EPS = 1e-5
ds = bass.ds


def tile(X, i):
    return X[:, ds(i, 1), :].rearrange("p a n -> p (a n)")


def group(X, i, n=GS):
    return X[:, ds(i, n), :]


def load_split(nc, name, parts, scale=WS):
    W = 2048
    pieces = []
    for dram, hi, lo in parts:
        n = dram.shape[1]
        for a in range(0, n, W):
            b = min(n, a + W)
            pieces.append((dram[:, a:b], hi[:, a:b], lo[:, a:b], b - a))
    with ExitStack() as ctx:
        stage = ctx.enter_context(nc.sbuf_tensor(f"{name}_stage", [P, 2, W], F32))
        loaded = [nc.alloc_semaphore(f"{name}_loaded{k}") for k in range(2)]
        hi_made = nc.alloc_semaphore(f"{name}_hi_made")
        lo_made = nc.alloc_semaphore(f"{name}_lo_made")
        with nc.Block() as block:

            @block.sync
            def _(sp):
                for k, (src, _, _, n) in enumerate(pieces):
                    if k >= 2:
                        sp.wait_ge(lo_made, k - 1)
                    sp.dma_start(stage[:, k % 2, 0:n], src).then_inc(loaded[k % 2], 16)

            @block.scalar
            def _(act):
                for k, (_, hi, _, n) in enumerate(pieces):
                    act.wait_ge(loaded[k % 2], 16 * (k // 2 + 1))
                    act.activation(hi, stage[:, k % 2, 0:n], ACT.Copy, scale=scale).then_inc(hi_made, 1)

            @block.vector
            def _(dve):
                for k, (_, hi, lo, n) in enumerate(pieces):
                    dve.wait_ge(hi_made, k + 1)
                    dve.wait_ge(loaded[k % 2], 16 * (k // 2 + 1))
                    dve.scalar_tensor_tensor(lo, stage[:, k % 2, 0:n], scale, hi, ALU.mult, ALU.subtract).then_inc(lo_made, 1)


class Norm:

    def __init__(self, nc, ctx, name, n=GS):
        self.n = n
        self.stats = ctx.enter_context(nc.sbuf_tensor(f"{name}_stats", [P, n, 6], F32))
        self.mv = ctx.enter_context(nc.sbuf_tensor(f"{name}_mv", [P, n, 2], F32))
        self.rstd = ctx.enter_context(nc.sbuf_tensor(f"{name}_rstd", [P, n], F32))
        self.consts = ctx.enter_context(nc.sbuf_tensor(f"{name}_consts", [P, 2 * n], F32))
        s = lambda n: nc.alloc_semaphore(f"{name}_{n}")
        self.rows_ready = s("rows_ready")
        self.stats_ready = s("stats_ready")
        self.mv_ready = s("mv_ready")
        self.var_eps = s("var_eps")
        self.rstd_ready = s("rstd_ready")
        self.normed = s("normed")
        self.consts_set = s("consts_set")
        self.waits_apart = s("waits_apart")


def norm_consts(pool, n):
    pool.memset(n.consts[:, 0:n.n], EPS).then_inc(n.consts_set, 1)
    pool.memset(n.consts[:, n.n:2 * n.n], -0.5).then_inc(n.consts_set, 1)


def norm_rstd(pool, n, i):
    pool.wait_ge(n.consts_set, 2)
    pool.wait_ge(n.mv_ready, n.n * i + n.n)
    pool.tensor_tensor(n.rstd[:, :], n.mv[:, :, 1], n.consts[:, 0:n.n], ALU.add).then_inc(n.var_eps, 1)
    pool.wait_ge(n.var_eps, i + 1)
    pool.tensor_tensor(n.rstd[:, :], n.rstd[:, :], n.consts[:, n.n:2 * n.n], ALU.pow).then_inc(n.rstd_ready, 1)


def wait_apart(eng, apart, sem, value):
    eng.wait_ge(sem, value)
    eng.sem_inc(apart, 1)


def norm_stats(dve, n, X, i, j):
    wait_apart(dve, n.waits_apart, n.rows_ready, n.n * i + j + 1)
    dve.bn_stats(n.stats[:, j, :], tile(X, n.n * i + j)).then_inc(n.stats_ready, 1)


def norm_aggr(dve, n, i, j):
    wait_apart(dve, n.waits_apart, n.stats_ready, n.n * i + j + 1)
    dve.bn_aggr(n.mv[:, j, :], n.stats[:, j, :]).then_inc(n.mv_ready, 1)


def norm_apply(dve, n, X, i, j):
    dve.wait_ge(n.rstd_ready, i + 1)
    x = tile(X, n.n * i + j)
    dve.tensor_scalar(x, x, n.mv[:, j, 0:1], n.rstd[:, j:j + 1], ALU.subtract, ALU.mult).then_inc(n.normed, 1)


def ffn(nc, X, w0T, w1T, bias0, bias1, idh):
    with ExitStack() as ctx:
        sb = lambda n, s, d=F32: ctx.enter_context(nc.sbuf_tensor(f"ffn_{n}", s, d))
        ps = lambda n, s, d=F32: ctx.enter_context(nc.psum_tensor(f"ffn_{n}", s, d))
        sem = lambda n: nc.alloc_semaphore(f"ffn_{n}")
        W0h, W0l = sb("W0h", [P, DC, FF], F16), sb("W0l", [P, DC, FF], F16)
        W1h, W1l = sb("W1h", [P, FC, D], F16), sb("W1l", [P, FC, D], F16)
        flat = lambda t: t[:, :, :].rearrange("p a n -> p (a n)")
        load_split(nc, "ffnw", [(w0T, flat(W0h), flat(W0l)), (w1T, flat(W1h), flat(W1l))])
        X16 = sb("X16", [P, GS, D], F16)
        XT = sb("XT", [P, DC, GT], F16)
        DT = sb("DT", [P, FC, GT], F16)
        E16 = sb("E16", [P, GS, D], F16)
        b0 = sb("b0", [P, FC])
        b1 = sb("b1", [P, D])
        psT = [ps(f"psT{k}", [P, GT], F16) for k in range(2)]
        psD = [ps(f"psD{k}", [P, GT]) for k in range(2)]
        psE = [ps(f"psE{k}", [P, D]) for k in range(GS)]
        norm = Norm(nc, ctx, "ffn_norm")
        consts_loaded = sem("consts_loaded")
        x16_ready, xT_psum, xT_ready = sem("x16_ready"), sem("xT_psum"), sem("xT_ready")
        d_psum, dT_ready, e_psum, e16_ready = sem("d_psum"), sem("dT_ready"), sem("e_psum"), sem("e16_ready")

        with nc.Block() as block:

            @block.sync
            def _(sp):
                sp.dma_start(b0[:, :], bias0).then_inc(consts_loaded, 16)
                sp.dma_start(b1[:, :], bias1.partition_broadcast(P)).then_inc(consts_loaded, 16)

            @block.gpsimd
            def _(pool):
                norm_consts(pool, norm)

                def cast(i):
                    pool.wait_ge(xT_psum, DC * i)
                    for j in range(GS):
                        pool.tensor_copy(X16[:, j, :], tile(X, GS * i + j)).then_inc(x16_ready, 1)

                cast(0)
                with pool.Fori(0, NG - 1) as i:
                    cast(i + 1)
                    norm_rstd(pool, norm, i)
                norm_rstd(pool, norm, NG - 1)

            @block.tensor
            def _(pe):
                with pe.Fori(0, NG) as i:
                    pe.wait_ge(x16_ready, GS * i + GS)
                    for c in range(DC):
                        pe.wait_ge(xT_ready, DC * i + max(0, c - 1))
                        for j in range(GS):
                            t = pe.transpose(psT[c % 2][:, j * P:(j + 1) * P], X16[:, j, c * P:(c + 1) * P], idh[:, :])
                        t.then_inc(xT_psum, 1)
                    pe.wait_ge(xT_ready, DC * i + DC)
                    for n in range(FC):
                        pe.wait_ge(dT_ready, FC * i + max(0, n - 1))
                        for c in range(DC):
                            for w in (W0h, W0l):
                                t = pe.matmul(psD[n % 2][:, :], w[:, c, n * P:(n + 1) * P], XT[:, c, :],
                                              start=(c == 0 and w is W0h), stop=(c == DC - 1 and w is W0l))
                        t.then_inc(d_psum, 1)
                    pe.wait_ge(dT_ready, FC * i + FC)
                    pe.wait_ge(e16_ready, GS * i)
                    for j in range(GS):
                        for n in range(FC):
                            for w in (W1h, W1l):
                                t = pe.matmul(psE[j][:, :], DT[:, n, j * P:(j + 1) * P], w[:, n, :],
                                              start=(n == 0 and w is W1h), stop=(n == FC - 1 and w is W1l))
                        t.then_inc(e_psum, 1)

            @block.scalar
            def _(act):
                act.wait_ge(consts_loaded, 32)
                with act.Fori(0, NG) as i:
                    for c in range(DC):
                        act.wait_ge(xT_psum, DC * i + c + 1)
                        act.activation(XT[:, c, :], psT[c % 2][:, :], ACT.Copy).then_inc(xT_ready, 1)
                    act.wait_ge(e_psum, GS * i)
                    for n in range(FC):
                        act.wait_ge(d_psum, FC * i + n + 1)
                        act.activation(DT[:, n, :], psD[n % 2][:, :], ACT.Gelu, bias=b0[:, n:n + 1],
                                       scale=1.0 / WS).then_inc(dT_ready, 1)

            @block.vector
            def _(dve):
                dve.wait_ge(consts_loaded, 32)
                with dve.Fori(0, NG) as i:
                    for j in range(GS):
                        dve.wait_ge(e_psum, GS * i + j + 1)
                        dve.scalar_tensor_tensor(E16[:, j, :], psE[j][:, :], 1.0 / WS, b1[:, :], ALU.mult, ALU.add)\
                           .then_inc(e16_ready, 1)
                        dve.wait_ge(e16_ready, GS * i + j + 1)
                        x = tile(X, GS * i + j)
                        dve.tensor_tensor(x, x, E16[:, j, :], ALU.add).then_inc(norm.rows_ready, 1)
                        norm_stats(dve, norm, X, i, j)
                        norm_aggr(dve, norm, i, j)
                    for j in range(GS):
                        norm_apply(dve, norm, X, i, j)


NR = 2
TT = 4
EROWS = B * P + P
NTILE = B * NR + NE
ETILE = EROWS // P
ZTILE = 3 * P
W12E = DC * 2 * FE
W3E = FE // P * D
MC_IOTA = 0
MC_ZONE = MC_IOTA + NE
MC_FULL = MC_ZONE + NE
MC_UPTO = MC_FULL + B
MC_TILE = MC_UPTO + NE * NE
MC_P = MC_TILE + NTILE
MC_W = MC_P + 1


def moe(nc, X, w12, w3, rw, idh, idf, tri, mc, out):
    xs = nc.dram_tensor("moe_xs", [B * P, 2 * D], F16, kind="Internal").ap()
    inv = nc.dram_tensor("moe_inv", [ZTILE * P, 1], F32, kind="Internal").ap()
    ys = nc.dram_tensor("moe_ys", [NTILE * P, D], F32, kind="Internal").ap()
    with ExitStack() as ctx:
        sb = lambda n, s, d=F32: ctx.enter_context(nc.sbuf_tensor(f"moe_{n}", s, d))
        rows_of = sb("rows_of", [P, B * NR], U32)
        gap = sb("gap", [P, B])
        tokens = sb("tokens", [P, ZTILE], U32)
        zone_tile = sb("zone_tile", [P, NTILE], U32)
        expert_at = sb("expert_at", [P, NTILE], U32)
        with ExitStack() as weights:
            wsb = lambda n, s, d=F16: weights.enter_context(nc.sbuf_tensor(f"moe_{n}", s, d))
            W12h, W12l = wsb("W12h", [P, NE * W12E]), wsb("W12l", [P, NE * W12E])
            W3h, W3l = wsb("W3h", [P, NE * W3E]), wsb("W3l", [P, NE * W3E])
            RWh, RWl = wsb("RWh", [P, DC * NE]), wsb("RWl", [P, DC * NE])
            load_split(nc, "moew", [(w12, W12h, W12l), (w3, W3h, W3l), (rw, RWh, RWl)])
            moe_route(nc, X, RWh, RWl, idh, idf, tri, mc, xs, inv, rows_of, gap, tokens, zone_tile, expert_at)
            moe_experts(nc, W12h, W12l, W3h, W3l, idh, xs, ys, tokens, zone_tile, expert_at)
        moe_combine(nc, X, ys, rows_of, gap, out)


def moe_route(nc, X, RWh, RWl, idh, idf, tri, mc, xs, inv, rows_of, gap, tokens, zone_tile, expert_at):
    with ExitStack() as ctx:
        sb = lambda n, s, d=F32: ctx.enter_context(nc.sbuf_tensor(f"route_{n}", s, d))
        ps = lambda n, s, d=F32: ctx.enter_context(nc.psum_tensor(f"route_{n}", s, d))
        sem = lambda n: nc.alloc_semaphore(f"route_{n}")
        R = sb("R", [P, 2, TT, 2 * D], F16)
        XT = sb("XT", [P, TT, 2 * D], F16)
        zero = sb("zero", [P, ZTILE])
        I = sb("I", [P, B, NR])
        row_all = sb("row_all", [P, B * NR])
        token = sb("token", [P, 2, TT])
        lst = sb("list", [P, 3, P])
        L = sb("L", [P, TT, NE])
        V8 = sb("V8", [P, TT, 8])
        I8 = sb("I8", [P, TT, 8], U32)
        pick = sb("pick", [P, TT, NR, NE])
        both = sb("both", [P, TT, NE], F16)
        next_row = sb("next_row", [P, NE])
        row = sb("row", [P, TT, NE])
        prow = sb("prow", [P, TT, NR, NE])
        rowf = sb("rowf", [P, TT * NR])
        J = sb("J", [P, 2, TT * NR], U32)
        n_of = sb("n_of", [P, NE])
        full = sb("full", [P, NE, B])
        tiles = sb("tiles", [P, NE])
        upto = sb("upto", [P, NE, NE])
        end = sb("end", [P, NE])
        past = sb("past", [P, NTILE, NE])
        ptiles = sb("ptiles", [P, NTILE, NE])
        shift = sb("shift", [P, NE])
        rowf64 = sb("rowf64", [P, B * NR])
        pshift = sb("pshift", [P, B * NR, NE])
        et, before, base = sb("et", [P, NTILE]), sb("before", [P, NTILE]), sb("base", [P, NTILE])
        T = [ps(f"T{k}", [P, D]) for k in range(4)]
        T16 = [t[:, :].bitcast(F16) for t in T]
        M = [ps(f"M{k}", [P, TT * NE]) for k in range(2)]
        C = [ps(f"C{k}", [P, (TT + 1) * NE]) for k in range(2)]
        hi_ready, lo_ready, xT_psum, xT_ready = sem("hi_ready"), sem("lo_ready"), sem("xT_psum"), sem("xT_ready")
        logits_psum, logits_ready, best_ready = sem("logits_psum"), sem("logits_ready"), sem("best_ready")
        gap_ready, index_ready, indexf_ready = sem("gap_ready"), sem("index_ready"), sem("indexf_ready")
        pick_ready, both_ready, counts_psum, row_ready = (sem("pick_ready"), sem("both_ready"), sem("counts_psum"),
                                                          sem("row_ready"))
        next_ready, prow_ready, rowf_ready, rows_ready = (sem("next_ready"), sem("prow_ready"), sem("rowf_ready"),
                                                          sem("rows_ready"))
        zero_set, zone_zeroed, apart = sem("zero_set"), sem("zone_zeroed"), sem("apart")
        table = sem("table")
        token_ready, list_loaded, list_psum = sem("token_ready"), sem("list_loaded"), sem("list_psum")
        scattered, xs_stored = [sem(f"scattered{k}") for k in range(2)], [sem(f"xs_stored{k}") for k in range(2)]
        NI = B // (2 * TT)
        cols = lambda k, n: mc[:, k:k + n]

        with nc.Block() as block:

            @block.gpsimd
            def _(pool):
                pool.wait_ge(zone_zeroed, 16)
                with pool.Fori(0, NI) as i:
                    for h in range(2):
                        wait_apart(pool, apart, token_ready, 2 * i + h + 1)
                        wait_apart(pool, apart, rows_ready, 2 * i + h + 1)
                        for j in range(TT):
                            for r in range(NR):
                                pool.indirect_dma_start(inv, bass.IndirectOffsetOnAxis(ap=J[:, h, NR * j + r:NR * j + r + 1], axis=0),
                                                        token[:, h, j:j + 1], None).then_inc(scattered[h], 16)

            @block.sync
            def _(sp):
                sp.wait_ge(zero_set, 1)
                sp.dma_start(inv.rearrange("(p n) o -> p (n o)", p=P), zero[:, :]).then_inc(zone_zeroed, 16)
                with sp.Fori(0, NI) as i:
                    for h in range(2):
                        sp.wait_ge(hi_ready, TT * (2 * i + h) + TT)
                        sp.wait_ge(lo_ready, TT * (2 * i + h) + TT)
                        sp.dma_start(xs[ds((8 * i + 4 * h) * P, TT * P), :].rearrange("(j p) n -> p j n", p=P), R[:, h, :, :])\
                          .then_inc(xs_stored[h], 16)
                for h in range(2):
                    sp.wait_ge(xs_stored[h], 16 * NI)

            @block.scalar
            def _(act):
                with act.Fori(0, NI) as i:
                    for h in range(2):
                        act.wait_ge(xs_stored[h], 16 * i)
                        act.wait_ge(xT_psum, TT * (2 * i + h))
                        for j in range(TT):
                            act.activation(R[:, h, j, 0:D], tile(X, 8 * i + TT * h + j), ACT.Copy).then_inc(hi_ready, 1)
                        act.wait_ge(logits_psum, 2 * i + h)
                        for j in range(TT):
                            act.wait_ge(xT_psum, TT * (2 * i + h) + j + 1)
                            act.activation(XT[:, j, :], T16[j], ACT.Copy).then_inc(xT_ready, 1)

            @block.tensor
            def _(pe):
                with pe.Fori(0, NI) as i:
                    for h in range(2):
                        g = 2 * i + h
                        for j in range(TT):
                            pe.wait_ge(hi_ready, TT * g + j + 1)
                            pe.wait_ge(xT_ready, TT * g)
                            for c in range(DC):
                                pe.transpose(T16[j][:, c * P:(c + 1) * P], R[:, h, j, c * P:(c + 1) * P], idh[:, :])
                            pe.wait_ge(lo_ready, TT * g + j + 1)
                            for c in range(DC, 2 * DC):
                                t = pe.transpose(T16[j][:, c * P:(c + 1) * P], R[:, h, j, c * P:(c + 1) * P], idh[:, :])
                            t.then_inc(xT_psum, 1)
                        pe.wait_ge(logits_ready, g)
                        for j in range(TT):
                            pe.wait_ge(xT_ready, TT * g + j + 1)
                            for c in range(DC):
                                for k, (x, w) in enumerate(((c, RWh), (DC + c, RWh), (c, RWl))):
                                    t = pe.matmul(M[h][:, j * NE:(j + 1) * NE], XT[:, j, x * P:(x + 1) * P],
                                                  w[:, c * NE:(c + 1) * NE],
                                                  start=(c == 0 and k == 0), stop=(c == DC - 1 and k == 2))
                        t.then_inc(logits_psum, 1)
                        pe.wait_ge(both_ready, g + 1)
                        pe.wait_ge(next_ready, g)
                        for j in range(TT + 1):
                            for b in range(min(j + 1, TT)):
                                last = b == min(j, TT - 1)
                                lhs = tri[:, 0:P] if b == j else tri[:, P:2 * P]
                                t = pe.matmul(C[h][:, j * NE:(j + 1) * NE], lhs, both[:, b, :], start=(b == 0), stop=last)
                        t.then_inc(counts_psum, 1)

            @block.vector
            def _(dve):
                dve.memset(zero[:, :], 0.0).then_inc(zero_set, 1)
                dve.tensor_copy(next_row[:, :], cols(MC_ZONE, NE)).then_inc(zero_set, 1)
                dve.wait_ge(zero_set, 2)
                with dve.Fori(0, NI) as i:
                    for h in range(2):
                        g = 2 * i + h
                        for j in range(TT):
                            dve.wait_ge(hi_ready, TT * g + j + 1)
                            dve.tensor_tensor(R[:, h, j, D:2 * D], tile(X, TT * g + j), R[:, h, j, 0:D], ALU.subtract)\
                               .then_inc(lo_ready, 1)
                        dve.wait_ge(logits_psum, g + 1)
                        dve.tensor_scalar(L[:, :, :].rearrange("p j e -> p (j e)"), M[h][:, :], 1.0 / WS, None, ALU.mult)\
                           .then_inc(logits_ready, 1)
                        for j in range(TT):
                            wait_apart(dve, apart, logits_ready, g + 1)
                            dve.max(V8[:, j, :], L[:, j, :]).then_inc(best_ready, 1)
                        dve.wait_ge(best_ready, TT * g + TT)
                        dve.tensor_tensor(gap[:, ds(TT * g, TT)], V8[:, :, 0], V8[:, :, 1], ALU.subtract).then_inc(gap_ready, 1)
                        for j in range(TT):
                            dve.max_index(I8[:, j, :], V8[:, j, :], L[:, j, :]).then_inc(index_ready, 1)
                        dve.wait_ge(index_ready, TT * g + TT)
                        dve.tensor_copy(I[:, ds(TT * g, TT), :], I8[:, :, 0:NR]).then_inc(indexf_ready, 1)
                        dve.wait_ge(indexf_ready, g + 1)
                        iota = cols(MC_IOTA, NE).unsqueeze(1).to_broadcast([P, TT * NR, NE])
                        index = I[:, ds(TT * g, TT), :].rearrange("p j r -> p (j r)").unsqueeze(2).to_broadcast([P, TT * NR, NE])
                        dve.tensor_tensor(pick[:, :, :, :].rearrange("p j r e -> p (j r) e"), iota, index, ALU.is_equal)\
                           .then_inc(pick_ready, 1)
                        dve.wait_ge(pick_ready, g + 1)
                        dve.wait_ge(counts_psum, g)
                        dve.tensor_tensor(both[:, :, :], pick[:, :, 0, :], pick[:, :, 1, :], ALU.add).then_inc(both_ready, 1)
                        dve.wait_ge(counts_psum, g + 1)
                        c = C[h][:, 0:TT * NE].rearrange("p (j e) -> p j e", e=NE)
                        dve.tensor_tensor(row[:, :, :], c, next_row[:, :].unsqueeze(1).to_broadcast([P, TT, NE]), ALU.add)\
                           .then_inc(row_ready, 1)
                        dve.wait_ge(row_ready, g + 1)
                        dve.tensor_tensor(next_row[:, :], next_row[:, :], C[h][:, TT * NE:(TT + 1) * NE], ALU.add)\
                           .then_inc(next_ready, 1)
                        for r in range(NR):
                            dve.tensor_tensor(prow[:, :, r, :], pick[:, :, r, :], row[:, :, :], ALU.mult).then_inc(prow_ready, 1)
                        dve.wait_ge(prow_ready, NR * g + NR)
                        dve.tensor_reduce(rowf[:, :], prow[:, :, :, :].rearrange("p j r e -> p (j r) e"), AX.X, ALU.add)\
                           .then_inc(rowf_ready, 1)
                        dve.wait_ge(rowf_ready, g + 1)
                        dve.wait_ge(scattered[h], 16 * TT * NR * i)
                        dve.tensor_copy(J[:, h, :], rowf[:, :]).then_inc(rows_ready, 1)
                        dve.tensor_scalar(token[:, h, :], mc[:, ds(MC_FULL + TT * g, TT)], cols(MC_P, 1), None, ALU.add)\
                           .then_inc(token_ready, 1)
                        dve.tensor_copy(row_all[:, ds(TT * NR * g, TT * NR)], rowf[:, :]).then_inc(table, 1)
                dve.wait_ge(next_ready, 2 * NI)
                n = 2 * NI

                def step(t):
                    nonlocal n
                    n += 1
                    t.then_inc(table, 1)
                    dve.wait_ge(table, n)

                dve.wait_ge(table, n)
                step(dve.tensor_tensor(n_of[:, :], next_row[:, :], cols(MC_ZONE, NE), ALU.subtract))
                step(dve.tensor_tensor(full[:, :, :], n_of[:, :].unsqueeze(2).to_broadcast([P, NE, B]),
                                       cols(MC_FULL, B).unsqueeze(1).to_broadcast([P, NE, B]), ALU.is_gt))
                step(dve.tensor_reduce(tiles[:, :], full[:, :, :], AX.X, ALU.add))
                step(dve.tensor_tensor(upto[:, :, :], cols(MC_UPTO, NE * NE).rearrange("p (e f) -> p e f", e=NE),
                                       tiles[:, :].unsqueeze(1).to_broadcast([P, NE, NE]), ALU.mult))
                step(dve.tensor_reduce(end[:, :], upto[:, :, :], AX.X, ALU.add))
                step(dve.tensor_tensor(past[:, :, :], end[:, :].unsqueeze(1).to_broadcast([P, NTILE, NE]),
                                       cols(MC_TILE, NTILE).unsqueeze(2).to_broadcast([P, NTILE, NE]), ALU.is_le))
                step(dve.tensor_reduce(et[:, :], past[:, :, :], AX.X, ALU.add))
                step(dve.tensor_tensor(ptiles[:, :, :], past[:, :, :], tiles[:, :].unsqueeze(1).to_broadcast([P, NTILE, NE]),
                                       ALU.mult))
                step(dve.tensor_reduce(before[:, :], ptiles[:, :, :], AX.X, ALU.add))
                step(dve.tensor_tensor(before[:, :], cols(MC_TILE, NTILE), before[:, :], ALU.subtract))
                step(dve.scalar_tensor_tensor(base[:, :], et[:, :], float(ETILE), before[:, :], ALU.mult, ALU.add))
                step(dve.tensor_copy(zone_tile[:, :], base[:, :]))
                step(dve.tensor_scalar(et[:, :], et[:, :], float(NE - 1), float(W3E), ALU.min, ALU.mult))
                step(dve.tensor_copy(expert_at[:, :], et[:, :]))
                step(dve.tensor_tensor(shift[:, :], end[:, :], tiles[:, :], ALU.subtract))
                step(dve.scalar_tensor_tensor(shift[:, :], shift[:, :], float(P), cols(MC_ZONE, NE), ALU.mult, ALU.subtract))
                step(dve.tensor_tensor(pshift[:, :, :], cols(MC_IOTA, NE).unsqueeze(1).to_broadcast([P, B * NR, NE]),
                                       I[:, :, :].rearrange("p j r -> p (j r)").unsqueeze(2).to_broadcast([P, B * NR, NE]),
                                       ALU.is_equal))
                step(dve.tensor_tensor(pshift[:, :, :], pshift[:, :, :], shift[:, :].unsqueeze(1).to_broadcast([P, B * NR, NE]),
                                       ALU.mult))
                step(dve.tensor_reduce(rowf64[:, :], pshift[:, :, :], AX.X, ALU.add))
                step(dve.tensor_tensor(rows_of[:, :], rowf64[:, :], row_all[:, :], ALU.add))

        with nc.Block() as block:

            @block.sync
            def _(sp):
                for h in range(2):
                    sp.wait_ge(scattered[h], 16 * TT * NR * NI)
                sp.dma_start(lst[:, :, :], inv.rearrange("(k q p) o -> q k (p o)", k=3, p=P)).then_inc(list_loaded, 16)

            @block.tensor
            def _(pe):
                pe.wait_ge(list_loaded, 16)
                for k in range(3):
                    t = pe.transpose(T[0][:, k * P:(k + 1) * P], lst[:, k, :], idf[:, :])
                t.then_inc(list_psum, 1)

            @block.vector
            def _(dve):
                dve.wait_ge(list_psum, 1)
                dve.tensor_copy(tokens[:, :], T[0][:, 0:ZTILE]).then_inc(table, 1)


def moe_experts(nc, W12h, W12l, W3h, W3l, idh, xs, ys, tokens, zone_tile, expert_at):
    with ExitStack() as ctx:
        sb = lambda n, s, d=F32: ctx.enter_context(nc.sbuf_tensor(f"ex_{n}", s, d))
        ps = lambda n: ctx.enter_context(nc.psum_tensor(f"ex_{n}", [P, D], F32))
        sem = lambda n: nc.alloc_semaphore(f"ex_{n}")
        K = 4
        NS = NTILE // K
        G = sb("G", [P, K, 2 * D], F16)
        J = sb("J", [P, K], U32)
        XT = sb("XT", [P, 2, 2 * D], F16)
        S = sb("S", [P, 2, FE])
        H = sb("H", [P, 2, 2 * FE], F16)
        HT = sb("HT", [P, 2, 2 * FE], F16)
        Y = sb("Y", [P, K, D])
        TB = [ps(f"TB{k}") for k in range(2)]
        UB = [ps(f"UB{k}") for k in range(2)]
        HB = [ps(f"HB{k}") for k in range(2)]
        DB = [ps(f"DB{k}") for k in range(2)]
        T16 = [t[:, :].bitcast(F16) for t in TB]
        H16 = [t[:, :].bitcast(F16)[:, 0:2 * FE] for t in HB]
        gathered, written = [sem(f"gathered{k}") for k in range(K)], [sem(f"written{k}") for k in range(K)]
        j_ready, xT_psum, xT_ready = sem("j_ready"), sem("xT_psum"), sem("xT_ready")
        up_psum, silu_ready, prod_ready, hi_ready, lo_ready = (sem("up_psum"), sem("silu_ready"), sem("prod_ready"),
                                                               sem("hi_ready"), sem("lo_ready"))
        hT_psum, hT_ready, down_psum, y_ready, apart = (sem("hT_psum"), sem("hT_ready"), sem("down_psum"), sem("y_ready"),
                                                        sem("apart"))

        with nc.Block() as block:

            @block.gpsimd
            def _(pool):

                def fetch(i, k):
                    column = pool.value_load(zone_tile[0:1, ds(K * i + k, 1)], min_val=0, max_val=ZTILE - 1)
                    pool.wait_ge(gathered[k], 16 * i)
                    pool.tensor_copy(J[:, k:k + 1], tokens[:, ds(column, 1)]).then_inc(j_ready, 1)
                    wait_apart(pool, apart, j_ready, K * i + k + 1)
                    if type(i) is not int:
                        wait_apart(pool, apart, xT_psum, K * i + k + 1 - K)
                    pool.indirect_dma_start(G[:, k, :], None, xs, bass.IndirectOffsetOnAxis(ap=J[:, k:k + 1], axis=0))\
                        .then_inc(gathered[k], 16)

                for k in range(K):
                    fetch(0, k)
                with pool.Fori(0, NS - 1) as i:
                    for k in range(K):
                        fetch(i + 1, k)

            @block.sync
            def _(sp):
                with sp.Fori(0, NS) as i:
                    for k in range(K):
                        sp.wait_ge(y_ready, K * i + k + 1)
                        sp.dma_start(ys[ds((K * i + k) * P, P), :], Y[:, k, :]).then_inc(written[k], 16)
                for k in range(K):
                    sp.wait_ge(written[k], 16 * NS)

            @block.tensor
            def _(pe):

                def turn_x(t, i, k):
                    pe.wait_ge(gathered[k], 16 * i + 16)
                    if type(t) is not int or t >= 2:
                        pe.wait_ge(xT_ready, t - 1)
                    for c in range(2 * DC):
                        m = pe.transpose(T16[k % 2][:, c * P:(c + 1) * P], G[:, k, c * P:(c + 1) * P], idh[:, :])
                    m.then_inc(xT_psum, 1)

                def up(t, k):
                    e = pe.value_load(expert_at[0:1, ds(t, 1)], min_val=0, max_val=(NE - 1) * W3E)
                    pe.wait_ge(xT_ready, t + 1)
                    if type(t) is not int or t >= 2:
                        pe.wait_ge(prod_ready, t - 1)
                    for c in range(DC):
                        for n, (x, w) in enumerate(((c, W12h), (DC + c, W12h), (c, W12l))):
                            m = pe.matmul(UB[k % 2][:, :], XT[:, k % 2, x * P:(x + 1) * P],
                                          w[:, ds(e * (W12E // W3E) + c * 2 * FE, 2 * FE)],
                                          start=(c == 0 and n == 0), stop=(c == DC - 1 and n == 2))
                    m.then_inc(up_psum, 1)

                def turn_h(t, k):
                    pe.wait_ge(lo_ready, t + 1)
                    pe.wait_ge(hi_ready, t + 1)
                    if type(t) is not int or t >= 2:
                        pe.wait_ge(hT_ready, t - 1)
                    for c in range(4):
                        m = pe.transpose(H16[k % 2][:, c * P:(c + 1) * P], H[:, k % 2, c * P:(c + 1) * P], idh[:, :])
                    m.then_inc(hT_psum, 1)

                def down(t, k):
                    e = pe.value_load(expert_at[0:1, ds(t, 1)], min_val=0, max_val=(NE - 1) * W3E)
                    pe.wait_ge(hT_ready, t + 1)
                    if type(t) is not int or t >= 2:
                        pe.wait_ge(y_ready, t - 1)
                    for f in range(2):
                        for n, (h, w) in enumerate(((f, W3h), (2 + f, W3h), (f, W3l))):
                            m = pe.matmul(DB[k % 2][:, :], HT[:, k % 2, h * P:(h + 1) * P], w[:, ds(e + f * D, D)],
                                          start=(f == 0 and n == 0), stop=(f == 1 and n == 2))
                    m.then_inc(down_psum, 1)

                def step(i, k, first=False, last=False):
                    s = K * i + k
                    if not last:
                        turn_x(s, i, k)
                    if not (first and s < 1) and not (last and s - 1 >= NTILE):
                        up(s - 1, (k - 1) % K)
                    if not (first and s < 2) and not (last and s - 2 >= NTILE):
                        turn_h(s - 2, (k - 2) % K)
                    if not (first and s < 3):
                        down(s - 3, (k - 3) % K)

                for k in range(K):
                    step(0, k, first=True)
                with pe.Fori(0, NS - 1) as r:
                    for k in range(K):
                        step(r + 1, k)
                for k in range(3):
                    step(NS, k, last=True)

            @block.scalar
            def _(act):

                def turned_x(t, k):
                    act.wait_ge(xT_psum, t + 1)
                    if type(t) is not int or t >= 2:
                        act.wait_ge(up_psum, t - 1)
                    act.activation(XT[:, k % 2, :], T16[k % 2], ACT.Copy).then_inc(xT_ready, 1)

                def silu(t, k):
                    act.wait_ge(up_psum, t + 1)
                    if type(t) is not int or t >= 2:
                        act.wait_ge(lo_ready, t - 1)
                    act.activation(S[:, k % 2, :], UB[k % 2][:, 0:FE], ACT.Silu, scale=1.0 / WS).then_inc(silu_ready, 1)

                turned_x(0, 0)
                turned_x(1, 1)
                silu(0, 0)
                turned_x(2, 2)
                silu(1, 1)
                with act.Fori(0, (NTILE - 4) // 2) as i:
                    for k in range(2):
                        turned_x(2 * i + 3 + k, k + 1)
                        silu(2 * i + 2 + k, k)
                turned_x(NTILE - 1, 1)
                silu(NTILE - 2, 0)
                silu(NTILE - 1, 1)

            @block.vector
            def _(dve):

                def split(t, k):
                    s = S[:, k % 2, :]
                    dve.wait_ge(silu_ready, t + 1)
                    dve.scalar_tensor_tensor(s, UB[k % 2][:, FE:2 * FE], 1.0 / WS, s, ALU.mult, ALU.mult).then_inc(prod_ready, 1)
                    dve.wait_ge(prod_ready, t + 1)
                    if type(t) is not int or t >= 2:
                        dve.wait_ge(hT_psum, t - 1)
                    dve.tensor_copy(H[:, k % 2, 0:FE], s).then_inc(hi_ready, 1)
                    dve.wait_ge(hi_ready, t + 1)
                    dve.tensor_tensor(H[:, k % 2, FE:2 * FE], s, H[:, k % 2, 0:FE], ALU.subtract).then_inc(lo_ready, 1)

                def turned_h(t, k):
                    dve.wait_ge(hT_psum, t + 1)
                    if type(t) is not int or t >= 2:
                        dve.wait_ge(down_psum, t - 1)
                    dve.tensor_copy(HT[:, k % 2, :], H16[k % 2]).then_inc(hT_ready, 1)

                def outputs(t, i, k):
                    dve.wait_ge(down_psum, t + 1)
                    dve.wait_ge(written[k], 16 * i)
                    dve.tensor_scalar(Y[:, k, :], DB[k % 2][:, :], 1.0 / WS, None, ALU.mult).then_inc(y_ready, 1)

                split(0, 0)
                split(1, 1)
                turned_h(0, 0)
                with dve.Fori(0, NS - 1) as i:
                    for k in range(K):
                        t = K * i + k
                        split(t + 2, k)
                        turned_h(t + 1, k + 1)
                        outputs(t, i, k)
                for k in range(K):
                    t = NTILE - K + k
                    if t + 2 < NTILE:
                        split(t + 2, k)
                    if t + 1 < NTILE:
                        turned_h(t + 1, k + 1)
                    outputs(t, NS - 1, k)


def moe_combine(nc, X, ys, rows_of, gap, out):
    with ExitStack() as ctx:
        sb = lambda n, s, d=F32: ctx.enter_context(nc.sbuf_tensor(f"comb_{n}", s, d))
        sem = lambda n: nc.alloc_semaphore(f"comb_{n}")
        th = sb("th", [P, B])
        wt = sb("wt", [P, NR, B])
        J = sb("J", [P, 2, TT * NR], U32)
        Y = sb("Y", [P, 2, TT, NR, D])
        norm = Norm(nc, ctx, "moe_norm")
        tanh_ready, weights_ready, j_ready, first_added, apart, stored = (
            sem("tanh_ready"), sem("weights_ready"), sem("j_ready"), sem("first_added"), sem("apart"), sem("stored"))
        fetched = [[sem(f"fetched{h}{j}") for j in range(TT)] for h in range(2)]
        NI = B // (2 * TT)

        with nc.Block() as block:

            @block.scalar
            def _(act):
                act.activation(th[:, :], gap[:, :], ACT.Tanh, scale=0.5).then_inc(tanh_ready, 1)

            @block.gpsimd
            def _(pool):

                def fetch(i, h):
                    g = 2 * i + h
                    for j in range(TT):
                        pool.wait_ge(fetched[h][j], 16 * NR * i)
                    pool.tensor_copy(J[:, h, :], rows_of[:, ds(TT * NR * g, TT * NR)]).then_inc(j_ready, 1)
                    wait_apart(pool, apart, j_ready, g + 1)
                    for j in range(TT):
                        wait_apart(pool, apart, norm.rows_ready, TT * 2 * i)
                        for r in range(NR):
                            pool.indirect_dma_start(Y[:, h, j, r, :], None, ys,
                                                    bass.IndirectOffsetOnAxis(ap=J[:, h, NR * j + r:NR * j + r + 1], axis=0))\
                                .then_inc(fetched[h][j], 16)

                norm_consts(pool, norm)
                fetch(0, 0)
                fetch(0, 1)
                with pool.Fori(0, NI - 1) as i:
                    for h in range(2):
                        norm_rstd(pool, norm, 2 * i + h)
                        fetch(i + 1, h)
                for h in range(2):
                    norm_rstd(pool, norm, 2 * (NI - 1) + h)

            @block.vector
            def _(dve):
                dve.wait_ge(tanh_ready, 1)
                dve.tensor_scalar(wt[:, 0, :], th[:, :], 0.5, 0.5, ALU.mult, ALU.add).then_inc(weights_ready, 1)
                dve.tensor_scalar(wt[:, 1, :], th[:, :], -0.5, 0.5, ALU.mult, ALU.add).then_inc(weights_ready, 1)
                dve.wait_ge(weights_ready, 2)

                def add(i, h):
                    g = 2 * i + h
                    for j in range(TT):
                        x = tile(X, TT * g + j)
                        dve.wait_ge(fetched[h][j], 16 * NR * (i + 1))
                        dve.scalar_tensor_tensor(x, Y[:, h, j, 0, :], wt[:, 0, ds(TT * g + j, 1)], x, ALU.mult, ALU.add)\
                           .then_inc(first_added, 1)
                    for j in range(TT):
                        x = tile(X, TT * g + j)
                        dve.wait_ge(first_added, TT * g + j + 1)
                        dve.scalar_tensor_tensor(x, Y[:, h, j, 1, :], wt[:, 1, ds(TT * g + j, 1)], x, ALU.mult, ALU.add)\
                           .then_inc(norm.rows_ready, 1)
                    for j in range(TT):
                        norm_stats(dve, norm, X, g, j)
                    for j in range(TT):
                        norm_aggr(dve, norm, g, j)

                def apply(g):
                    for j in range(TT):
                        norm_apply(dve, norm, X, g, j)

                with dve.Fori(0, NI) as i:
                    for h in range(2):
                        add(i, h)
                        apply(2 * i + h)

            @block.sync
            def _(sp):
                n = TT * D
                with sp.Fori(0, B // TT) as g:
                    sp.wait_ge(norm.normed, TT * g + TT)
                    sp.dma_start(out[:, ds(n * g, n)], group(X, TT * g, TT).rearrange("p b n -> p (b n)")).then_inc(stored, 16)
                sp.wait_ge(stored, 16 * (B // TT))


KH = 8
HD = 16
QH = 32
QG = QH // KH
SL = 4
ORDER = (0, 2, 1, 3)
VW = HD + 1


KVW = KH * P + 2 * KH * VW


def context(nc, ctx_dram, kv_dram, idh):
    with ExitStack() as ctx:
        sb = lambda n, s, d=F32: ctx.enter_context(nc.sbuf_tensor(f"ctx_{n}", s, d))
        sem = lambda n: nc.alloc_semaphore(f"ctx_{n}")
        NB = 4
        BB = B // NB
        C = sb("C", [P, B * P])
        K = sb("K", [P, B * KH, SL, HD], F16)
        KT = sb("KT", [SL * HD, B, KH, P], F16)
        V = sb("V", [P, B, 2, KH, VW], F16)
        psK = [ctx.enter_context(nc.psum_tensor(f"ctx_psK{k}", [SL * HD, KH * P], F16)) for k in range(4)]
        loaded = [sem(f"loaded{n}") for n in range(NB)]
        zeros_set, hi_made, lo_made, copied = sem("zeros_set"), sem("hi_made"), sem("lo_made"), sem("copied")
        vhi_made, v_made, turned, out_act, out_dve = (sem("vhi_made"), sem("v_made"), sem("turned"), sem("out_act"),
                                                      sem("out_dve"))
        stored = sem("stored")
        c = C[:, :].rearrange("p (h d) -> p h d", d=HD)
        c4 = C[:, :].rearrange("p (b h d) -> p b h d", d=HD, h=KH)

        with nc.Block() as block:

            @block.sync
            def _(sp):
                for n in range(NB):
                    w = slice(n * BB * P, (n + 1) * BB * P)
                    sp.dma_start(C[:, w], ctx_dram[:, w]).then_inc(loaded[n], 16)
                for n in range(NB):
                    w = slice(n * BB, (n + 1) * BB)
                    sp.wait_ge(v_made, n + 1)
                    sp.dma_start(kv_dram[:, w, KH * P:KVW], V[:, w, :, :, :].rearrange("p b a h d -> p b (a h d)"))\
                      .then_inc(stored, 16)
                    sp.wait_ge(out_act, BB // 2 * (n + 1))
                    sp.wait_ge(out_dve, BB // 2 * (n + 1))
                    sp.dma_start(kv_dram[0:SL * HD, w, 0:KH * P], KT[:, w, :, :].rearrange("p b a t -> p b (a t)"))\
                      .then_inc(stored, 16)
                sp.wait_ge(stored, 32 * NB)

            @block.gpsimd
            def _(pool):
                pool.memset(K[:, :, 3, :], 0.0).then_inc(zeros_set, 1)
                pool.memset(V[:, :, 0, :, HD:VW], 1.0).then_inc(zeros_set, 1)
                pool.memset(V[:, :, 1, :, HD:VW], 0.0).then_inc(zeros_set, 1)
                pool.wait_ge(zeros_set, 3)
                for n in range(NB):
                    w = slice(n * BB, (n + 1) * BB)
                    pool.wait_ge(vhi_made, n + 1)
                    pool.tensor_tensor(V[:, w, 1, :, 0:HD], c4[:, w], V[:, w, 0, :, 0:HD], ALU.subtract).then_inc(v_made, 1)

            @block.scalar
            def _(act):

                def keys_out(n):
                    for b in range(n * BB, (n + 1) * BB, 2):
                        act.wait_ge(turned, b + 1)
                        act.activation(KT[:, b, :, :].rearrange("p a t -> p (a t)"), psK[b % 4][:, :], ACT.Copy).then_inc(out_act, 1)

                for n in range(NB):
                    w, h = slice(n * BB, (n + 1) * BB), slice(n * BB * KH, (n + 1) * BB * KH)
                    act.wait_ge(loaded[n], 16)
                    act.activation(K[:, h, 2, :], c[:, h], ACT.Copy).then_inc(copied, 1)
                    act.activation(V[:, w, 0, :, 0:HD], c4[:, w], ACT.Copy).then_inc(vhi_made, 1)
                    if n:
                        keys_out(n - 1)
                keys_out(NB - 1)

            @block.vector
            def _(dve):

                def keys_out(n):
                    for b in range(n * BB + 1, (n + 1) * BB, 2):
                        dve.wait_ge(turned, b + 1)
                        dve.tensor_copy(KT[:, b, :, :].rearrange("p a t -> p (a t)"), psK[b % 4][:, :]).then_inc(out_dve, 1)

                for n in range(NB):
                    h = slice(n * BB * KH, (n + 1) * BB * KH)
                    dve.wait_ge(loaded[n], 16)
                    dve.tensor_copy(K[:, h, 0, :], c[:, h]).then_inc(hi_made, 1)
                    dve.wait_ge(hi_made, n + 1)
                    dve.tensor_tensor(K[:, h, 1, :], c[:, h], K[:, h, 0, :], ALU.subtract).then_inc(lo_made, 1)
                    if n:
                        keys_out(n - 1)
                keys_out(NB - 1)

            @block.tensor
            def _(pe):
                pe.wait_ge(zeros_set, 3)
                for b in range(B):
                    if b % BB == 0:
                        pe.wait_ge(lo_made, b // BB + 1)
                        pe.wait_ge(copied, b // BB + 1)
                    if b >= 4:
                        pe.wait_ge(out_dve if b % 2 else out_act, (b - 4) // 2 + 1)
                    for a in range(KH):
                        k = K[:, b * KH + a, :, :].rearrange("p s d -> p (s d)")
                        t = pe.transpose(psK[b % 4][:, a * P:(a + 1) * P], k, idh[:, :])
                    t.then_inc(turned, 1)


def cross_attention(nc, name, X, kv_dram, idh, nsel, gmask):
    with ExitStack() as ctx:
        sb = lambda n, s, d=F32: ctx.enter_context(nc.sbuf_tensor(f"{name}_{n}", s, d))
        ps = lambda n, s, d=F32: ctx.enter_context(nc.psum_tensor(f"{name}_{n}", s, d))
        sem = lambda n: nc.alloc_semaphore(f"{name}_{n}")
        LAG = 3
        KT = sb("KT", [P, 3, 2, KH, P], F16)
        V = sb("V", [P, 3, 2, KH, VW], F16)
        Q = sb("Q", [P, QH, SL, HD], F16)
        QT = sb("QT", [P, 3, 16, P], F16)
        Mx = sb("Mx", [P, QH], F16)
        MD = sb("MD", [QH, 3, QG, P], F16)
        W32, Wh, Wl = sb("W32", [P, KH, GT]), sb("Wh", [P, KH, GT], F16), sb("Wl", [P, KH, GT], F16)
        rinv = sb("rinv", [P, QH])
        O = sb("O", [P, D])
        psQ = ps("psQ", [P, 8, P], F16)
        psM = ps("psM", [QH, P], F16)
        psS = [ps(f"psS{k}", [P, QG, P]) for k in range(2)]
        psW = [ps(f"psW{k}", [P, GT]) for k in range(2)]
        psO = [ps(f"psO{k}", [P, 16, VW]) for k in range(2)]
        norm = Norm(nc, ctx, f"{name}_norm", 1)
        qh_ready, ql_ready, q_psum, q_ready = sem("qh_ready"), sem("ql_ready"), sem("q_psum"), sem("q_ready")
        s_psum, max_ready, m_psum, md_ready = sem("s_psum"), sem("max_ready"), sem("m_psum"), sem("md_ready")
        w_psum, w32_ready, wh_ready, wl_dve, wl_pool = (sem("w_psum"), sem("w32_ready"), sem("wh_ready"), sem("wl_dve"),
                                                        sem("wl_pool"))
        kv_loaded = [sem(f"kv_loaded{u}") for u in range(3)]
        zeros_set, pv_done, rinv_ready, o_ready = sem("zeros_set"), sem("pv_done"), sem("rinv_ready"), sem("o_ready")
        qh2_ready = sem("qh2_ready")


        LO_DVE = (0, 2, 4)

        def first(b):
            return type(b) is int and b == 0

        def lo_count(k):
            if k in LO_DVE:
                return wl_dve, len(LO_DVE), LO_DVE.index(k) + 1
            return wl_pool, KH - len(LO_DVE), k + 1 - sum(d < k for d in LO_DVE)


        def q_hi(pool, b):
            pool.wait_ge(q_psum, 2 * b)
            pool.tensor_copy(Q[:, :, 0, :], tile(X, b).rearrange("p (h d) -> p h d", d=HD)).then_inc(qh_ready, 1)

        def q_hi_again(act, b):
            act.wait_ge(q_psum, 2 * b)
            act.activation(Q[:, :, 1, :], tile(X, b).rearrange("p (h d) -> p h d", d=HD), ACT.Copy).then_inc(qh2_ready, 1)

        def q_lo(pool, b):
            wait_apart(pool, norm.waits_apart, qh_ready, b + 1)
            x = tile(X, b).rearrange("p (h d) -> p h d", d=HD)
            pool.tensor_tensor(Q[:, :, 2, :], x, Q[:, :, 0, :], ALU.subtract).then_inc(ql_ready, 1)

        def turn_q(pe, b, half):
            if half == 0:
                pe.wait_ge(ql_ready, b + 1)
                pe.wait_ge(qh_ready, b + 1)
                pe.wait_ge(qh2_ready, b + 1)
            pe.wait_ge(q_ready, 2 * b + half)
            for n in range(8):
                h = 2 * (8 * half + n)
                q = Q[:, h:h + 2, :, :].rearrange("p h s d -> p (h s d)")
                t = pe.transpose(psQ[:, n, :], q, idh[:, :])
            t.then_inc(q_psum, 1)

        def q_out(act, b, u, half):
            act.wait_ge(q_psum, 2 * b + half + 1)
            act.activation(QT[:, u, 8 * half:8 * half + 8, :].rearrange("p a t -> p (a t)"),
                           psQ[:, :, :].rearrange("p a t -> p (a t)"), ACT.Copy).then_inc(q_ready, 1)

        def scores(pe, b, u, k):
            if k == 0:
                pe.wait_ge(kv_loaded[u], 16 * (b - u) + 48)
            pe.wait_ge(q_ready, 2 * b + 1 + k // 4)
            if not (first(b) and k < 2):
                pe.wait_ge(max_ready, KH * b + k - 1)
            if k == 0:
                pe.wait_ge(zeros_set, 7)
            for a in range(2):
                t = pe.matmul(psS[k % 2][:, 2 * a:2 * a + 2, :], QT[:, u, 2 * k + a, :], KT[:, u, :, k, :], start=True, stop=True)
            t.then_inc(s_psum, 1)

        def load(sp, b, u):
            for e in range(2):
                r = slice(64 * e, 64 * e + 64)
                sp.dma_start(KT[r, u, e, :, :].rearrange("p k t -> p (k t)"),
                             kv_dram[0:64, ds(b, 1), 0:KH * P].rearrange("p a n -> p (a n)")).then_inc(kv_loaded[u], 16)
            sp.dma_start(V[:, u, :, :, :].rearrange("p a k d -> p (a k d)"),
                         kv_dram[:, ds(b, 1), KH * P:KVW].rearrange("p a n -> p (a n)")).then_inc(kv_loaded[u], 16)

        def maxima(dve, b, k):
            dve.wait_ge(s_psum, KH * b + k + 1)
            if k == 0:
                dve.wait_ge(m_psum, b)
            dve.tensor_reduce(Mx[:, QG * k:QG * k + QG], psS[k % 2][:, :, :], AX.X, ALU.max).then_inc(max_ready, 1)

        def turn_max(pe, b):
            pe.wait_ge(max_ready, KH * b + KH)
            pe.wait_ge(md_ready, b)
            pe.transpose(psM[:, :], Mx[:, :], idh[:, :]).then_inc(m_psum, 1)

        def spread_max(dve, b, u):
            dve.wait_ge(m_psum, b + 1)
            dve.tensor_tensor(MD[:, u, :, :], psM[:, :].unsqueeze(1).to_broadcast([QH, QG, P]), gmask, ALU.mult)\
               .then_inc(md_ready, 1)

        def turned_scores(pe, b, u, k):
            if not (first(b) and k < 2):
                pe.wait_ge(wh_ready, KH * b + k - 1)
            if k == 0:
                pe.wait_ge(md_ready, b + 1)
            pe.matmul(psW[k % 2][:, :], nsel[:, k * P:(k + 1) * P], MD[:, u, :, :].rearrange("p g t -> p (g t)"),
                      start=True, stop=False)
            for e in range(2):
                t = pe.matmul(psW[k % 2][:, 2 * P * e:2 * P * e + 2 * P], KT[:, u, e, k, :],
                              QT[:, u, 2 * k:2 * k + 2, :].rearrange("p a t -> p (a t)"), start=False, stop=(e == 1))
            t.then_inc(w_psum, 1)

        def weights(act, b, k):
            act.wait_ge(w_psum, KH * b + k + 1)
            wl, n, m = lo_count(k)
            if not first(b):
                act.wait_ge(wl, n * (b - 1) + m)
            act.activation(W32[:, k, :], psW[k % 2][:, :], ACT.Exp, scale=0.25).then_inc(w32_ready, 1)
            if not first(b):
                act.wait_ge(pv_done, KH * (b - 1) + k + 1)
            act.activation(Wh[:, k, :], psW[k % 2][:, :], ACT.Exp, scale=0.25).then_inc(wh_ready, 1)

        def weights_lo(eng, b, k):
            eng.wait_ge(w32_ready, KH * b + k + 1)
            eng.wait_ge(wh_ready, KH * b + k + 1)
            if not first(b):
                eng.wait_ge(pv_done, KH * (b - 1) + k + 1)
            eng.tensor_tensor(Wl[:, k, :], W32[:, k, :], Wh[:, k, :], ALU.subtract)\
               .then_inc(lo_count(k)[0], 1)

        def values(pe, b, u, k):
            pe.wait_ge(wh_ready, KH * b + k + 1)
            wl, n, m = lo_count(k)
            pe.wait_ge(wl, n * b + m)
            if k % 4 == 0 and not first(b):
                pe.wait_ge(o_ready, 2 * (b - 1) + k // 4 + 1)
            v = [V[:, u, h, k, :] for h in range(2)]
            for g in range(QG):
                h = QG * k + g
                at = ORDER.index(g) * P
                w = slice(at, at + P)
                out = psO[h // 16][:, h % 16, :]
                pe.matmul(out, Wh[:, k, w], v[0], start=True, stop=False)
                pe.matmul(out, Wh[:, k, w], v[1], start=False, stop=False)
                t = pe.matmul(out, Wl[:, k, w], v[0], start=False, stop=True)
            t.then_inc(pv_done, 1)

        def divide(dve, b, a):
            r = rinv[:, 16 * a:16 * a + 16]
            dve.wait_ge(pv_done, KH * b + 4 * a + 4)
            dve.reciprocal(r, psO[a][:, :, HD]).then_inc(rinv_ready, 1)
            dve.wait_ge(rinv_ready, 2 * b + a + 1)
            dve.tensor_tensor(O[:, 256 * a:256 * a + 256].rearrange("p (h d) -> p h d", d=HD), psO[a][:, :, 0:HD],
                              r.unsqueeze(2).to_broadcast([P, 16, HD]), ALU.mult).then_inc(o_ready, 1)

        def add(dve, b):
            dve.wait_ge(o_ready, 2 * b + 2)
            x = tile(X, b)
            dve.tensor_tensor(x, x, O[:, :], ALU.add).then_inc(norm.rows_ready, 1)

        def every_sequence(eng, sequence):
            for b in range(2):
                sequence(b, b, lambda d: b + d >= 0)
            with eng.Fori(0, (B - 5) // 3) as r:
                for v in range(3):
                    sequence(r * 3 + (v + 2), (v + 2) % 3, lambda d: True)
            for b in range(B - 3, B):
                sequence(b, b % 3, lambda d: b + d < B)

        with nc.Block() as block:

            @block.sync
            def _(sp):
                for b in range(3):
                    load(sp, b, b)

                def reload(b, u):
                    sp.wait_ge(w_psum, KH * (b + 1))
                    sp.wait_ge(pv_done, KH * (b + 1))
                    load(sp, b + 3, u)

                with sp.Fori(0, (B - 5) // 3) as r:
                    for v in range(3):
                        reload(r * 3 + v, v)
                for b in range(B - 5, B - 3):
                    reload(b, b % 3)

            @block.gpsimd
            def _(pool):
                norm_consts(pool, norm)
                for b in range(3):
                    q_hi(pool, b)
                    q_lo(pool, b)

                def sequence(b, u, has):
                    weights_lo(pool, b, 1)
                    weights_lo(pool, b, 3)
                    weights_lo(pool, b, 5)
                    if has(3):
                        q_hi(pool, b + 3)
                    weights_lo(pool, b, 6)
                    weights_lo(pool, b, 7)
                    if has(-1):
                        norm_rstd(pool, norm, b - 1)
                    if has(3):
                        q_lo(pool, b + 3)

                every_sequence(pool, sequence)
                norm_rstd(pool, norm, B - 1)

            @block.tensor
            def _(pe):

                def sequence(b, u, has):
                    for k in range(KH):
                        turned_scores(pe, b, u, k)
                        if k < KH - 1 and has(1):
                            scores(pe, b + 1, (u + 1) % 3, k + 1)
                        if k >= LAG:
                            values(pe, b, u, k - LAG)
                        elif has(-1):
                            values(pe, b - 1, (u + 2) % 3, KH + k - LAG)
                        if k in (3, 5) and has(2):
                            turn_q(pe, b + 2, k // 4)
                    if has(1):
                        turn_max(pe, b + 1)
                    if has(2):
                        scores(pe, b + 2, (u + 2) % 3, 0)

                pe.wait_ge(zeros_set, 7)
                for half in range(2):
                    turn_q(pe, 0, half)
                for k in range(KH):
                    scores(pe, 0, 0, k)
                turn_max(pe, 0)
                for half in range(2):
                    turn_q(pe, 1, half)
                scores(pe, 1, 1, 0)
                every_sequence(pe, sequence)
                for k in range(KH - LAG, KH):
                    values(pe, B - 1, (B - 1) % 3, k)

            @block.scalar
            def _(act):

                def sequence(b, u, has):
                    for k in range(KH):
                        weights(act, b, k)
                        if k in (3, 5) and has(2):
                            q_out(act, b + 2, (u + 2) % 3, k // 4)
                    if has(3):
                        q_hi_again(act, b + 3)

                for b in range(2):
                    q_hi_again(act, b)
                    for half in range(2):
                        q_out(act, b, b, half)
                q_hi_again(act, 2)
                every_sequence(act, sequence)

            @block.vector
            def _(dve):

                def sequence(b, u, has):
                    for k in range(KH):
                        if k < KH - 1 and has(1):
                            maxima(dve, b + 1, k + 1)
                        if k - 1 in LO_DVE:
                            weights_lo(dve, b, k - 1)
                        if k == 2 and has(-2):
                            norm_apply(dve, norm, X, b - 2, 0)
                        if k == 3 and has(-1):
                            divide(dve, b - 1, 1)
                        if k == 4 and has(-1):
                            add(dve, b - 1)
                        if k == 5 and has(-1):
                            norm_stats(dve, norm, X, b - 1, 0)
                        if k == 6 and has(-1):
                            norm_aggr(dve, norm, b - 1, 0)
                    if has(1):
                        spread_max(dve, b + 1, (u + 1) % 3)
                    divide(dve, b, 0)
                    if has(2):
                        maxima(dve, b + 2, 0)

                dve.memset(Q[:, :, 3, :], 0.0).then_inc(zeros_set, 1)
                for u in range(3):
                    for e in range(2):
                        dve.memset(KT[64 - 64 * e:128 - 64 * e, u, e, :, :], 0.0).then_inc(zeros_set, 1)
                for k in range(KH):
                    maxima(dve, 0, k)
                spread_max(dve, 0, 0)
                maxima(dve, 1, 0)
                every_sequence(dve, sequence)
                norm_apply(dve, norm, X, B - 2, 0)
                divide(dve, B - 1, 1)
                add(dve, B - 1)
                norm_stats(dve, norm, X, B - 1, 0)
                norm_aggr(dve, norm, B - 1, 0)
                norm_apply(dve, norm, X, B - 1, 0)


LAT = 128
LA_LOADS = 16 * 11
DCMP = 64


def latent_attention(nc, X, w, idf):
    with ExitStack() as ctx:
        sb = lambda n, s, d=F32: ctx.enter_context(nc.sbuf_tensor(f"la_{n}", s, d))
        sem = lambda n: nc.alloc_semaphore(f"la_{n}")
        bank = [ctx.enter_context(nc.psum_tensor(f"la_bank{k}", [P, GT], F32)) for k in range(8)]
        WkvT = sb("WkvT", [P, DC, LAT])
        Wkv = sb("Wkv", [P, D])
        WoT = sb("WoT", [P, D])
        WcT = sb("WcT", [P, DCMP])
        Wqk = sb("Wqk", [DCMP, 4, DCMP])
        WvT = sb("WvT", [DCMP, DCMP])
        WlT = sb("WlT", [DCMP, LAT])
        gb = sb("gb", [DCMP, 2])
        rope = sb("rope", [DCMP, 2, GT])
        mask = sb("mask", [P, P])
        bout = sb("bout", [P, D])
        X4 = sb("X4", [P, GS, D])
        XT = sb("XT", [P, DC, GT])
        x_copied = sem("x_copied")
        LT = sb("LT", [P, GT])
        CN = sb("CN", [P, GS, DCMP])
        CT = sb("CT", [DCMP, GT])
        RT = sb("RT", [DCMP, 4, GT])
        QK = sb("QK", [DCMP, 2, GT])
        V = sb("V", [P, GS, DCMP])
        S = sb("S", [P, GS, P])
        E = sb("E", [P, GS, P])
        ET = sb("ET", [P, GS, P])
        OT = sb("OT", [DCMP, GT])
        ZT = sb("ZT", [P, GT])
        mx, nmx = sb("mx", [P, GS]), sb("nmx", [P, GS])
        rs, rinv = sb("rs", [P, GS]), sb("rinv", [P, GS])
        norm = Norm(nc, ctx, "la_norm")
        cn = Norm(nc, ctx, "la_cnorm")
        loaded, w_summed = sem("loaded"), sem("w_summed")
        xT_psum, xT_ready, lat_psum, lat_ready = sem("xT_psum"), sem("xT_ready"), sem("lat_psum"), sem("lat_ready")
        c_psum, cn_ready, cT_psum, cT_ready = sem("c_psum"), sem("cn_ready"), sem("cT_psum"), sem("cT_ready")
        qk_psum, rope_mult, qk_ready, v_psum, v_ready = (sem("qk_psum"), sem("rope_mult"), sem("qk_ready"), sem("v_psum"),
                                                         sem("v_ready"))
        s_psum, s_masked, mx_ready, nmx_ready, e_ready = (sem("s_psum"), sem("s_masked"), sem("mx_ready"), sem("nmx_ready"),
                                                          sem("e_ready"))
        eT_psum, eT_ready, oT_psum, oT_ready = sem("eT_psum"), sem("eT_ready"), sem("oT_psum"), sem("oT_ready")
        zT_psum, zT_ready, out_psum, rinv_ready, biased = (sem("zT_psum"), sem("zT_ready"), sem("out_psum"),
                                                           sem("rinv_ready"), sem("biased"))
        j4 = lambda t: t.rearrange("p (j n) -> p j n", j=GS)

        with nc.Block() as block:

            @block.sync
            def _(sp):
                pairs = [(WkvT[:, :, :].rearrange("p c n -> p (c n)"), w["WkvT"]), (Wkv[:, :], w["Wkv"]),
                         (WoT[:, :], w["WoT"]), (WcT[:, :], w["WcT"]),
                         (Wqk[:, :, :].rearrange("p c n -> p (c n)"), w["Wqk"]), (WvT[:, :], w["WvT"]),
                         (WlT[:, :], w["WlT"]), (gb[:, :], w["gb"]), (rope[:, :, :].rearrange("p c n -> p (c n)"), w["rope"]),
                         (mask[:, :], w["mask"]), (bout[:, :], w["bout"].partition_broadcast(P))]
                for to, of in pairs:
                    sp.dma_start(to, of).then_inc(loaded, 16)
                sp.wait_ge(loaded, LA_LOADS)

                def copy(i):
                    sp.dma_start(X4[:, :, :], group(X, GS * i)).then_inc(x_copied, 16)

                copy(0)
                with sp.Fori(0, NG - 1) as i:
                    sp.wait_ge(xT_psum, DC * i + DC)
                    copy(i + 1)
                sp.wait_ge(x_copied, 16 * NG)


            @block.gpsimd
            def _(pool):
                norm_consts(pool, norm)
                norm_consts(pool, cn)
                pool.wait_ge(loaded, LA_LOADS)
                pool.tensor_tensor(Wkv[:, :], Wkv[:, :], WoT[:, :], ALU.add).then_inc(w_summed, 1)
                norm_rstd(pool, cn, 0)

                def bias(i):
                    wait_apart(pool, norm.waits_apart, xT_psum, DC * i + DC)
                    for j in range(GS):
                        x = tile(X, GS * i + j)
                        pool.tensor_tensor(x, x, bout[:, :], ALU.add).then_inc(biased, 1)

                with pool.Fori(0, NG - 1) as i:
                    bias(i)
                    norm_rstd(pool, cn, i + 1)
                    norm_rstd(pool, norm, i)
                bias(NG - 1)
                norm_rstd(pool, norm, NG - 1)

            @block.tensor
            def _(pe):

                def turn_x(i):
                    pe.wait_ge(x_copied, 16 * i + 16)
                    pe.wait_ge(lat_ready, i)
                    for c in range(DC):
                        pe.wait_ge(xT_ready, DC * i + max(0, c - 1))
                        if c == 0:
                            pe.wait_ge(lat_psum, i)
                        for j in range(GS):
                            x = X4[:, j, c * P:(c + 1) * P]
                            t = pe.transpose(bank[c % 2][:, j * P:(j + 1) * P], x, idf[:, :])
                        t.then_inc(xT_psum, 1)

                def latents(i):
                    pe.wait_ge(xT_ready, DC * i + DC)
                    for c in range(DC):
                        t = pe.matmul(bank[0][:, :], WkvT[:, c, :], XT[:, c, :], start=(c == 0), stop=(c == DC - 1))
                    t.then_inc(lat_psum, 1)

                def compressed(i):
                    pe.wait_ge(lat_ready, i + 1)
                    pe.wait_ge(cn_ready, GS * i)
                    for j in range(GS):
                        t = pe.matmul(bank[2][:, j * DCMP:(j + 1) * DCMP], LT[:, j * P:(j + 1) * P], WcT[:, :],
                                      start=True, stop=True)
                    t.then_inc(c_psum, 1)

                def turn_c(i):
                    wait_apart(pe, cn.waits_apart, v_ready, i)
                    wait_apart(pe, cn.waits_apart, cn_ready, GS * i + GS)
                    for j in range(GS):
                        t = pe.transpose(bank[3][0:DCMP, j * P:(j + 1) * P], CN[:, j, :], idf[:, :])
                    t.then_inc(cT_psum, 1)

                def queries_keys(i):
                    wait_apart(pe, norm.waits_apart, norm.rows_ready, GS * i)
                    wait_apart(pe, norm.waits_apart, cT_ready, i + 1)
                    for n in range(4):
                        pe.matmul(bank[4 + n][0:DCMP, :], Wqk[:, n, :], CT[:, :], start=True, stop=True).then_inc(qk_psum, 1)
                    for j in range(GS):
                        t = pe.matmul(bank[3][:, j * DCMP:(j + 1) * DCMP], CT[:, j * P:(j + 1) * P], WvT[:, :],
                                      start=True, stop=True)
                    t.then_inc(v_psum, 1)

                def scores(i):
                    pe.wait_ge(qk_ready, 2 * i + 2)
                    for j in range(GS):
                        c = slice(j * P, (j + 1) * P)
                        t = pe.matmul(bank[4][:, c], QK[:, 0, c], QK[:, 1, c], start=True, stop=True)
                    t.then_inc(s_psum, 1)

                def turn_e(i):
                    pe.wait_ge(e_ready, GS * i + GS)
                    for j in range(GS):
                        t = pe.transpose(bank[5][:, j * P:(j + 1) * P], E[:, j, :], idf[:, :])
                    t.then_inc(eT_psum, 1)

                def outputs(i):
                    pe.wait_ge(eT_ready, i + 1)
                    pe.wait_ge(v_ready, i + 1)
                    for j in range(GS):
                        t = pe.matmul(bank[6][0:DCMP, j * P:(j + 1) * P], V[:, j, :], ET[:, j, :], start=True, stop=True)
                    t.then_inc(oT_psum, 1)
                    pe.wait_ge(oT_ready, i + 1)
                    pe.matmul(bank[7][:, :], WlT[:, :], OT[:, :], start=True, stop=True).then_inc(zT_psum, 1)
                    pe.wait_ge(zT_ready, i + 1)
                    for j in range(GS):
                        pe.matmul(bank[4 + j][:, :], ZT[:, j * P:(j + 1) * P], Wkv[:, :], start=True, stop=True)\
                          .then_inc(out_psum, 1)

                pe.wait_ge(loaded, LA_LOADS)
                pe.wait_ge(w_summed, 1)
                turn_x(0)
                latents(0)
                compressed(0)
                turn_c(0)
                with pe.Fori(0, NG - 1) as i:
                    queries_keys(i)
                    turn_x(i + 1)
                    scores(i)
                    latents(i + 1)
                    turn_e(i)
                    compressed(i + 1)
                    outputs(i)
                    turn_c(i + 1)
                queries_keys(NG - 1)
                scores(NG - 1)
                turn_e(NG - 1)
                outputs(NG - 1)

            @block.scalar
            def _(act):

                def x_out(i):
                    for c in range(DC):
                        act.wait_ge(xT_psum, DC * i + c + 1)
                        if c == 0:
                            act.wait_ge(lat_psum, i)
                        act.activation(XT[:, c, :], bank[c % 2][:, :], ACT.Copy).then_inc(xT_ready, 1)

                def latent_out(i):
                    act.wait_ge(lat_psum, i + 1)
                    act.wait_ge(c_psum, i)
                    act.activation(LT[:, :], bank[0][:, :], ACT.Copy).then_inc(lat_ready, 1)

                def v_out(i):
                    act.wait_ge(v_psum, i + 1)
                    act.wait_ge(oT_psum, i)
                    act.activation(V[:, :, :].rearrange("p j n -> p (j n)"), bank[3][:, 0:GS * DCMP], ACT.Copy)\
                       .then_inc(v_ready, 1)

                def exps(i):
                    act.wait_ge(nmx_ready, i + 1)
                    act.wait_ge(eT_psum, i)
                    act.wait_ge(rinv_ready, i)
                    for j in range(GS):
                        act.activation(E[:, j, :], S[:, j, :], ACT.Exp, bias=nmx[:, j:j + 1], scale=0.125,
                                       accum_out=rs[:, j:j + 1]).then_inc(e_ready, 1)

                def e_out(i):
                    act.wait_ge(eT_psum, i + 1)
                    act.wait_ge(oT_psum, i)
                    act.activation(ET[:, :, :].rearrange("p j n -> p (j n)"), bank[5][:, :], ACT.Copy).then_inc(eT_ready, 1)

                def z_out(i):
                    act.wait_ge(zT_psum, i + 1)
                    act.wait_ge(out_psum, GS * i)
                    act.activation(ZT[:, :], bank[7][:, :], ACT.Copy).then_inc(zT_ready, 1)

                x_out(0)
                latent_out(0)
                with act.Fori(0, NG - 1) as i:
                    v_out(i)
                    x_out(i + 1)
                    exps(i)
                    latent_out(i + 1)
                    e_out(i)
                    z_out(i)
                v_out(NG - 1)
                exps(NG - 1)
                e_out(NG - 1)
                z_out(NG - 1)

            @block.vector
            def _(dve):

                def compressed_norm(i):
                    wait_apart(dve, cn.waits_apart, c_psum, i + 1)
                    for j in range(GS):
                        dve.bn_stats(cn.stats[:, j, :], bank[2][:, j * DCMP:(j + 1) * DCMP]).then_inc(cn.stats_ready, 1)
                    for j in range(GS):
                        norm_aggr(dve, cn, i, j)
                    dve.wait_ge(cn.rstd_ready, i + 1)
                    dve.wait_ge(cT_psum, i)
                    for j in range(GS):
                        dve.tensor_scalar(CN[:, j, :], bank[2][:, j * DCMP:(j + 1) * DCMP], cn.mv[:, j, 0:1],
                                          cn.rstd[:, j:j + 1], ALU.subtract, ALU.mult).then_inc(cn_ready, 1)

                def c_out(i):
                    dve.wait_ge(cT_psum, i + 1)
                    dve.wait_ge(v_psum, i)
                    dve.tensor_scalar(CT[:, :], bank[3][0:DCMP, :], gb[:, 0:1], gb[:, 1:2], ALU.mult, ALU.add)\
                       .then_inc(cT_ready, 1)

                def apply_rope(i):
                    dve.wait_ge(s_psum, i)
                    for n in range(4):
                        dve.wait_ge(qk_psum, 4 * i + n + 1)
                        dve.tensor_tensor(RT[:, n, :], bank[4 + n][0:DCMP, :], rope[:, n % 2, :], ALU.mult)\
                           .then_inc(rope_mult, 1)
                    for n in range(2):
                        dve.wait_ge(rope_mult, 4 * i + 2 * n + 2)
                        dve.tensor_tensor(QK[:, n, :], RT[:, 2 * n, :], RT[:, 2 * n + 1, :], ALU.add).then_inc(qk_ready, 1)

                def masked(i):
                    dve.wait_ge(s_psum, i + 1)
                    dve.wait_ge(e_ready, GS * i)
                    dve.tensor_tensor(S[:, :, :], j4(bank[4][:, :]), mask[:, :].unsqueeze(1).to_broadcast([P, GS, P]), ALU.add)\
                       .then_inc(s_masked, 1)
                    dve.wait_ge(s_masked, i + 1)
                    dve.tensor_reduce(mx[:, :], S[:, :, :], AX.X, ALU.max).then_inc(mx_ready, 1)
                    dve.wait_ge(mx_ready, i + 1)
                    dve.tensor_scalar(nmx[:, :], mx[:, :], -0.125, None, ALU.mult).then_inc(nmx_ready, 1)

                def o_out(i):
                    dve.wait_ge(e_ready, GS * i + GS)
                    dve.reciprocal(rinv[:, :], rs[:, :]).then_inc(rinv_ready, 1)
                    dve.wait_ge(oT_psum, i + 1)
                    dve.wait_ge(zT_psum, i)
                    dve.tensor_copy(OT[:, :], bank[6][0:DCMP, :]).then_inc(oT_ready, 1)

                def add(i):
                    dve.wait_ge(rinv_ready, i + 1)
                    for j in range(GS):
                        dve.wait_ge(out_psum, GS * i + j + 1)
                        dve.wait_ge(biased, GS * i + j + 1)
                        x = tile(X, GS * i + j)
                        dve.scalar_tensor_tensor(x, bank[4 + j][:, :], rinv[:, j:j + 1], x, ALU.mult, ALU.add)\
                           .then_inc(norm.rows_ready, 1)
                    for j in range(GS):
                        norm_stats(dve, norm, X, i, j)
                    for j in range(GS):
                        norm_aggr(dve, norm, i, j)
                    for j in range(GS):
                        norm_apply(dve, norm, X, i, j)

                dve.wait_ge(loaded, LA_LOADS)
                compressed_norm(0)
                c_out(0)
                with dve.Fori(0, NG - 1) as i:
                    apply_rope(i)
                    masked(i)
                    compressed_norm(i + 1)
                    o_out(i)
                    add(i)
                    c_out(i + 1)
                apply_rope(NG - 1)
                masked(NG - 1)
                o_out(NG - 1)
                add(NG - 1)


CT = 16
NCT = P // CT
LC = 2 * P


def hyena_taps(nc, kerT, dskip, taps):
    with ExitStack() as ctx:
        sb = lambda n, s, d=F32: ctx.enter_context(nc.sbuf_tensor(f"ht_{n}", s, d))
        sem = lambda n: nc.alloc_semaphore(f"ht_{n}")
        E = sb("E", [P, 2, D])
        Dk = sb("Dk", [P, D])
        H = [sb("Eh", [P, 2, D], F16), sb("El", [P, 2, D], F16)]
        loaded, added, hi_made, lo_made, stored = sem("loaded"), sem("added"), sem("hi_made"), sem("lo_made"), sem("stored")
        with nc.Block() as block:

            @block.sync
            def _(sp):
                sp.dma_start(E[:, :, :].rearrange("p a c -> p (a c)"), kerT).then_inc(loaded, 16)
                sp.dma_start(Dk[:, :], dskip).then_inc(loaded, 16)
                for k, made in enumerate((hi_made, lo_made)):
                    sp.wait_ge(made, 1)
                    for a in range(2):
                        sp.dma_start(taps[k, :, a * P:(a + 1) * P, :].rearrange("n i c -> i n c"),
                                     H[k][:, a, :].rearrange("p (n c) -> p n c", c=CT)).then_inc(stored, 16)
                sp.wait_ge(stored, 64)

            @block.vector
            def _(dve):
                dve.wait_ge(loaded, 32)
                dve.tensor_tensor(E[:, 0, :], E[:, 0, :], Dk[:, :], ALU.add).then_inc(added, 1)
                dve.wait_ge(added, 1)
                dve.tensor_scalar(H[0][:, :, :], E[:, :, :], WS, None, ALU.mult).then_inc(hi_made, 1)
                dve.wait_ge(hi_made, 1)
                flat = lambda t: t[:, :, :].rearrange("p a c -> p (a c)")
                dve.scalar_tensor_tensor(flat(H[1]), flat(E), WS, flat(H[0]), ALU.mult, ALU.subtract).then_inc(lo_made, 1)


def hyena(nc, X, w, taps, idf, flip):
    with ExitStack() as ctx:
        sb = lambda n, s, d=F32: ctx.enter_context(nc.sbuf_tensor(f"hy_{n}", s, d))
        sem = lambda n: nc.alloc_semaphore(f"hy_{n}")
        bank = [ctx.enter_context(nc.psum_tensor(f"hy_bank{k}", [P, GT], F32)) for k in range(8)]
        T = B * P
        xflat = X[:, :, :].rearrange("p b n -> p (b n)").bitcast(F16)
        XT = [xflat[:, k * DC * T:(k + 1) * DC * T] for k in range(2)]
        load_split(nc, "hyx", [(w["xT"], XT[0], XT[1])], scale=1.0)
        XT = [x.rearrange("p (c t) -> p c t", c=DC) for x in XT]
        Y = sb("Y", [P, DC, T])
        cst = sb("cst", [P, DC, 11])
        with ExitStack() as ctx1:
            sb1 = lambda n, s, d=F32: ctx1.enter_context(nc.sbuf_tensor(f"hy_{n}", s, d))
            W32 = sb1("W32", [P, DC * 3 * P])
            Wh, Wl = sb1("Wh", [P, DC, 3, P], F16), sb1("Wl", [P, DC, 3, P], F16)
            pad = sb1("pad", [P, 2, GS, P + 2])
            K = sb1("K", [P, GT])
            Vv = sb1("Vv", [P, GT])
            KVh, KVl = sb1("KVh", [P, P, B], F16), sb1("KVl", [P, P, B], F16)
            TP = sb1("TP", [P, 2, 2, P, CT], F16)
            C = sb1("C", [P, B, P])
            loaded, w_loaded, zeros_set = sem("loaded"), sem("w_loaded"), sem("zeros_set")
            waits_apart = sem("waits_apart")
            wh_made, wl_made = sem("wh_made"), sem("wl_made")
            qkv_psum, qk_padded, v_ready = sem("qkv_psum"), sem("qk_padded"), sem("v_ready")
            q_tap, k_tap, kv_ready = sem("q_tap"), sem("k_tap"), sem("kv_ready")
            kvT_psum, kvh_ready, kvl_ready = sem("kvT_psum"), sem("kvh_ready"), sem("kvl_ready")
            t_loaded = [sem(f"t_loaded{u}") for u in range(2)]
            c_psum, c_ready, cT_psum, gated = sem("c_psum"), sem("c_ready"), sem("cT_psum"), sem("gated")
            cs = lambda cc, n: cst[:, ds(cc, 1), n:n + 1].rearrange("p a n -> p (a n)")

            with nc.Block() as block:

                @block.sync
                def _(sp):

                    def load_w(cc):
                        sp.dma_start(W32[:, :], w["wqkv"][:, ds(cc * (DC * 3 * P), DC * 3 * P)]).then_inc(w_loaded, 16)

                    def load_t(cc, q):
                        for k in range(2):
                            src = bass.AP(tensor=taps.tensor, offset=taps.offset + ((k * DC + cc) * NCT + q) * (LC * CT),
                                          ap=[[CT, P], [1, P * CT]])
                            sp.dma_start(TP[:, q % 2, k, :, :].rearrange("p t c -> p (t c)"), src).then_inc(t_loaded[q % 2], 16)

                    sp.dma_start(cst[:, :, :].rearrange("p a n -> p (a n)"), w["cst"]).then_inc(loaded, 16)
                    load_w(0)
                    load_t(0, 0)
                    load_t(0, 1)

                    def refill(cc):
                        for q in range(NCT - 2):
                            sp.wait_ge(c_psum, NCT * cc + q + 1)
                            load_t(cc, q + 2)

                    with sp.Fori(0, DC - 1) as cc:
                        sp.wait_ge(wl_made, cc + 1)
                        load_w(cc + 1)
                        refill(cc)
                        for q in range(2):
                            sp.wait_ge(c_psum, NCT * cc + NCT - 1 + q)
                            load_t(cc + 1, q)
                    refill(DC - 1)

                @block.tensor
                def _(pe):
                    with pe.Fori(0, DC) as cc:
                        wait_apart(pe, waits_apart, wl_made, cc + 1)
                        wait_apart(pe, waits_apart, wh_made, cc + 1)
                        with pe.Fori(0, NG) as i:
                            n = cc * NG + i
                            for m in range(3):
                                pe.wait_ge(v_ready, n) if m == 2 else pe.wait_ge(qk_padded, 2 * n)
                                k = 0
                                for c in range(DC):
                                    for ww, x in ((Wh, XT[0]), (Wh, XT[1]), (Wl, XT[0])):
                                        t = pe.matmul(bank[m][:, :], ww[:, c, m, :], x[:, c, ds(i * GT, GT)], start=(k == 0),
                                                      stop=(k == 3 * DC - 1))
                                        k += 1
                                t.then_inc(qkv_psum, 1)
                            pe.wait_ge(kv_ready, n + 1)
                            pe.wait_ge(kvl_ready, n)
                            for j in range(GS):
                                t = pe.transpose(bank[3][:, j * P:(j + 1) * P], K[:, j * P:(j + 1) * P], idf[:, :])
                            t.then_inc(kvT_psum, 1)
                        pe.wait_ge(kvl_ready, NG * cc + NG)
                        for q in range(NCT):
                            pe.wait_ge(t_loaded[q % 2], NCT // 2 * 32 * cc + 32 * (q // 2 + 1))
                            pe.wait_ge(c_ready, NCT * cc + max(0, q - 1))
                            for c in range(CT):
                                out = bank[4 + q % 2][:, c * B:(c + 1) * B]
                                ch = q * CT + c
                                pe.matmul(out, TP[:, q % 2, 0, :, c], KVh[:, ch, :], start=True, stop=False)
                                pe.matmul(out, TP[:, q % 2, 1, :, c], KVh[:, ch, :], start=False, stop=False)
                                t = pe.matmul(out, TP[:, q % 2, 0, :, c], KVl[:, ch, :], start=False, stop=True)
                            t.then_inc(c_psum, 1)
                        pe.wait_ge(c_ready, NCT * cc + NCT)
                        for i in range(NG):
                            pe.wait_ge(gated, NG * cc + max(0, i - 1))
                            for j in range(GS):
                                t = pe.transpose(bank[6 + i % 2][:, j * P:(j + 1) * P], C[:, GS * i + j, :], flip[:, :])
                            t.then_inc(cT_psum, 1)

                @block.scalar
                def _(act):
                    act.wait_ge(loaded, 16)
                    act.wait_ge(zeros_set, 1)
                    with act.Fori(0, DC) as cc:
                        act.wait_ge(w_loaded, 16 * cc + 16)
                        act.wait_ge(cT_psum, NG * cc)
                        act.activation(Wh[:, :, :, :].rearrange("p c m n -> p (c m n)"), W32[:, :], ACT.Copy, scale=WS)\
                           .then_inc(wh_made, 1)
                        with act.Fori(0, NG) as i:
                            n = cc * NG + i
                            for m, taken in enumerate((q_tap, k_tap)):
                                act.wait_ge(qkv_psum, 3 * n + m + 1)
                                act.wait_ge(taken, 3 * n)
                                act.activation(pad[:, m, :, 2:P + 2], bank[m][:, :].rearrange("p (j t) -> p j t", j=GS),
                                               ACT.Identity, bias=cs(cc, m), scale=1.0 / WS).then_inc(qk_padded, 1)
                            act.wait_ge(qkv_psum, 3 * n + 3)
                            act.wait_ge(kv_ready, n)
                            act.activation(Vv[:, :], bank[2][:, :], ACT.Identity, bias=cs(cc, 2), scale=1.0 / WS)\
                               .then_inc(v_ready, 1)
                            act.wait_ge(kvT_psum, n + 1)
                            act.activation(KVh[:, :, ds(i * GS, GS)].rearrange("p c j -> p j c"),
                                           bank[3][:, :].rearrange("p (j c) -> p j c", j=GS), ACT.Copy).then_inc(kvh_ready, 1)
                        for q in range(NCT):
                            act.wait_ge(c_psum, NCT * cc + q + 1)
                            act.activation(C[:, :, q * CT:(q + 1) * CT].rearrange("p b c -> p c b"),
                                           bank[4 + q % 2][:, :].rearrange("p (c b) -> p c b", c=CT), ACT.Copy, scale=1.0 / WS)\
                               .then_inc(c_ready, 1)

                @block.vector
                def _(dve):
                    dve.memset(pad[:, :, :, 0:2], 0.0).then_inc(zeros_set, 1)
                    dve.wait_ge(loaded, 16)
                    with dve.Fori(0, DC) as cc:
                        dve.wait_ge(wh_made, cc + 1)
                        dve.scalar_tensor_tensor(Wl[:, :, :, :].rearrange("p c m n -> p (c m n)"), W32[:, :], WS,
                                                 Wh[:, :, :, :].rearrange("p c m n -> p (c m n)"), ALU.mult, ALU.subtract)\
                           .then_inc(wl_made, 1)
                        with dve.Fori(0, NG) as i:
                            n = cc * NG + i
                            yq = Y[:, ds(cc, 1), ds(i * GT, GT)].rearrange("p a (j t) -> p (a j) t", j=GS)
                            for m, (to, taken) in enumerate(((yq, q_tap), (K[:, :].rearrange("p (j t) -> p j t", j=GS), k_tap))):
                                dve.wait_ge(qk_padded, 2 * n + m + 1)
                                if m:
                                    dve.wait_ge(kvT_psum, n)
                                dve.tensor_scalar(to, pad[:, m, :, 2:P + 2], cs(cc, 3 + 4 * m + 2), cs(cc, 3 + 4 * m + 3),
                                                  ALU.mult, ALU.add).then_inc(taken, 1)
                                for s in (1, 0):
                                    dve.wait_ge(taken, 3 * n + 2 - s)
                                    dve.scalar_tensor_tensor(to, pad[:, m, :, s:P + s], cs(cc, 3 + 4 * m + s), to,
                                                             ALU.mult, ALU.add).then_inc(taken, 1)
                            dve.wait_ge(k_tap, 3 * n + 3)
                            dve.wait_ge(v_ready, n + 1)
                            dve.tensor_tensor(K[:, :], K[:, :], Vv[:, :], ALU.mult).then_inc(kv_ready, 1)
                            dve.wait_ge(kvT_psum, n + 1)
                            dve.wait_ge(kvh_ready, n + 1)
                            b4 = ds(i * GS, GS)
                            dve.tensor_tensor(KVl[:, :, b4].rearrange("p c j -> p j c"),
                                              bank[3][:, :].rearrange("p (j c) -> p j c", j=GS),
                                              KVh[:, :, b4].rearrange("p c j -> p j c"), ALU.subtract).then_inc(kvl_ready, 1)
                        for i in range(NG):
                            dve.wait_ge(cT_psum, NG * cc + i + 1)
                            y = Y[:, ds(cc, 1), i * GT:(i + 1) * GT].rearrange("p a t -> p (a t)")
                            dve.tensor_tensor(y, bank[6 + i % 2][:, :], y, ALU.mult).then_inc(gated, 1)

        with ExitStack() as ctx2:
            sb2 = lambda n, s, d=F32: ctx2.enter_context(nc.sbuf_tensor(f"hy_{n}", s, d))
            Woh, Wol = sb2("Woh", [P, DC * D], F16), sb2("Wol", [P, DC * D], F16)
            load_split(nc, "hyo", [(w["WoT_hy"], Woh, Wol)])
            bo = sb2("bo", [P, D])
            Yh, Yl = sb2("Yh", [P, 2, DC, GT], F16), sb2("Yl", [P, 2, DC, GT], F16)
            norm = Norm(nc, ctx2, "hy_norm")
            x_loaded = [sem(f"x_loaded{k}") for k in range(NG)]
            bo_loaded, biased = sem("bo_loaded"), sem("biased")
            yh_ready, yl_ready, o_psum = sem("yh_ready"), sem("yl_ready"), sem("o_psum")

            with nc.Block() as block:

                @block.sync
                def _(sp):
                    sp.dma_start(bo[:, :], w["bo"].partition_broadcast(P)).then_inc(bo_loaded, 16)
                    for k in range(NG):
                        sp.dma_start(X[:, GS * k:GS * k + GS, :].rearrange("p b n -> p (b n)"),
                                     w["x"][:, GS * k * D:(GS * k + GS) * D]).then_inc(x_loaded[k], 16)

                @block.gpsimd
                def _(pool):
                    norm_consts(pool, norm)
                    pool.wait_ge(bo_loaded, 16)
                    for i in range(NG):
                        pool.wait_ge(x_loaded[i], 16)
                        for j in range(GS):
                            x = X[:, GS * i + j, :]
                            pool.tensor_tensor(x, x, bo[:, :], ALU.add).then_inc(biased, 1)
                        norm_rstd(pool, norm, i)

                @block.scalar
                def _(act):
                    for i in range(NG):
                        if i >= 2:
                            act.wait_ge(o_psum, GS * (i - 1))
                        act.activation(Yh[:, i % 2, :, :], Y[:, :, i * GT:(i + 1) * GT], ACT.Copy).then_inc(yh_ready, 1)

                @block.tensor
                def _(pe):
                    for i in range(NG):
                        pe.wait_ge(yh_ready, i + 1)
                        pe.wait_ge(yl_ready, i + 1)
                        for j in range(GS):
                            if i:
                                pe.wait_ge(norm.rows_ready, GS * (i - 1) + j + 1)
                            k = 0
                            for c in range(DC):
                                for y, ww in ((Yh, Woh), (Yl, Woh), (Yh, Wol)):
                                    t = pe.matmul(bank[j][:, :], y[:, i % 2, c, j * P:(j + 1) * P], ww[:, c * D:(c + 1) * D],
                                                  start=(k == 0), stop=(k == 3 * DC - 1))
                                    k += 1
                            t.then_inc(o_psum, 1)

                @block.vector
                def _(dve):

                    def split(i):
                        dve.wait_ge(yh_ready, i + 1)
                        if i >= 2:
                            dve.wait_ge(o_psum, GS * (i - 1))
                        dve.tensor_tensor(Yl[:, i % 2, :, :], Y[:, :, i * GT:(i + 1) * GT], Yh[:, i % 2, :, :], ALU.subtract)\
                           .then_inc(yl_ready, 1)

                    split(0)
                    for i in range(NG):
                        if i + 1 < NG:
                            split(i + 1)
                        for j in range(GS):
                            dve.wait_ge(o_psum, GS * i + j + 1)
                            dve.wait_ge(biased, GS * i + j + 1)
                            x = X[:, GS * i + j, :]
                            dve.scalar_tensor_tensor(x, bank[j][:, :], 1.0 / WS, x, ALU.mult, ALU.add).then_inc(norm.rows_ready, 1)
                        for j in range(GS):
                            norm_stats(dve, norm, X, i, j)
                        for j in range(GS):
                            norm_aggr(dve, norm, i, j)
                        for j in range(GS):
                            norm_apply(dve, norm, X, i, j)


def load_consts(nc, ctx, name, arrays, wanted):
    tiles = {n: ctx.enter_context(nc.sbuf_tensor(f"{name}_{n}", list(arrays[n].shape), arrays[n].dtype)) for n in wanted}
    loaded = nc.alloc_semaphore(f"{name}_tiles_loaded")
    with nc.Block() as block:

        @block.sync
        def _(sp):
            for n in wanted:
                sp.dma_start(tiles[n][:, :], arrays[n]).then_inc(loaded, 16)
            sp.wait_ge(loaded, 16 * len(wanted))

    return tiles


def decoder(nc, a, out):
    with ExitStack() as ctx:
        X = ctx.enter_context(nc.sbuf_tensor("X", [P, B, D], F32))
        taps = nc.dram_tensor("taps", [2, D // CT, LC, CT], F16, kind="Internal").ap()
        kv = nc.dram_tensor("kv", [P, B, KVW], F16, kind="Internal").ap()

        with nc.cleanup_on_exit(), ExitStack() as stage:
            hyena_taps(nc, a["kerT"], a["dskip"], taps)
            c = load_consts(nc, stage, "hy", a, ("idf", "flip"))
            hyena(nc, X, a, taps, c["idf"], c["flip"])
        with nc.cleanup_on_exit(), ExitStack() as stage:
            c = load_consts(nc, stage, "xa", a, ("idh", "nsel", "gmask"))
            context(nc, a["ctx"], kv, c["idh"])
            cross_attention(nc, "xa", X, kv, c["idh"], c["nsel"], c["gmask"][:, :].rearrange("p (g t) -> p g t", g=QG))
        with nc.cleanup_on_exit(), ExitStack() as stage:
            c = load_consts(nc, stage, "ffn", a, ("idh",))
            ffn(nc, X, a["w0T"], a["w1T"], a["bias0"], a["bias1"], c["idh"])
        with nc.cleanup_on_exit(), ExitStack() as stage:
            c = load_consts(nc, stage, "la", a, ("idf",))
            latent_attention(nc, X, a, c["idf"])
        with nc.cleanup_on_exit(), ExitStack() as stage:
            c = load_consts(nc, stage, "xb", a, ("idh", "nsel", "gmask"))
            cross_attention(nc, "xb", X, kv, c["idh"], c["nsel"], c["gmask"][:, :].rearrange("p (g t) -> p g t", g=QG))
        with nc.cleanup_on_exit(), ExitStack() as stage:
            c = load_consts(nc, stage, "moe", a, ("idh", "idf", "tri", "mc"))
            moe(nc, X, a["mw12"], a["mw3"], a["rw"], c["idh"], c["idf"], c["tri"], c["mc"], out)



def _layout(np, i):
    c = np.ascontiguousarray

    def rows(w):
        n = w.shape[0] // P
        return c(w.reshape(n, P, -1).transpose(1, 0, 2).reshape(P, -1))

    def by_channel(v):
        return v.reshape(DC, P).T

    a = {}
    x = i["x"]
    a["x"] = c(x.transpose(1, 0, 2).reshape(P, -1))
    a["xT"] = rows(c(x.transpose(2, 0, 1)).reshape(D, -1))
    a["ctx"] = c(i["ctx_512"].transpose(1, 0, 2).reshape(P, -1))
    w = np.stack([i["L0_attn_Wq"].T, i["L0_attn_Wk"].T, i["L0_attn_Wv"].T], 1)
    a["wqkv"] = c(w.reshape(DC, P, 3, DC, P).transpose(1, 3, 0, 2, 4).reshape(P, -1))
    qw, kw = i["L0_attn_convq_w"], i["L0_attn_convk_w"]
    per_channel = [i["L0_attn_bq"], i["L0_attn_bk"], i["L0_attn_bv"], qw[:, 0, 0], qw[:, 0, 1], qw[:, 0, 2],
                   i["L0_attn_convq_b"], kw[:, 0, 0], kw[:, 0, 1], kw[:, 0, 2], i["L0_attn_convk_b"]]
    a["cst"] = c(np.stack([by_channel(v) for v in per_channel], 2).reshape(P, -1))
    ker = i["L0_attn_ssm_kernel"]
    a["kerT"] = rows(np.concatenate([ker[:, :P][:, ::-1], ker[:, P:LC][:, ::-1]], 1).T)
    a["dskip"] = np.zeros((P, D), x.dtype)
    a["dskip"][P - 1] = i["L0_attn_D_skip"]
    a["WoT_hy"] = rows(i["L0_attn_Wo"].T)
    a["bo"] = i["L0_attn_bo"]
    a["w0T"] = rows(i["L0_ffn_W0"].T)
    a["w1T"] = rows(i["L0_ffn_W1"].T)
    a["bias0"] = c(i["L0_ffn_bias0"].reshape(FC, P).T)
    a["bias1"] = i["L0_ffn_bias1"]
    q, kv = i["L1_attn_W_q_comp"], i["L1_attn_W_kv_comp"]

    def halves_swapped(m):
        return np.concatenate([m[DCMP // 2:], m[:DCMP // 2]], 0)

    k = kv[:DCMP]
    a["WkvT"] = rows(i["L1_attn_W_to_kv"].T)
    a["Wkv"] = i["L1_attn_W_to_kv"]
    a["WoT"] = c(i["L1_attn_W_out_res"].T)
    a["WcT"] = c(i["L1_attn_W_compress"].T)
    a["Wqk"] = c(np.stack([q.T, halves_swapped(q).T, k.T, halves_swapped(k).T], 1).reshape(DCMP, -1))
    a["WvT"] = c(kv[DCMP:].T)
    a["WlT"] = c(i["L1_attn_W_comp2lat"].T)
    a["gb"] = c(np.stack([i["L1_attn_ln_gamma"], i["L1_attn_ln_beta"]], 1))
    a["bout"] = i["L1_attn_b_out_res"]
    up = np.stack([i["L1_ffn_w1"], i["L1_ffn_w2"]], 2)
    a["mw12"] = c(up.reshape(NE, DC, P, 2 * FE).transpose(2, 0, 1, 3).reshape(P, -1))
    a["mw3"] = c(i["L1_ffn_w3"].reshape(NE, FE // P, P, D).transpose(2, 0, 1, 3).reshape(P, -1))
    a["rw"] = rows(i["L1_ffn_router_w"].T)
    f32, f16 = np.float32, np.float16
    a["idf"], a["idh"], a["flip"] = np.eye(P, dtype=f32), np.eye(P, dtype=f16), c(np.eye(P, dtype=f32)[:, ::-1])
    inv = (1.0 / (10000.0 ** (np.arange(0, DCMP, 2, dtype=f32) / DCMP))).astype(f32)
    angle = np.arange(P, dtype=f32)[:, None] * inv[None, :]
    cos = np.concatenate([np.cos(angle), np.cos(angle)], 1).T
    sin = np.concatenate([-np.sin(angle), np.sin(angle)], 1).T
    a["rope"] = c(np.stack([np.tile(cos, (1, GS)), np.tile(sin, (1, GS))], 1).astype(f32).reshape(DCMP, -1))
    a["mask"] = np.where(np.tril(np.ones((P, P), bool)), 0, -1e30).astype(f32)
    nsel, gmask = np.zeros((QH, KH, P), f16), np.zeros((QH, QG, P), f16)
    for h in range(QH):
        nsel[h, h // QG] = -1
        gmask[h, ORDER.index(h % QG)] = 1
    a["nsel"], a["gmask"] = nsel.reshape(QH, -1), gmask.reshape(QH, -1)
    t = np.arange(P)
    a["tri"] = np.concatenate([t[:, None] < t[None, :], np.ones((P, P), bool)], 1).astype(f16)
    e = np.arange(NE)
    row = np.concatenate([e, e * EROWS, np.arange(B) * P, (e[None, :] <= e[:, None]).reshape(-1), np.arange(NTILE)])
    a["mc"] = np.concatenate([np.tile(row, (P, 1)), t[:, None]], 1).astype(f32)
    return a


def kernel(**inputs):
    import numpy as np
    import concourse.bacc as bacc
    from concourse.bass_utils import run_bass_kernel_spmd

    nc = bacc.Bacc("TRN2", target_bir_lowering=False, num_devices=1)
    arrays = _layout(np, {n: np.asarray(v) for n, v in inputs.items()})
    aps = {n: nc.dram_tensor(f"in_{n}", v.shape, mybir.dt.from_np(v.dtype), kind="ExternalInput").ap()
           for n, v in arrays.items()}
    out = nc.dram_tensor("out_0", (P, B * D), F32, kind="ExternalOutput").ap()
    decoder(nc, aps, out)
    r = run_bass_kernel_spmd(nc, [{f"in_{n}": v for n, v in arrays.items()}], core_ids=[0])
    y = r.results[0]["out_0"]
    return np.ascontiguousarray(y.reshape(P, B, D).transpose(1, 0, 2))
```

```python
from contextlib import ExitStack

import concourse.bass as bass
from concourse import mybir

F32 = mybir.dt.float32
F16 = mybir.dt.float16
U32 = mybir.dt.uint32
ALU = mybir.AluOpType
ACT = mybir.ActivationFunctionType
AX = mybir.AxisListType

P = 128
B = 32
D = 512
DC = D // P
GS = 4
GT = GS * P
NG = B // GS
FF = 2048
FC = FF // P
NE = 8
FE = 256
WS = 256.0
EPS = 1e-5
ds = bass.ds


def tile(X, i):
    return X[:, ds(i, 1), :].rearrange("p a n -> p (a n)")


def group(X, i, n=GS):
    return X[:, ds(i, n), :]


def load_split(nc, name, parts, scale=WS):
    W = 2048
    pieces = []
    for dram, hi, lo in parts:
        n = dram.shape[1]
        for a in range(0, n, W):
            b = min(n, a + W)
            pieces.append((dram[:, a:b], hi[:, a:b], lo[:, a:b], b - a))
    with ExitStack() as ctx:
        stage = ctx.enter_context(nc.sbuf_tensor(f"{name}_stage", [P, 2, W], F32))
        loaded = [nc.alloc_semaphore(f"{name}_loaded{k}") for k in range(2)]
        hi_made = nc.alloc_semaphore(f"{name}_hi_made")
        lo_made = nc.alloc_semaphore(f"{name}_lo_made")
        with nc.Block() as block:

            @block.sync
            def _(sp):
                for k, (src, _, _, n) in enumerate(pieces):
                    if k >= 2:
                        sp.wait_ge(lo_made, k - 1)
                    sp.dma_start(stage[:, k % 2, 0:n], src).then_inc(loaded[k % 2], 16)

            @block.scalar
            def _(act):
                for k, (_, hi, _, n) in enumerate(pieces):
                    act.wait_ge(loaded[k % 2], 16 * (k // 2 + 1))
                    act.activation(hi, stage[:, k % 2, 0:n], ACT.Copy, scale=scale).then_inc(hi_made, 1)

            @block.vector
            def _(dve):
                for k, (_, hi, lo, n) in enumerate(pieces):
                    dve.wait_ge(hi_made, k + 1)
                    dve.wait_ge(loaded[k % 2], 16 * (k // 2 + 1))
                    dve.scalar_tensor_tensor(lo, stage[:, k % 2, 0:n], scale, hi, ALU.mult, ALU.subtract).then_inc(lo_made, 1)


class Norm:

    def __init__(self, nc, ctx, name, n=GS):
        self.n = n
        self.stats = ctx.enter_context(nc.sbuf_tensor(f"{name}_stats", [P, n, 6], F32))
        self.mv = ctx.enter_context(nc.sbuf_tensor(f"{name}_mv", [P, n, 2], F32))
        self.rstd = ctx.enter_context(nc.sbuf_tensor(f"{name}_rstd", [P, n], F32))
        self.consts = ctx.enter_context(nc.sbuf_tensor(f"{name}_consts", [P, 2 * n], F32))
        s = lambda n: nc.alloc_semaphore(f"{name}_{n}")
        self.rows_ready = s("rows_ready")
        self.stats_ready = s("stats_ready")
        self.mv_ready = s("mv_ready")
        self.var_eps = s("var_eps")
        self.rstd_ready = s("rstd_ready")
        self.normed = s("normed")
        self.consts_set = s("consts_set")
        self.waits_apart = s("waits_apart")


def norm_consts(pool, n):
    pool.memset(n.consts[:, 0:n.n], EPS).then_inc(n.consts_set, 1)
    pool.memset(n.consts[:, n.n:2 * n.n], -0.5).then_inc(n.consts_set, 1)


def norm_rstd(pool, n, i):
    pool.wait_ge(n.consts_set, 2)
    pool.wait_ge(n.mv_ready, n.n * i + n.n)
    pool.tensor_tensor(n.rstd[:, :], n.mv[:, :, 1], n.consts[:, 0:n.n], ALU.add).then_inc(n.var_eps, 1)
    pool.wait_ge(n.var_eps, i + 1)
    pool.tensor_tensor(n.rstd[:, :], n.rstd[:, :], n.consts[:, n.n:2 * n.n], ALU.pow).then_inc(n.rstd_ready, 1)


def wait_apart(eng, apart, sem, value):
    eng.wait_ge(sem, value)
    eng.sem_inc(apart, 1)


def norm_stats(dve, n, X, i, j, at=None):
    wait_apart(dve, n.waits_apart, n.rows_ready, n.n * i + j + 1)
    dve.bn_stats(n.stats[:, j, :], tile(X, n.n * i + j if at is None else at)).then_inc(n.stats_ready, 1)


def norm_aggr(dve, n, i, j):
    wait_apart(dve, n.waits_apart, n.stats_ready, n.n * i + j + 1)
    dve.bn_aggr(n.mv[:, j, :], n.stats[:, j, :]).then_inc(n.mv_ready, 1)


def norm_apply(dve, n, X, i, j, at=None):
    dve.wait_ge(n.rstd_ready, i + 1)
    x = tile(X, n.n * i + j if at is None else at)
    dve.tensor_scalar(x, x, n.mv[:, j, 0:1], n.rstd[:, j:j + 1], ALU.subtract, ALU.mult).then_inc(n.normed, 1)


def ffn(nc, X, raw, bias0, bias1, idh):
    with ExitStack() as ctx:
        sb = lambda n, s, d=F32: ctx.enter_context(nc.sbuf_tensor(f"ffn_{n}", s, d))
        ps = lambda n, s, d=F32: ctx.enter_context(nc.psum_tensor(f"ffn_{n}", s, d))
        sem = lambda n: nc.alloc_semaphore(f"ffn_{n}")
        W0h, W0l = sb("W0h", [P, DC, FF], F16), sb("W0l", [P, DC, FF], F16)
        W1h, W1l = sb("W1h", [P, FC, D], F16), sb("W1l", [P, FC, D], F16)
        flat = lambda t: t[:, :, :].rearrange("p a n -> p (a n)")
        X16 = sb("X16", [P, GS, D], F16)
        XT = sb("XT", [P, DC, GT], F16)
        DT = raw[:, 0, :].bitcast(F16)[:, 0:FC * GT].rearrange("p (n t) -> p n t", n=FC)
        E16 = raw[:, 1, :].bitcast(F16)[:, 0:GS * D].rearrange("p (j n) -> p j n", j=GS)
        b0 = sb("b0", [P, FC])
        b1 = sb("b1", [P, D])
        psT = [ps(f"psT{k}", [P, GT], F16) for k in range(2)]
        psD = [ps(f"psD{k}", [P, GT]) for k in range(2)]
        psE = [ps(f"psE{k}", [P, D]) for k in range(GS)]
        norm = Norm(nc, ctx, "ffn_norm")
        consts_loaded, wh_made, wl_made = sem("consts_loaded"), sem("wh_made"), sem("wl_made")
        HALF = FF * DC // 2
        pieces = [(raw[:, k, a:a + HALF], flat(h)[:, a:a + HALF], flat(l)[:, a:a + HALF])
                  for k, (h, l) in enumerate(((W0h, W0l), (W1h, W1l))) for a in (0, HALF)]
        x16_ready, xT_psum, xT_ready = sem("x16_ready"), sem("xT_psum"), sem("xT_ready")
        d_psum, dT_ready, e_psum, e16_ready = sem("d_psum"), sem("dT_ready"), sem("e_psum"), sem("e16_ready")

        with nc.Block() as block:

            @block.sync
            def _(sp):
                sp.dma_start(b0[:, :], bias0).then_inc(consts_loaded, 16)
                sp.dma_start(b1[:, :], bias1.partition_broadcast(P)).then_inc(consts_loaded, 16)

            @block.gpsimd
            def _(pool):
                norm_consts(pool, norm)

                def cast(i):
                    pool.wait_ge(xT_psum, DC * i)
                    for j in range(GS):
                        pool.tensor_copy(X16[:, j, :], tile(X, GS * i + j)).then_inc(x16_ready, 1)

                cast(0)
                with pool.Fori(0, NG - 1) as i:
                    cast(i + 1)
                    norm_rstd(pool, norm, i)
                norm_rstd(pool, norm, NG - 1)

            @block.tensor
            def _(pe):

                def turn_x(i):
                    pe.wait_ge(x16_ready, GS * i + GS)
                    for c in range(DC):
                        pe.wait_ge(xT_ready, DC * i + max(0, c - 1))
                        for j in range(GS):
                            t = pe.transpose(psT[c % 2][:, j * P:(j + 1) * P], X16[:, j, c * P:(c + 1) * P], idh[:, :])
                        t.then_inc(xT_psum, 1)

                def up(i):
                    pe.wait_ge(xT_ready, DC * i + DC)
                    for n in range(FC):
                        pe.wait_ge(dT_ready, FC * i + max(0, n - 1))
                        for c in range(DC):
                            for w in (W0h, W0l):
                                t = pe.matmul(psD[n % 2][:, :], w[:, c, n * P:(n + 1) * P], XT[:, c, :],
                                              start=(c == 0 and w is W0h), stop=(c == DC - 1 and w is W0l))
                        t.then_inc(d_psum, 1)

                def down(i):
                    pe.wait_ge(dT_ready, FC * i + FC)
                    pe.wait_ge(e16_ready, GS * i)
                    for j in range(GS):
                        for n in range(FC):
                            for w in (W1h, W1l):
                                t = pe.matmul(psE[j][:, :], DT[:, n, j * P:(j + 1) * P], w[:, n, :],
                                              start=(n == 0 and w is W1h), stop=(n == FC - 1 and w is W1l))
                        t.then_inc(e_psum, 1)

                turn_x(0)
                pe.wait_ge(wh_made, 4)
                pe.wait_ge(wl_made, 4)
                with pe.Fori(0, NG - 1) as i:
                    up(i)
                    turn_x(i + 1)
                    down(i)
                up(NG - 1)
                down(NG - 1)

            @block.scalar
            def _(act):
                act.wait_ge(consts_loaded, 32)
                for w, h, _ in pieces:
                    act.activation(h, w, ACT.Copy, scale=WS).then_inc(wh_made, 1)
                act.wait_ge(wl_made, 4)
                with act.Fori(0, NG) as i:
                    act.wait_ge(e_psum, GS * i)
                    for n in range(FC):
                        act.wait_ge(d_psum, FC * i + n + 1)
                        act.activation(DT[:, n, :], psD[n % 2][:, :], ACT.Gelu, bias=b0[:, n:n + 1],
                                       scale=1.0 / WS).then_inc(dT_ready, 1)

            @block.vector
            def _(dve):

                def x_out(i):
                    for c in range(DC):
                        dve.wait_ge(xT_psum, DC * i + c + 1)
                        if c == 0:
                            dve.wait_ge(d_psum, FC * i)
                        dve.tensor_copy(XT[:, c, :], psT[c % 2][:, :]).then_inc(xT_ready, 1)

                def add(i):
                    for j in range(GS):
                        dve.wait_ge(e_psum, GS * i + j + 1)
                        dve.scalar_tensor_tensor(E16[:, j, :], psE[j][:, :], 1.0 / WS, b1[:, :], ALU.mult, ALU.add)\
                           .then_inc(e16_ready, 1)
                        dve.wait_ge(e16_ready, GS * i + j + 1)
                        x = tile(X, GS * i + j)
                        dve.tensor_tensor(x, x, E16[:, j, :], ALU.add).then_inc(norm.rows_ready, 1)
                        norm_stats(dve, norm, X, i, j)
                        norm_aggr(dve, norm, i, j)
                    for j in range(GS):
                        norm_apply(dve, norm, X, i, j)

                dve.wait_ge(consts_loaded, 32)
                x_out(0)
                for n, (w, h, l) in enumerate(pieces):
                    dve.wait_ge(wh_made, n + 1)
                    dve.scalar_tensor_tensor(l, w, WS, h, ALU.mult, ALU.subtract).then_inc(wl_made, 1)
                dve.wait_ge(wl_made, 4)
                with dve.Fori(0, NG - 1) as i:
                    x_out(i + 1)
                    add(i)
                add(NG - 1)


NR = 2
TT = 4
EROWS = B * P + P
NTILE = B * NR + NE
ETILE = EROWS // P
ZTILE = 3 * P
W12E = DC * 2 * FE
W3E = FE // P * D
MC_IOTA = 0
MC_ZONE = MC_IOTA + NE
MC_FULL = MC_ZONE + NE
MC_UPTO = MC_FULL + B
MC_TILE = MC_UPTO + NE * NE
MC_P = MC_TILE + NTILE
MC_W = MC_P + 1


def moe(nc, X, W12h, W12l, w3, rw, idh, idf, tri, mc, out):
    xs = nc.dram_tensor("moe_xs", [B * P, 2 * D], F16, kind="Internal").ap()
    inv = nc.dram_tensor("moe_inv", [ZTILE * P, 1], F32, kind="Internal").ap()
    ys = nc.dram_tensor("moe_ys", [NTILE * P, D], F32, kind="Internal").ap()
    with ExitStack() as ctx:
        sb = lambda n, s, d=F32: ctx.enter_context(nc.sbuf_tensor(f"moe_{n}", s, d))
        rows_of = sb("rows_of", [P, B * NR], U32)
        gap = sb("gap", [P, B])
        tokens = sb("tokens", [P, ZTILE], U32)
        zone_tile = sb("zone_tile", [P, NTILE], U32)
        expert_at = sb("expert_at", [P, NTILE], U32)
        with ExitStack() as weights:
            wsb = lambda n, s, d=F16: weights.enter_context(nc.sbuf_tensor(f"moe_{n}", s, d))
            W3h, W3l = wsb("W3h", [P, NE * W3E]), wsb("W3l", [P, NE * W3E])
            RWh, RWl = wsb("RWh", [P, DC * NE]), wsb("RWl", [P, DC * NE])
            load_split(nc, "moew", [(rw, RWh, RWl)])
            moe_route(nc, X, RWh, RWl, idh, idf, tri, mc, xs, inv, rows_of, gap, tokens, zone_tile, expert_at, (w3, W3h, W3l))
            moe_experts(nc, W12h, W12l, W3h, W3l, idh, xs, ys, tokens, zone_tile, expert_at)
        moe_combine(nc, X, ys, rows_of, gap, out)


def moe_route(nc, X, RWh, RWl, idh, idf, tri, mc, xs, inv, rows_of, gap, tokens, zone_tile, expert_at, down):
    with ExitStack() as ctx:
        sb = lambda n, s, d=F32: ctx.enter_context(nc.sbuf_tensor(f"route_{n}", s, d))
        ps = lambda n, s, d=F32: ctx.enter_context(nc.psum_tensor(f"route_{n}", s, d))
        sem = lambda n: nc.alloc_semaphore(f"route_{n}")
        R = sb("R", [P, 2, TT, 2 * D], F16)
        XT = sb("XT", [P, TT, 2 * D], F16)
        zero = sb("zero", [P, ZTILE])
        I = sb("I", [P, B, NR])
        row_all = sb("row_all", [P, B * NR])
        token = sb("token", [P, 2, TT])
        lst = sb("list", [P, 3, P])
        L = sb("L", [P, TT, NE])
        V8 = sb("V8", [P, TT, 8])
        I8 = sb("I8", [P, TT, 8], U32)
        pick = sb("pick", [P, TT, NR, NE])
        both = sb("both", [P, TT, NE], F16)
        next_row = sb("next_row", [P, NE])
        row = sb("row", [P, TT, NE])
        prow = sb("prow", [P, TT, NR, NE])
        rowf = sb("rowf", [P, TT * NR])
        J = sb("J", [P, 2, TT * NR], U32)
        n_of = sb("n_of", [P, NE])
        room = XT[:, :, :].rearrange("p j n -> p (j n)").bitcast(F32)
        full = room[:, 0:NE * B].rearrange("p (e k) -> p e k", e=NE)
        tiles = sb("tiles", [P, NE])
        upto = sb("upto", [P, NE, NE])
        end = sb("end", [P, NE])
        past = room[:, 0:NTILE * NE].rearrange("p (t e) -> p t e", e=NE)
        shift = sb("shift", [P, NE])
        rowf64 = sb("rowf64", [P, B * NR])
        pshift = room[:, 0:B * NR * NE].rearrange("p (t e) -> p t e", e=NE)
        et, before, base = sb("et", [P, NTILE]), sb("before", [P, NTILE]), sb("base", [P, NTILE])
        down_dram, down_hi, down_lo = down
        DW = NE * W3E // (B // TT)
        Dn = sb("Dn", [P, 2, DW])
        d_loaded, dh_made, dl_made = [sem(f"d_loaded{h}") for h in range(2)], sem("dh_made"), sem("dl_made")
        T = [ps(f"T{k}", [P, D]) for k in range(4)]
        T16 = [t[:, :].bitcast(F16) for t in T]
        M = [ps(f"M{k}", [P, TT * NE]) for k in range(2)]
        C = [ps(f"C{k}", [P, (TT + 1) * NE]) for k in range(2)]
        hi_ready, lo_ready, xT_psum, xT_ready = sem("hi_ready"), sem("lo_ready"), sem("xT_psum"), sem("xT_ready")
        logits_psum, logits_ready, best_ready = sem("logits_psum"), sem("logits_ready"), sem("best_ready")
        gap_ready, index_ready, indexf_ready = sem("gap_ready"), sem("index_ready"), sem("indexf_ready")
        pick_ready, both_ready, counts_psum, row_ready = (sem("pick_ready"), sem("both_ready"), sem("counts_psum"),
                                                          sem("row_ready"))
        next_ready, prow_ready, rowf_ready, rows_ready = (sem("next_ready"), sem("prow_ready"), sem("rowf_ready"),
                                                          sem("rows_ready"))
        zero_set, zone_zeroed, apart = sem("zero_set"), sem("zone_zeroed"), sem("apart")
        table = sem("table")
        token_ready, list_loaded, list_psum = sem("token_ready"), sem("list_loaded"), sem("list_psum")
        scattered, xs_stored = [sem(f"scattered{k}") for k in range(2)], [sem(f"xs_stored{k}") for k in range(2)]
        NI = B // (2 * TT)
        cols = lambda k, n: mc[:, k:k + n]

        with nc.Block() as block:

            @block.gpsimd
            def _(pool):
                pool.wait_ge(zone_zeroed, 16)
                with pool.Fori(0, NI) as i:
                    for h in range(2):
                        wait_apart(pool, apart, token_ready, 2 * i + h + 1)
                        wait_apart(pool, apart, rows_ready, 2 * i + h + 1)
                        for j in range(TT):
                            for r in range(NR):
                                pool.indirect_dma_start(inv, bass.IndirectOffsetOnAxis(ap=J[:, h, NR * j + r:NR * j + r + 1], axis=0),
                                                        token[:, h, j:j + 1], None).then_inc(scattered[h], 16)

            @block.sync
            def _(sp):
                sp.wait_ge(zero_set, 1)
                sp.dma_start(inv.rearrange("(p n) o -> p (n o)", p=P), zero[:, :]).then_inc(zone_zeroed, 16)

                def load_down(g, h):
                    sp.dma_start(Dn[:, h, :], down_dram[:, ds(g * DW, DW)]).then_inc(d_loaded[h], 16)

                def store_x(i, h):
                    sp.wait_ge(hi_ready, TT * (2 * i + h) + TT)
                    sp.wait_ge(lo_ready, TT * (2 * i + h) + TT)
                    sp.dma_start(xs[ds((8 * i + 4 * h) * P, TT * P), :].rearrange("(j p) n -> p j n", p=P), R[:, h, :, :])\
                      .then_inc(xs_stored[h], 16)

                for h in range(2):
                    load_down(h, h)
                with sp.Fori(0, NI - 1) as i:
                    for h in range(2):
                        store_x(i, h)
                        sp.wait_ge(dl_made, 2 * i + h + 1)
                        load_down(2 * i + (h + 2), h)
                for h in range(2):
                    store_x(NI - 1, h)
                for h in range(2):
                    sp.wait_ge(xs_stored[h], 16 * NI)

            @block.scalar
            def _(act):
                with act.Fori(0, NI) as i:
                    for h in range(2):
                        act.wait_ge(xs_stored[h], 16 * i)
                        act.wait_ge(xT_psum, TT * (2 * i + h))
                        for j in range(TT):
                            act.activation(R[:, h, j, 0:D], tile(X, 8 * i + TT * h + j), ACT.Copy).then_inc(hi_ready, 1)
                        act.wait_ge(logits_psum, 2 * i + h)
                        for j in range(TT):
                            act.wait_ge(xT_psum, TT * (2 * i + h) + j + 1)
                            act.activation(XT[:, j, :], T16[j], ACT.Copy).then_inc(xT_ready, 1)
                        act.wait_ge(d_loaded[h], 16 * i + 16)
                        act.activation(down_hi[:, ds((2 * i + h) * DW, DW)], Dn[:, h, :], ACT.Copy, scale=WS).then_inc(dh_made, 1)

            @block.tensor
            def _(pe):

                def turn(g, h):
                    for j in range(TT):
                        pe.wait_ge(hi_ready, TT * g + j + 1)
                        pe.wait_ge(xT_ready, TT * g)
                        for c in range(DC):
                            pe.transpose(T16[j][:, c * P:(c + 1) * P], R[:, h, j, c * P:(c + 1) * P], idh[:, :])
                        pe.wait_ge(lo_ready, TT * g + j + 1)
                        for c in range(DC, 2 * DC):
                            t = pe.transpose(T16[j][:, c * P:(c + 1) * P], R[:, h, j, c * P:(c + 1) * P], idh[:, :])
                        t.then_inc(xT_psum, 1)

                def logits(g, h):
                    pe.wait_ge(logits_ready, g)
                    for j in range(TT):
                        pe.wait_ge(xT_ready, TT * g + j + 1)
                        for c in range(DC):
                            for k, (x, w) in enumerate(((c, RWh), (DC + c, RWh), (c, RWl))):
                                t = pe.matmul(M[h][:, j * NE:(j + 1) * NE], XT[:, j, x * P:(x + 1) * P],
                                              w[:, c * NE:(c + 1) * NE],
                                              start=(c == 0 and k == 0), stop=(c == DC - 1 and k == 2))
                    t.then_inc(logits_psum, 1)

                def counts(g, h):
                    pe.wait_ge(both_ready, g + 1)
                    pe.wait_ge(next_ready, g)
                    for j in range(TT + 1):
                        for b in range(min(j + 1, TT)):
                            last = b == min(j, TT - 1)
                            lhs = tri[:, 0:P] if b == j else tri[:, P:2 * P]
                            t = pe.matmul(C[h][:, j * NE:(j + 1) * NE], lhs, both[:, b, :], start=(b == 0), stop=last)
                    t.then_inc(counts_psum, 1)

                turn(0, 0)
                logits(0, 0)
                with pe.Fori(0, NI - 1) as i:
                    for h in range(2):
                        turn(2 * i + h + 1, 1 - h)
                        counts(2 * i + h, h)
                        logits(2 * i + h + 1, 1 - h)
                turn(2 * NI - 1, 1)
                counts(2 * NI - 2, 0)
                logits(2 * NI - 1, 1)
                counts(2 * NI - 1, 1)

            @block.vector
            def _(dve):
                dve.memset(zero[:, :], 0.0).then_inc(zero_set, 1)
                dve.tensor_copy(next_row[:, :], cols(MC_ZONE, NE)).then_inc(zero_set, 1)
                dve.wait_ge(zero_set, 2)

                def lo(g, h):
                    for j in range(TT):
                        dve.wait_ge(hi_ready, TT * g + j + 1)
                        dve.tensor_tensor(R[:, h, j, D:2 * D], tile(X, TT * g + j), R[:, h, j, 0:D], ALU.subtract)\
                           .then_inc(lo_ready, 1)

                def route(i, h):
                    g = 2 * i + h
                    dve.wait_ge(logits_psum, g + 1)
                    dve.tensor_scalar(L[:, :, :].rearrange("p j e -> p (j e)"), M[h][:, :], 1.0 / WS, None, ALU.mult)\
                       .then_inc(logits_ready, 1)
                    for j in range(TT):
                        wait_apart(dve, apart, logits_ready, g + 1)
                        dve.max(V8[:, j, :], L[:, j, :]).then_inc(best_ready, 1)
                    dve.wait_ge(best_ready, TT * g + TT)
                    dve.tensor_tensor(gap[:, ds(TT * g, TT)], V8[:, :, 0], V8[:, :, 1], ALU.subtract).then_inc(gap_ready, 1)
                    for j in range(TT):
                        dve.max_index(I8[:, j, :], V8[:, j, :], L[:, j, :]).then_inc(index_ready, 1)
                    dve.wait_ge(index_ready, TT * g + TT)
                    dve.tensor_copy(I[:, ds(TT * g, TT), :], I8[:, :, 0:NR]).then_inc(indexf_ready, 1)
                    dve.wait_ge(indexf_ready, g + 1)
                    iota = cols(MC_IOTA, NE).unsqueeze(1).to_broadcast([P, TT * NR, NE])
                    index = I[:, ds(TT * g, TT), :].rearrange("p j r -> p (j r)").unsqueeze(2).to_broadcast([P, TT * NR, NE])
                    dve.tensor_tensor(pick[:, :, :, :].rearrange("p j r e -> p (j r) e"), iota, index, ALU.is_equal)\
                       .then_inc(pick_ready, 1)
                    dve.wait_ge(pick_ready, g + 1)
                    dve.wait_ge(counts_psum, g)
                    dve.tensor_tensor(both[:, :, :], pick[:, :, 0, :], pick[:, :, 1, :], ALU.add).then_inc(both_ready, 1)
                    dve.wait_ge(counts_psum, g + 1)
                    c = C[h][:, 0:TT * NE].rearrange("p (j e) -> p j e", e=NE)
                    dve.tensor_tensor(row[:, :, :], c, next_row[:, :].unsqueeze(1).to_broadcast([P, TT, NE]), ALU.add)\
                       .then_inc(row_ready, 1)
                    dve.wait_ge(row_ready, g + 1)
                    dve.tensor_tensor(next_row[:, :], next_row[:, :], C[h][:, TT * NE:(TT + 1) * NE], ALU.add)\
                       .then_inc(next_ready, 1)
                    for r in range(NR):
                        dve.tensor_tensor(prow[:, :, r, :], pick[:, :, r, :], row[:, :, :], ALU.mult).then_inc(prow_ready, 1)
                    dve.wait_ge(prow_ready, NR * g + NR)
                    dve.tensor_reduce(rowf[:, :], prow[:, :, :, :].rearrange("p j r e -> p (j r) e"), AX.X, ALU.add)\
                       .then_inc(rowf_ready, 1)
                    dve.wait_ge(rowf_ready, g + 1)
                    dve.wait_ge(scattered[h], 16 * TT * NR * i)
                    dve.tensor_copy(J[:, h, :], rowf[:, :]).then_inc(rows_ready, 1)
                    dve.tensor_scalar(token[:, h, :], mc[:, ds(MC_FULL + TT * g, TT)], cols(MC_P, 1), None, ALU.add)\
                       .then_inc(token_ready, 1)
                    dve.tensor_copy(row_all[:, ds(TT * NR * g, TT * NR)], rowf[:, :]).then_inc(table, 1)

                def down_piece(i, h):
                    g = 2 * i + h
                    dve.wait_ge(dh_made, g + 1)
                    dve.wait_ge(d_loaded[h], 16 * i + 16)
                    at = ds(g * DW, DW)
                    dve.scalar_tensor_tensor(down_lo[:, at], Dn[:, h, :], WS, down_hi[:, at], ALU.mult, ALU.subtract)\
                       .then_inc(dl_made, 1)

                lo(0, 0)
                with dve.Fori(0, NI - 1) as i:
                    for h in range(2):
                        lo(2 * i + h + 1, 1 - h)
                        route(i, h)
                        down_piece(i, h)
                lo(2 * NI - 1, 1)
                for h in range(2):
                    route(NI - 1, h)
                    down_piece(NI - 1, h)
                dve.wait_ge(next_ready, 2 * NI)
                n = 2 * NI

                def step(t):
                    nonlocal n
                    n += 1
                    t.then_inc(table, 1)
                    dve.wait_ge(table, n)

                dve.wait_ge(table, n)
                step(dve.tensor_tensor(n_of[:, :], next_row[:, :], cols(MC_ZONE, NE), ALU.subtract))
                step(dve.tensor_tensor(full[:, :, :], n_of[:, :].unsqueeze(2).to_broadcast([P, NE, B]),
                                       cols(MC_FULL, B).unsqueeze(1).to_broadcast([P, NE, B]), ALU.is_gt))
                step(dve.tensor_reduce(tiles[:, :], full[:, :, :], AX.X, ALU.add))
                step(dve.tensor_tensor(upto[:, :, :], cols(MC_UPTO, NE * NE).rearrange("p (e f) -> p e f", e=NE),
                                       tiles[:, :].unsqueeze(1).to_broadcast([P, NE, NE]), ALU.mult))
                step(dve.tensor_reduce(end[:, :], upto[:, :, :], AX.X, ALU.add))
                step(dve.tensor_tensor(past[:, :, :], end[:, :].unsqueeze(1).to_broadcast([P, NTILE, NE]),
                                       cols(MC_TILE, NTILE).unsqueeze(2).to_broadcast([P, NTILE, NE]), ALU.is_le))
                step(dve.tensor_reduce(et[:, :], past[:, :, :], AX.X, ALU.add))
                step(dve.tensor_tensor(past[:, :, :], past[:, :, :], tiles[:, :].unsqueeze(1).to_broadcast([P, NTILE, NE]),
                                       ALU.mult))
                step(dve.tensor_reduce(before[:, :], past[:, :, :], AX.X, ALU.add))
                step(dve.tensor_tensor(before[:, :], cols(MC_TILE, NTILE), before[:, :], ALU.subtract))
                step(dve.scalar_tensor_tensor(base[:, :], et[:, :], float(ETILE), before[:, :], ALU.mult, ALU.add))
                step(dve.tensor_copy(zone_tile[:, :], base[:, :]))
                step(dve.tensor_scalar(et[:, :], et[:, :], float(NE - 1), float(W3E), ALU.min, ALU.mult))
                step(dve.tensor_copy(expert_at[:, :], et[:, :]))
                step(dve.tensor_tensor(shift[:, :], end[:, :], tiles[:, :], ALU.subtract))
                step(dve.scalar_tensor_tensor(shift[:, :], shift[:, :], float(P), cols(MC_ZONE, NE), ALU.mult, ALU.subtract))
                step(dve.tensor_tensor(pshift[:, :, :], cols(MC_IOTA, NE).unsqueeze(1).to_broadcast([P, B * NR, NE]),
                                       I[:, :, :].rearrange("p j r -> p (j r)").unsqueeze(2).to_broadcast([P, B * NR, NE]),
                                       ALU.is_equal))
                step(dve.tensor_tensor(pshift[:, :, :], pshift[:, :, :], shift[:, :].unsqueeze(1).to_broadcast([P, B * NR, NE]),
                                       ALU.mult))
                step(dve.tensor_reduce(rowf64[:, :], pshift[:, :, :], AX.X, ALU.add))
                step(dve.tensor_tensor(rows_of[:, :], rowf64[:, :], row_all[:, :], ALU.add))

        with nc.Block() as block:

            @block.sync
            def _(sp):
                for h in range(2):
                    sp.wait_ge(scattered[h], 16 * TT * NR * NI)
                sp.dma_start(lst[:, :, :], inv.rearrange("(k q p) o -> q k (p o)", k=3, p=P)).then_inc(list_loaded, 16)

            @block.tensor
            def _(pe):
                pe.wait_ge(list_loaded, 16)
                for k in range(3):
                    t = pe.transpose(T[0][:, k * P:(k + 1) * P], lst[:, k, :], idf[:, :])
                t.then_inc(list_psum, 1)

            @block.vector
            def _(dve):
                dve.wait_ge(list_psum, 1)
                dve.tensor_copy(tokens[:, :], T[0][:, 0:ZTILE]).then_inc(table, 1)


def moe_experts(nc, W12h, W12l, W3h, W3l, idh, xs, ys, tokens, zone_tile, expert_at):
    with ExitStack() as ctx:
        sb = lambda n, s, d=F32: ctx.enter_context(nc.sbuf_tensor(f"ex_{n}", s, d))
        ps = lambda n: ctx.enter_context(nc.psum_tensor(f"ex_{n}", [P, D], F32))
        sem = lambda n: nc.alloc_semaphore(f"ex_{n}")
        K = 4
        NS = NTILE // K
        G = sb("G", [P, K, 2 * D], F16)
        J = sb("J", [P, K], U32)
        XT = sb("XT", [P, 2, 2 * D], F16)
        S = sb("S", [P, 2, FE])
        H = sb("H", [P, 2, 2 * FE], F16)
        HT = sb("HT", [P, 2, 2 * FE], F16)
        Y = sb("Y", [P, K, D])
        TB = [ps(f"TB{k}") for k in range(2)]
        UB = [ps(f"UB{k}") for k in range(2)]
        HB = [ps(f"HB{k}") for k in range(2)]
        DB = [ps(f"DB{k}") for k in range(2)]
        T16 = [t[:, :].bitcast(F16) for t in TB]
        H16 = [t[:, :].bitcast(F16)[:, 0:2 * FE] for t in HB]
        gathered, written = [sem(f"gathered{k}") for k in range(K)], [sem(f"written{k}") for k in range(K)]
        j_ready, xT_psum, xT_ready = sem("j_ready"), sem("xT_psum"), sem("xT_ready")
        up_psum, silu_ready, prod_ready, hi_ready, lo_ready = (sem("up_psum"), sem("silu_ready"), sem("prod_ready"),
                                                               sem("hi_ready"), sem("lo_ready"))
        hT_psum, hT_ready, down_psum, y_ready, apart = (sem("hT_psum"), sem("hT_ready"), sem("down_psum"), sem("y_ready"),
                                                        sem("apart"))

        with nc.Block() as block:

            @block.gpsimd
            def _(pool):

                def fetch(i, k):
                    column = pool.value_load(zone_tile[0:1, ds(K * i + k, 1)], min_val=0, max_val=ZTILE - 1)
                    pool.wait_ge(gathered[k], 16 * i)
                    pool.tensor_copy(J[:, k:k + 1], tokens[:, ds(column, 1)]).then_inc(j_ready, 1)
                    wait_apart(pool, apart, j_ready, K * i + k + 1)
                    if type(i) is not int:
                        wait_apart(pool, apart, xT_psum, K * i + k + 1 - K)
                    pool.indirect_dma_start(G[:, k, :], None, xs, bass.IndirectOffsetOnAxis(ap=J[:, k:k + 1], axis=0))\
                        .then_inc(gathered[k], 16)

                for k in range(K):
                    fetch(0, k)
                with pool.Fori(0, NS - 1) as i:
                    for k in range(K):
                        fetch(i + 1, k)

            @block.sync
            def _(sp):
                with sp.Fori(0, NS) as i:
                    for k in range(K):
                        sp.wait_ge(y_ready, K * i + k + 1)
                        sp.dma_start(ys[ds((K * i + k) * P, P), :], Y[:, k, :]).then_inc(written[k], 16)
                for k in range(K):
                    sp.wait_ge(written[k], 16 * NS)

            @block.tensor
            def _(pe):

                def turn_x(t, i, k):
                    pe.wait_ge(gathered[k], 16 * i + 16)
                    if type(t) is not int or t >= 2:
                        pe.wait_ge(xT_ready, t - 1)
                    for c in range(2 * DC):
                        m = pe.transpose(T16[k % 2][:, c * P:(c + 1) * P], G[:, k, c * P:(c + 1) * P], idh[:, :])
                    m.then_inc(xT_psum, 1)

                def up(t, k):
                    e = pe.value_load(expert_at[0:1, ds(t, 1)], min_val=0, max_val=(NE - 1) * W3E)
                    pe.wait_ge(xT_ready, t + 1)
                    if type(t) is not int or t >= 2:
                        pe.wait_ge(prod_ready, t - 1)
                    for c in range(DC):
                        for n, (x, w) in enumerate(((c, W12h), (DC + c, W12h), (c, W12l))):
                            m = pe.matmul(UB[k % 2][:, :], XT[:, k % 2, x * P:(x + 1) * P],
                                          w[:, ds(e * (W12E // W3E) + c * 2 * FE, 2 * FE)],
                                          start=(c == 0 and n == 0), stop=(c == DC - 1 and n == 2))
                    m.then_inc(up_psum, 1)

                def turn_h(t, k):
                    pe.wait_ge(lo_ready, t + 1)
                    pe.wait_ge(hi_ready, t + 1)
                    if type(t) is not int or t >= 2:
                        pe.wait_ge(hT_ready, t - 1)
                    for c in range(4):
                        m = pe.transpose(H16[k % 2][:, c * P:(c + 1) * P], H[:, k % 2, c * P:(c + 1) * P], idh[:, :])
                    m.then_inc(hT_psum, 1)

                def down(t, k):
                    e = pe.value_load(expert_at[0:1, ds(t, 1)], min_val=0, max_val=(NE - 1) * W3E)
                    pe.wait_ge(hT_ready, t + 1)
                    if type(t) is not int or t >= 2:
                        pe.wait_ge(y_ready, t - 1)
                    for f in range(2):
                        for n, (h, w) in enumerate(((f, W3h), (2 + f, W3h), (f, W3l))):
                            m = pe.matmul(DB[k % 2][:, :], HT[:, k % 2, h * P:(h + 1) * P], w[:, ds(e + f * D, D)],
                                          start=(f == 0 and n == 0), stop=(f == 1 and n == 2))
                    m.then_inc(down_psum, 1)

                def step(i, k, first=False, last=False):
                    s = K * i + k
                    if not last:
                        turn_x(s, i, k)
                    if not (first and s < 1) and not (last and s - 1 >= NTILE):
                        up(s - 1, (k - 1) % K)
                    if not (first and s < 2) and not (last and s - 2 >= NTILE):
                        turn_h(s - 2, (k - 2) % K)
                    if not (first and s < 3):
                        down(s - 3, (k - 3) % K)

                for k in range(K):
                    step(0, k, first=True)
                with pe.Fori(0, NS - 1) as r:
                    for k in range(K):
                        step(r + 1, k)
                for k in range(3):
                    step(NS, k, last=True)

            @block.scalar
            def _(act):

                def turned_x(t, k):
                    act.wait_ge(xT_psum, t + 1)
                    if type(t) is not int or t >= 2:
                        act.wait_ge(up_psum, t - 1)
                    act.activation(XT[:, k % 2, :], T16[k % 2], ACT.Copy).then_inc(xT_ready, 1)

                def silu(t, k):
                    act.wait_ge(up_psum, t + 1)
                    if type(t) is not int or t >= 2:
                        act.wait_ge(lo_ready, t - 1)
                    act.activation(S[:, k % 2, :], UB[k % 2][:, 0:FE], ACT.Silu, scale=1.0 / WS).then_inc(silu_ready, 1)

                turned_x(0, 0)
                turned_x(1, 1)
                silu(0, 0)
                turned_x(2, 2)
                silu(1, 1)
                with act.Fori(0, (NTILE - 4) // 2) as i:
                    for k in range(2):
                        turned_x(2 * i + 3 + k, k + 1)
                        silu(2 * i + 2 + k, k)
                turned_x(NTILE - 1, 1)
                silu(NTILE - 2, 0)
                silu(NTILE - 1, 1)

            @block.vector
            def _(dve):

                def split(t, k):
                    s = S[:, k % 2, :]
                    dve.wait_ge(silu_ready, t + 1)
                    dve.scalar_tensor_tensor(s, UB[k % 2][:, FE:2 * FE], 1.0 / WS, s, ALU.mult, ALU.mult).then_inc(prod_ready, 1)
                    dve.wait_ge(prod_ready, t + 1)
                    if type(t) is not int or t >= 2:
                        dve.wait_ge(hT_psum, t - 1)
                    dve.tensor_copy(H[:, k % 2, 0:FE], s).then_inc(hi_ready, 1)
                    dve.wait_ge(hi_ready, t + 1)
                    dve.tensor_tensor(H[:, k % 2, FE:2 * FE], s, H[:, k % 2, 0:FE], ALU.subtract).then_inc(lo_ready, 1)

                def turned_h(t, k):
                    dve.wait_ge(hT_psum, t + 1)
                    if type(t) is not int or t >= 2:
                        dve.wait_ge(down_psum, t - 1)
                    dve.tensor_copy(HT[:, k % 2, :], H16[k % 2]).then_inc(hT_ready, 1)

                def outputs(t, i, k):
                    dve.wait_ge(down_psum, t + 1)
                    dve.wait_ge(written[k], 16 * i)
                    dve.tensor_scalar(Y[:, k, :], DB[k % 2][:, :], 1.0 / WS, None, ALU.mult).then_inc(y_ready, 1)

                split(0, 0)
                split(1, 1)
                turned_h(0, 0)
                with dve.Fori(0, NS - 1) as i:
                    for k in range(K):
                        t = K * i + k
                        split(t + 2, k)
                        turned_h(t + 1, k + 1)
                        outputs(t, i, k)
                for k in range(K):
                    t = NTILE - K + k
                    if t + 2 < NTILE:
                        split(t + 2, k)
                    if t + 1 < NTILE:
                        turned_h(t + 1, k + 1)
                    outputs(t, NS - 1, k)


def moe_combine(nc, X, ys, rows_of, gap, out):
    with ExitStack() as ctx:
        sb = lambda n, s, d=F32: ctx.enter_context(nc.sbuf_tensor(f"comb_{n}", s, d))
        sem = lambda n: nc.alloc_semaphore(f"comb_{n}")
        th = sb("th", [P, B])
        wt = sb("wt", [P, NR, B])
        J = sb("J", [P, 2, TT * NR], U32)
        Y = sb("Y", [P, 2, TT, NR, D])
        norms = [Norm(nc, ctx, f"moe_norm{h}") for h in range(2)]
        tanh_ready, weights_ready, j_ready, first_added, apart, stored = (
            sem("tanh_ready"), sem("weights_ready"), sem("j_ready"), sem("first_added"), sem("apart"), sem("stored"))
        fetched = [[sem(f"fetched{h}{j}") for j in range(TT)] for h in range(2)]
        NI = B // (2 * TT)

        with nc.Block() as block:

            @block.scalar
            def _(act):
                act.activation(th[:, :], gap[:, :], ACT.Tanh, scale=0.5).then_inc(tanh_ready, 1)

            @block.gpsimd
            def _(pool):

                def fetch(i, h):
                    g = 2 * i + h
                    for j in range(TT):
                        pool.wait_ge(fetched[h][j], 16 * NR * i)
                    pool.tensor_copy(J[:, h, :], rows_of[:, ds(TT * NR * g, TT * NR)]).then_inc(j_ready, 1)
                    wait_apart(pool, apart, j_ready, g + 1)
                    for j in range(TT):
                        if type(i) is not int:
                            wait_apart(pool, apart, norms[h].rows_ready, TT * (i - 1) + j + 1)
                        for r in range(NR):
                            pool.indirect_dma_start(Y[:, h, j, r, :], None, ys,
                                                    bass.IndirectOffsetOnAxis(ap=J[:, h, NR * j + r:NR * j + r + 1], axis=0))\
                                .then_inc(fetched[h][j], 16)

                for n in norms:
                    norm_consts(pool, n)
                fetch(0, 0)
                fetch(0, 1)
                with pool.Fori(0, NI - 1) as i:
                    for h in range(2):
                        fetch(i + 1, h)
                        norm_rstd(pool, norms[h], i)
                for h in range(2):
                    norm_rstd(pool, norms[h], NI - 1)

            @block.vector
            def _(dve):
                dve.wait_ge(tanh_ready, 1)
                dve.tensor_scalar(wt[:, 0, :], th[:, :], 0.5, 0.5, ALU.mult, ALU.add).then_inc(weights_ready, 1)
                dve.tensor_scalar(wt[:, 1, :], th[:, :], -0.5, 0.5, ALU.mult, ALU.add).then_inc(weights_ready, 1)
                dve.wait_ge(weights_ready, 2)

                def add(i, h):
                    g = 2 * i + h
                    for j in range(TT):
                        x = tile(X, TT * g + j)
                        dve.wait_ge(fetched[h][j], 16 * NR * (i + 1))
                        dve.scalar_tensor_tensor(x, Y[:, h, j, 0, :], wt[:, 0, ds(TT * g + j, 1)], x, ALU.mult, ALU.add)\
                           .then_inc(first_added, 1)
                    for j in range(TT):
                        x = tile(X, TT * g + j)
                        dve.wait_ge(first_added, TT * g + j + 1)
                        dve.scalar_tensor_tensor(x, Y[:, h, j, 1, :], wt[:, 1, ds(TT * g + j, 1)], x, ALU.mult, ALU.add)\
                           .then_inc(norms[h].rows_ready, 1)
                    for j in range(TT):
                        norm_stats(dve, norms[h], X, i, j, TT * g + j)
                    for j in range(TT):
                        norm_aggr(dve, norms[h], i, j)

                def apply(i, h):
                    for j in range(TT):
                        norm_apply(dve, norms[h], X, i, j, TT * (2 * i + h) + j)

                add(0, 0)
                add(0, 1)
                apply(0, 0)
                with dve.Fori(0, NI - 1) as i:
                    add(i + 1, 0)
                    apply(i, 1)
                    add(i + 1, 1)
                    apply(i + 1, 0)
                apply(NI - 1, 1)

            @block.sync
            def _(sp):
                n = TT * D
                with sp.Fori(0, NI) as i:
                    for h in range(2):
                        sp.wait_ge(norms[h].normed, TT * i + TT)
                        sp.dma_start(out[:, ds(n * (2 * i + h), n)], group(X, TT * (2 * i + h), TT).rearrange("p b n -> p (b n)"))\
                          .then_inc(stored, 16)
                sp.wait_ge(stored, 16 * (B // TT))


KH = 8
HD = 16
QH = 32
QG = QH // KH
SL = 4
ORDER = (0, 2, 1, 3)
VW = HD + 1


KVW = KH * P + 2 * KH * VW


def context(nc, ctx_dram, kv_dram, idh):
    with ExitStack() as ctx:
        sb = lambda n, s, d=F32: ctx.enter_context(nc.sbuf_tensor(f"ctx_{n}", s, d))
        sem = lambda n: nc.alloc_semaphore(f"ctx_{n}")
        NB = 4
        BB = B // NB
        C = sb("C", [P, B * P])
        K = sb("K", [P, B * KH, SL, HD], F16)
        KT = sb("KT", [SL * HD, B, KH, P], F16)
        V = sb("V", [P, B, 2, KH, VW], F16)
        psK = [ctx.enter_context(nc.psum_tensor(f"ctx_psK{k}", [SL * HD, KH * P], F16)) for k in range(4)]
        loaded = [sem(f"loaded{n}") for n in range(NB)]
        zeros_set, hi_made, lo_made, copied = sem("zeros_set"), sem("hi_made"), sem("lo_made"), sem("copied")
        vhi_made, v_made, turned, out_act, out_dve = (sem("vhi_made"), sem("v_made"), sem("turned"), sem("out_act"),
                                                      sem("out_dve"))
        stored = sem("stored")
        c = C[:, :].rearrange("p (h d) -> p h d", d=HD)
        c4 = C[:, :].rearrange("p (b h d) -> p b h d", d=HD, h=KH)

        with nc.Block() as block:

            @block.sync
            def _(sp):
                for n in range(NB):
                    w = slice(n * BB * P, (n + 1) * BB * P)
                    sp.dma_start(C[:, w], ctx_dram[:, w]).then_inc(loaded[n], 16)
                for n in range(NB):
                    w = slice(n * BB, (n + 1) * BB)
                    sp.wait_ge(v_made, n + 1)
                    sp.dma_start(kv_dram[:, w, KH * P:KVW], V[:, w, :, :, :].rearrange("p b a h d -> p b (a h d)"))\
                      .then_inc(stored, 16)
                    sp.wait_ge(out_act, BB // 2 * (n + 1))
                    sp.wait_ge(out_dve, BB // 2 * (n + 1))
                    sp.dma_start(kv_dram[0:SL * HD, w, 0:KH * P], KT[:, w, :, :].rearrange("p b a t -> p b (a t)"))\
                      .then_inc(stored, 16)
                sp.wait_ge(stored, 32 * NB)

            @block.gpsimd
            def _(pool):
                pool.memset(K[:, :, 3, :], 0.0).then_inc(zeros_set, 1)
                pool.memset(V[:, :, 0, :, HD:VW], 1.0).then_inc(zeros_set, 1)
                pool.memset(V[:, :, 1, :, HD:VW], 0.0).then_inc(zeros_set, 1)
                pool.wait_ge(zeros_set, 3)
                for n in range(NB):
                    w = slice(n * BB, (n + 1) * BB)
                    pool.wait_ge(vhi_made, n + 1)
                    pool.tensor_tensor(V[:, w, 1, :, 0:HD], c4[:, w], V[:, w, 0, :, 0:HD], ALU.subtract).then_inc(v_made, 1)

            @block.scalar
            def _(act):

                def keys_out(n):
                    for b in range(n * BB, (n + 1) * BB, 2):
                        act.wait_ge(turned, b + 1)
                        act.activation(KT[:, b, :, :].rearrange("p a t -> p (a t)"), psK[b % 4][:, :], ACT.Copy).then_inc(out_act, 1)

                for n in range(NB):
                    w, h = slice(n * BB, (n + 1) * BB), slice(n * BB * KH, (n + 1) * BB * KH)
                    act.wait_ge(loaded[n], 16)
                    act.activation(K[:, h, 2, :], c[:, h], ACT.Copy).then_inc(copied, 1)
                    act.activation(V[:, w, 0, :, 0:HD], c4[:, w], ACT.Copy).then_inc(vhi_made, 1)
                    if n:
                        keys_out(n - 1)
                keys_out(NB - 1)

            @block.vector
            def _(dve):

                def keys_out(n):
                    for b in range(n * BB + 1, (n + 1) * BB, 2):
                        dve.wait_ge(turned, b + 1)
                        dve.tensor_copy(KT[:, b, :, :].rearrange("p a t -> p (a t)"), psK[b % 4][:, :]).then_inc(out_dve, 1)

                for n in range(NB):
                    h = slice(n * BB * KH, (n + 1) * BB * KH)
                    dve.wait_ge(loaded[n], 16)
                    dve.tensor_copy(K[:, h, 0, :], c[:, h]).then_inc(hi_made, 1)
                    dve.wait_ge(hi_made, n + 1)
                    dve.tensor_tensor(K[:, h, 1, :], c[:, h], K[:, h, 0, :], ALU.subtract).then_inc(lo_made, 1)
                    if n:
                        keys_out(n - 1)
                keys_out(NB - 1)

            @block.tensor
            def _(pe):
                pe.wait_ge(zeros_set, 3)
                for b in range(B):
                    if b % BB == 0:
                        pe.wait_ge(lo_made, b // BB + 1)
                        pe.wait_ge(copied, b // BB + 1)
                    if b >= 4:
                        pe.wait_ge(out_dve if b % 2 else out_act, (b - 4) // 2 + 1)
                    for a in range(KH):
                        k = K[:, b * KH + a, :, :].rearrange("p s d -> p (s d)")
                        t = pe.transpose(psK[b % 4][:, a * P:(a + 1) * P], k, idh[:, :])
                    t.then_inc(turned, 1)


def cross_attention(nc, name, X, kv_dram, idh, nsel, gmask, prefetch=()):
    with ExitStack() as ctx:
        sb = lambda n, s, d=F32: ctx.enter_context(nc.sbuf_tensor(f"{name}_{n}", s, d))
        ps = lambda n, s, d=F32: ctx.enter_context(nc.psum_tensor(f"{name}_{n}", s, d))
        sem = lambda n: nc.alloc_semaphore(f"{name}_{n}")
        LAG = 3
        KT = sb("KT", [P, 3, 2, KH, P], F16)
        V = sb("V", [P, 3, 2, KH, VW], F16)
        Q = sb("Q", [P, QH, SL, HD], F16)
        QT = sb("QT", [P, 3, 16, P], F16)
        Mx = sb("Mx", [P, QH], F16)
        MD = sb("MD", [QH, 3, QG, P], F16)
        W32, Wh, Wl = sb("W32", [P, KH, GT]), sb("Wh", [P, KH, GT], F16), sb("Wl", [P, KH, GT], F16)
        rinv = sb("rinv", [P, QH])
        O = sb("O", [P, D])
        psQ = ps("psQ", [P, 8, P], F16)
        psM = ps("psM", [QH, P], F16)
        psS = [ps(f"psS{k}", [P, QG, P]) for k in range(2)]
        psW = [ps(f"psW{k}", [P, GT]) for k in range(2)]
        psO = [ps(f"psO{k}", [P, 16, VW]) for k in range(2)]
        norm = Norm(nc, ctx, f"{name}_norm", 1)
        qh_ready, ql_ready, q_psum, q_ready = sem("qh_ready"), sem("ql_ready"), sem("q_psum"), sem("q_ready")
        s_psum, max_ready, m_psum, md_ready = sem("s_psum"), sem("max_ready"), sem("m_psum"), sem("md_ready")
        w_psum, w32_ready, wh_ready, wl_dve, wl_pool = (sem("w_psum"), sem("w32_ready"), sem("wh_ready"), sem("wl_dve"),
                                                        sem("wl_pool"))
        kv_loaded = [sem(f"kv_loaded{u}") for u in range(3)]
        zeros_set, pv_done, rinv_ready, o_ready = sem("zeros_set"), sem("pv_done"), sem("rinv_ready"), sem("o_ready")
        qh2_ready, prefetched = sem("qh2_ready"), sem("prefetched")


        LO_DVE = (0, 2, 4)

        def first(b):
            return type(b) is int and b == 0

        def lo_count(k):
            if k in LO_DVE:
                return wl_dve, len(LO_DVE), LO_DVE.index(k) + 1
            return wl_pool, KH - len(LO_DVE), k + 1 - sum(d < k for d in LO_DVE)


        def q_hi(pool, b):
            pool.wait_ge(q_psum, 2 * b)
            pool.tensor_copy(Q[:, :, 0, :], tile(X, b).rearrange("p (h d) -> p h d", d=HD)).then_inc(qh_ready, 1)

        def q_hi_again(act, b):
            act.wait_ge(q_psum, 2 * b)
            act.activation(Q[:, :, 1, :], tile(X, b).rearrange("p (h d) -> p h d", d=HD), ACT.Copy).then_inc(qh2_ready, 1)

        def q_lo(pool, b):
            wait_apart(pool, norm.waits_apart, qh_ready, b + 1)
            x = tile(X, b).rearrange("p (h d) -> p h d", d=HD)
            pool.tensor_tensor(Q[:, :, 2, :], x, Q[:, :, 0, :], ALU.subtract).then_inc(ql_ready, 1)

        def turn_q(pe, b, half):
            if half == 0:
                pe.wait_ge(ql_ready, b + 1)
                pe.wait_ge(qh_ready, b + 1)
                pe.wait_ge(qh2_ready, b + 1)
            pe.wait_ge(q_ready, 2 * b + half)
            for n in range(8):
                h = 2 * (8 * half + n)
                q = Q[:, h:h + 2, :, :].rearrange("p h s d -> p (h s d)")
                t = pe.transpose(psQ[:, n, :], q, idh[:, :])
            t.then_inc(q_psum, 1)

        def q_out(act, b, u, half):
            act.wait_ge(q_psum, 2 * b + half + 1)
            act.activation(QT[:, u, 8 * half:8 * half + 8, :].rearrange("p a t -> p (a t)"),
                           psQ[:, :, :].rearrange("p a t -> p (a t)"), ACT.Copy).then_inc(q_ready, 1)

        def scores(pe, b, u, k):
            if k == 0:
                pe.wait_ge(kv_loaded[u], 16 * (b - u) + 48)
            pe.wait_ge(q_ready, 2 * b + 1 + k // 4)
            if not (first(b) and k < 2):
                pe.wait_ge(max_ready, KH * b + k - 1)
            if k == 0:
                pe.wait_ge(zeros_set, 7)
            for a in range(2):
                t = pe.matmul(psS[k % 2][:, 2 * a:2 * a + 2, :], QT[:, u, 2 * k + a, :], KT[:, u, :, k, :], start=True, stop=True)
            t.then_inc(s_psum, 1)

        def load(sp, b, u):
            for e in range(2):
                r = slice(64 * e, 64 * e + 64)
                sp.dma_start(KT[r, u, e, :, :].rearrange("p k t -> p (k t)"),
                             kv_dram[0:64, ds(b, 1), 0:KH * P].rearrange("p a n -> p (a n)")).then_inc(kv_loaded[u], 16)
            sp.dma_start(V[:, u, :, :, :].rearrange("p a k d -> p (a k d)"),
                         kv_dram[:, ds(b, 1), KH * P:KVW].rearrange("p a n -> p (a n)")).then_inc(kv_loaded[u], 16)

        def maxima(dve, b, k):
            dve.wait_ge(s_psum, KH * b + k + 1)
            if k == 0:
                dve.wait_ge(m_psum, b)
            dve.tensor_reduce(Mx[:, QG * k:QG * k + QG], psS[k % 2][:, :, :], AX.X, ALU.max).then_inc(max_ready, 1)

        def turn_max(pe, b):
            pe.wait_ge(max_ready, KH * b + KH)
            pe.wait_ge(md_ready, b)
            pe.transpose(psM[:, :], Mx[:, :], idh[:, :]).then_inc(m_psum, 1)

        def spread_max(dve, b, u):
            dve.wait_ge(m_psum, b + 1)
            dve.tensor_tensor(MD[:, u, :, :], psM[:, :].unsqueeze(1).to_broadcast([QH, QG, P]), gmask, ALU.mult)\
               .then_inc(md_ready, 1)

        def turned_scores(pe, b, u, k):
            if not (first(b) and k < 2):
                pe.wait_ge(wh_ready, KH * b + k - 1)
            if k == 0:
                pe.wait_ge(md_ready, b + 1)
            pe.matmul(psW[k % 2][:, :], nsel[:, k * P:(k + 1) * P], MD[:, u, :, :].rearrange("p g t -> p (g t)"),
                      start=True, stop=False)
            for e in range(2):
                t = pe.matmul(psW[k % 2][:, 2 * P * e:2 * P * e + 2 * P], KT[:, u, e, k, :],
                              QT[:, u, 2 * k:2 * k + 2, :].rearrange("p a t -> p (a t)"), start=False, stop=(e == 1))
            t.then_inc(w_psum, 1)

        def weights(act, b, k):
            act.wait_ge(w_psum, KH * b + k + 1)
            wl, n, m = lo_count(k)
            if not first(b):
                act.wait_ge(wl, n * (b - 1) + m)
            act.activation(W32[:, k, :], psW[k % 2][:, :], ACT.Exp, scale=0.25).then_inc(w32_ready, 1)
            if not first(b):
                act.wait_ge(pv_done, KH * (b - 1) + k + 1)
            act.activation(Wh[:, k, :], psW[k % 2][:, :], ACT.Exp, scale=0.25).then_inc(wh_ready, 1)

        def weights_lo(eng, b, k):
            eng.wait_ge(w32_ready, KH * b + k + 1)
            eng.wait_ge(wh_ready, KH * b + k + 1)
            if not first(b):
                eng.wait_ge(pv_done, KH * (b - 1) + k + 1)
            eng.tensor_tensor(Wl[:, k, :], W32[:, k, :], Wh[:, k, :], ALU.subtract)\
               .then_inc(lo_count(k)[0], 1)

        def values(pe, b, u, k):
            pe.wait_ge(wh_ready, KH * b + k + 1)
            wl, n, m = lo_count(k)
            pe.wait_ge(wl, n * b + m)
            if k % 4 == 0 and not first(b):
                pe.wait_ge(o_ready, 2 * (b - 1) + k // 4 + 1)
            v = [V[:, u, h, k, :] for h in range(2)]
            for g in range(QG):
                h = QG * k + g
                at = ORDER.index(g) * P
                w = slice(at, at + P)
                out = psO[h // 16][:, h % 16, :]
                pe.matmul(out, Wh[:, k, w], v[0], start=True, stop=False)
                pe.matmul(out, Wh[:, k, w], v[1], start=False, stop=False)
                t = pe.matmul(out, Wl[:, k, w], v[0], start=False, stop=True)
            t.then_inc(pv_done, 1)

        def divide(dve, b, a):
            r = rinv[:, 16 * a:16 * a + 16]
            dve.wait_ge(pv_done, KH * b + 4 * a + 4)
            dve.reciprocal(r, psO[a][:, :, HD]).then_inc(rinv_ready, 1)
            dve.wait_ge(rinv_ready, 2 * b + a + 1)
            dve.tensor_tensor(O[:, 256 * a:256 * a + 256].rearrange("p (h d) -> p h d", d=HD), psO[a][:, :, 0:HD],
                              r.unsqueeze(2).to_broadcast([P, 16, HD]), ALU.mult).then_inc(o_ready, 1)

        def add(dve, b):
            dve.wait_ge(o_ready, 2 * b + 2)
            x = tile(X, b)
            dve.tensor_tensor(x, x, O[:, :], ALU.add).then_inc(norm.rows_ready, 1)

        def every_sequence(eng, sequence):
            for b in range(2):
                sequence(b, b, lambda d: b + d >= 0)
            with eng.Fori(0, (B - 5) // 3) as r:
                for v in range(3):
                    sequence(r * 3 + (v + 2), (v + 2) % 3, lambda d: True)
            for b in range(B - 3, B):
                sequence(b, b % 3, lambda d: b + d < B)

        with nc.Block() as block:

            @block.sync
            def _(sp):
                for b in range(3):
                    load(sp, b, b)
                for to, of in prefetch:
                    sp.dma_start(to, of).then_inc(prefetched, 16)

                def reload(b, u):
                    sp.wait_ge(w_psum, KH * (b + 1))
                    sp.wait_ge(pv_done, KH * (b + 1))
                    load(sp, b + 3, u)

                with sp.Fori(0, (B - 5) // 3) as r:
                    for v in range(3):
                        reload(r * 3 + v, v)
                for b in range(B - 5, B - 3):
                    reload(b, b % 3)
                if prefetch:
                    sp.wait_ge(prefetched, 16 * len(prefetch))

            @block.gpsimd
            def _(pool):
                norm_consts(pool, norm)
                for b in range(3):
                    q_hi(pool, b)
                    q_lo(pool, b)

                def sequence(b, u, has):
                    weights_lo(pool, b, 1)
                    weights_lo(pool, b, 3)
                    weights_lo(pool, b, 5)
                    if has(3):
                        q_hi(pool, b + 3)
                    weights_lo(pool, b, 6)
                    weights_lo(pool, b, 7)
                    if has(-1):
                        norm_rstd(pool, norm, b - 1)
                    if has(3):
                        q_lo(pool, b + 3)

                every_sequence(pool, sequence)
                norm_rstd(pool, norm, B - 1)

            @block.tensor
            def _(pe):

                def sequence(b, u, has):
                    for k in range(KH):
                        turned_scores(pe, b, u, k)
                        if k < KH - 1 and has(1):
                            scores(pe, b + 1, (u + 1) % 3, k + 1)
                        if k >= LAG:
                            values(pe, b, u, k - LAG)
                        elif has(-1):
                            values(pe, b - 1, (u + 2) % 3, KH + k - LAG)
                        if k in (3, 5) and has(2):
                            turn_q(pe, b + 2, k // 4)
                    if has(1):
                        turn_max(pe, b + 1)
                    if has(2):
                        scores(pe, b + 2, (u + 2) % 3, 0)

                pe.wait_ge(zeros_set, 7)
                for half in range(2):
                    turn_q(pe, 0, half)
                for k in range(KH):
                    scores(pe, 0, 0, k)
                turn_max(pe, 0)
                for half in range(2):
                    turn_q(pe, 1, half)
                scores(pe, 1, 1, 0)
                every_sequence(pe, sequence)
                for k in range(KH - LAG, KH):
                    values(pe, B - 1, (B - 1) % 3, k)

            @block.scalar
            def _(act):

                def sequence(b, u, has):
                    for k in range(KH):
                        weights(act, b, k)
                        if k in (3, 5) and has(2):
                            q_out(act, b + 2, (u + 2) % 3, k // 4)
                    if has(3):
                        q_hi_again(act, b + 3)

                for b in range(2):
                    q_hi_again(act, b)
                    for half in range(2):
                        q_out(act, b, b, half)
                q_hi_again(act, 2)
                every_sequence(act, sequence)

            @block.vector
            def _(dve):

                def sequence(b, u, has):
                    for k in range(KH):
                        if k < KH - 1 and has(1):
                            maxima(dve, b + 1, k + 1)
                        if k - 1 in LO_DVE:
                            weights_lo(dve, b, k - 1)
                        if k == 2 and has(-2):
                            norm_apply(dve, norm, X, b - 2, 0)
                        if k == 3 and has(-1):
                            divide(dve, b - 1, 1)
                        if k == 4 and has(-1):
                            add(dve, b - 1)
                        if k == 5 and has(-1):
                            norm_stats(dve, norm, X, b - 1, 0)
                        if k == 6 and has(-1):
                            norm_aggr(dve, norm, b - 1, 0)
                    if has(1):
                        spread_max(dve, b + 1, (u + 1) % 3)
                    divide(dve, b, 0)
                    if has(2):
                        maxima(dve, b + 2, 0)

                dve.memset(Q[:, :, 3, :], 0.0).then_inc(zeros_set, 1)
                for u in range(3):
                    for e in range(2):
                        dve.memset(KT[64 - 64 * e:128 - 64 * e, u, e, :, :], 0.0).then_inc(zeros_set, 1)
                for k in range(KH):
                    maxima(dve, 0, k)
                spread_max(dve, 0, 0)
                maxima(dve, 1, 0)
                every_sequence(dve, sequence)
                norm_apply(dve, norm, X, B - 2, 0)
                divide(dve, B - 1, 1)
                add(dve, B - 1)
                norm_stats(dve, norm, X, B - 1, 0)
                norm_aggr(dve, norm, B - 1, 0)
                norm_apply(dve, norm, X, B - 1, 0)


LAT = 128
LA_LOADS = 16 * 10
DCMP = 64


def latent_attention(nc, X, w, idf, up):
    with ExitStack() as ctx:
        sb = lambda n, s, d=F32: ctx.enter_context(nc.sbuf_tensor(f"la_{n}", s, d))
        sem = lambda n: nc.alloc_semaphore(f"la_{n}")
        ps = lambda n: ctx.enter_context(nc.psum_tensor(f"la_{n}", [P, GT], F32))
        psT = [ps(f"psT{k}") for k in range(2)]
        psC = ps("psC")
        psCT = ps("psCT")
        psQ = [ps(f"psQ{k}") for k in range(2)]
        psS = ps("psS")
        psE = ps("psE")
        Wkv = sb("Wkv", [P, D])
        Wsum = sb("Wsum", [P, D])
        WcT = sb("WcT", [P, DCMP])
        Wl = sb("Wl", [P, DCMP])
        Win = sb("Win", [P, DC, DCMP])
        Wout = sb("Wout", [P, D])
        Wqk = sb("Wqk", [P, 3, P])
        WvT = sb("WvT", [P, DCMP])
        gb = sb("gb", [DCMP, 2])
        rope = sb("rope", [P, 2, GT])
        mask = sb("mask", [P, P])
        bout = sb("bout", [P, D])
        X4 = sb("X4", [P, GS, D])
        XT = sb("XT", [P, DC, GT])
        x_copied = sem("x_copied")
        CN = sb("CN", [P, GS, DCMP])
        CT = sb("CT", [P, GT])
        RT = sb("RT", [P, 3, GT])
        V = sb("V", [P, GS, DCMP])
        S = sb("S", [P, GS, P])
        E = sb("E", [P, GS, P])
        ET = sb("ET", [P, GS, P])
        OT = sb("OT", [P, GT])
        up_dram, up_hi, up_lo = up
        UW = NE * W12E // (2 * NG)
        U = sb("U", [P, 2, 2 * UW])
        mx, nmx = sb("mx", [P, GS]), sb("nmx", [P, GS])
        rs, rinv = sb("rs", [P, GS]), sb("rinv", [P, GS])
        norm = Norm(nc, ctx, "la_norm")
        cn = Norm(nc, ctx, "la_cnorm")
        loaded, w_summed = sem("loaded"), sem("w_summed")
        u_loaded, u_scaled, uh_made, ul_made = ([sem(f"u_loaded{h}") for h in range(2)], sem("u_scaled"), sem("uh_made"),
                                                  sem("ul_made"))
        xT_psum, xT_ready, win_psum, win_ready = sem("xT_psum"), sem("xT_ready"), sem("win_psum"), sem("win_ready")
        c_psum, cn_ready, cT_psum, cT_ready = sem("c_psum"), sem("cn_ready"), sem("cT_psum"), sem("cT_ready")
        qk_psum, roped, zeros_set, v_psum, v_ready = (sem("qk_psum"), sem("roped"), sem("zeros_set"), sem("v_psum"),
                                                      sem("v_ready"))
        s_psum, s_masked, mx_ready, nmx_ready, e_ready = (sem("s_psum"), sem("s_masked"), sem("mx_ready"), sem("nmx_ready"),
                                                          sem("e_ready"))
        eT_psum, eT_ready, oT_psum, oT_ready = sem("eT_psum"), sem("eT_ready"), sem("oT_psum"), sem("oT_ready")
        wout_psum, wout_ready, out_psum, rinv_ready, biased = (sem("wout_psum"), sem("wout_ready"), sem("out_psum"),
                                                               sem("rinv_ready"), sem("biased"))
        j4 = lambda t: t.rearrange("p (j n) -> p j n", j=GS)

        with nc.Block() as block:

            @block.sync
            def _(sp):
                pairs = [(Wkv[:, :], w["Wkv"]), (Wsum[:, :], w["WoT"]), (WcT[:, :], w["WcT"]),
                         (Wqk[:, :, :].rearrange("p c n -> p (c n)"), w["Wqk"]), (WvT[:, :], w["WvT"]),
                         (Wl[:, :], w["Wl"]), (gb[:, :], w["gb"]), (rope[:, :, :].rearrange("p c n -> p (c n)"), w["rope"]),
                         (mask[:, :], w["mask"]), (bout[:, :], w["bout"].partition_broadcast(P))]
                for to, of in pairs:
                    sp.dma_start(to, of).then_inc(loaded, 16)
                sp.wait_ge(loaded, LA_LOADS)

                def copy(i):
                    sp.dma_start(X4[:, :, :], group(X, GS * i)).then_inc(x_copied, 16)

                def load_up(g, h):
                    sp.dma_start(U[:, h, :], up_dram[:, ds(g * (2 * UW), 2 * UW)]).then_inc(u_loaded[h], 16)

                copy(0)
                for h in range(2):
                    load_up(h, h)
                sp.wait_ge(xT_psum, DC)
                copy(1)
                with sp.Fori(0, NG // 2 - 1) as r:
                    for h in range(2):
                        sp.wait_ge(xT_psum, DC * (2 * r + h) + 2 * DC)
                        copy(r * 2 + (h + 2))
                        sp.wait_ge(ul_made, 4 * r + 2 * h + 2)
                        load_up(r * 2 + (h + 2), h)
                sp.wait_ge(x_copied, 16 * NG)

            @block.gpsimd
            def _(pool):
                norm_consts(pool, norm)
                norm_consts(pool, cn)
                pool.wait_ge(loaded, LA_LOADS)
                pool.tensor_tensor(Wsum[:, :], Wsum[:, :], Wkv[:, :], ALU.add).then_inc(w_summed, 1)
                norm_rstd(pool, cn, 0)

                def bias(i):
                    wait_apart(pool, norm.waits_apart, xT_psum, DC * i + DC)
                    for j in range(GS):
                        x = tile(X, GS * i + j)
                        pool.tensor_tensor(x, x, bout[:, :], ALU.add).then_inc(biased, 1)

                bias(0)
                norm_rstd(pool, cn, 1)
                bias(1)

                def up_los(i, h):
                    for k in range(2):
                        pool.wait_ge(uh_made, 2 * i + k + 1)
                        at = ds((2 * i + k) * UW, UW)
                        pool.tensor_tensor(up_lo[:, at], U[:, h, k * UW:(k + 1) * UW], up_hi[:, at], ALU.subtract)\
                            .then_inc(ul_made, 1)

                with pool.Fori(0, NG // 2 - 1) as r:
                    for h in range(2):
                        i = r * 2 + h
                        bias(i + 2)
                        norm_rstd(pool, cn, i + 2)
                        norm_rstd(pool, norm, i)
                        up_los(i, h)
                for i in range(NG - 2, NG):
                    up_los(i, i % 2)
                norm_rstd(pool, norm, NG - 2)
                norm_rstd(pool, norm, NG - 1)

            @block.tensor
            def _(pe):

                def weights_products():
                    pe.wait_ge(loaded, LA_LOADS)
                    for c in range(DC):
                        m = pe.matmul(psC[:, c * DCMP:(c + 1) * DCMP], Wkv[:, c * P:(c + 1) * P], WcT[:, :], start=True, stop=True)
                    m.then_inc(win_psum, 1)
                    pe.wait_ge(w_summed, 1)
                    pe.matmul(psS[0:DCMP, :], Wl[:, :], Wsum[:, :], start=True, stop=True).then_inc(wout_psum, 1)

                def turn_x(i):
                    pe.wait_ge(x_copied, 16 * i + 16)
                    if type(i) is not int or i > 0:
                        pe.wait_ge(norm.rows_ready, GS * (i - 1))
                    for c in range(DC):
                        pe.wait_ge(xT_ready, DC * i + max(0, c - 1))
                        for j in range(GS):
                            x = X4[:, j, c * P:(c + 1) * P]
                            t = pe.transpose(psT[c % 2][:, j * P:(j + 1) * P], x, idf[:, :])
                        t.then_inc(xT_psum, 1)

                def compressed(i):
                    pe.wait_ge(xT_ready, DC * i + DC)
                    pe.wait_ge(cn_ready, GS * i)
                    for j in range(GS):
                        for c in range(DC):
                            t = pe.matmul(psC[:, j * DCMP:(j + 1) * DCMP], XT[:, c, j * P:(j + 1) * P], Win[:, c, :],
                                          start=(c == 0), stop=(c == DC - 1))
                    t.then_inc(c_psum, 1)

                def turn_c(i):
                    wait_apart(pe, cn.waits_apart, cT_ready, i)
                    wait_apart(pe, cn.waits_apart, cn_ready, GS * i + GS)
                    for j in range(GS):
                        t = pe.transpose(psCT[0:DCMP, j * P:(j + 1) * P], CN[:, j, :], idf[:, :])
                    t.then_inc(cT_psum, 1)

                def queries_keys(i):
                    wait_apart(pe, norm.waits_apart, cT_ready, i + 1)
                    for n in range(3):
                        if n == 2:
                            wait_apart(pe, norm.waits_apart, roped, 3 * i + 1)
                        elif type(i) is not int or i > 0:
                            wait_apart(pe, norm.waits_apart, roped, 3 * i)
                        pe.matmul(psQ[n % 2][:, :], Wqk[:, n, :], CT[:, :], start=True, stop=True).then_inc(qk_psum, 1)
                    wait_apart(pe, norm.waits_apart, v_ready, i)
                    for j in range(GS):
                        t = pe.matmul(psC[:, (GS + j) * DCMP:(GS + j + 1) * DCMP], CT[:, j * P:(j + 1) * P], WvT[:, :],
                                      start=True, stop=True)
                    t.then_inc(v_psum, 1)

                def scores(i):
                    pe.wait_ge(roped, 3 * i + 3)
                    pe.wait_ge(oT_ready, i)
                    for j in range(GS):
                        c = slice(j * P, (j + 1) * P)
                        pe.matmul(psS[:, c], RT[:, 0, c], RT[:, 1, c], start=True, stop=False)
                        t = pe.matmul(psS[:, c], RT[:, 0, c], RT[:, 2, c], start=False, stop=True)
                    t.then_inc(s_psum, 1)

                def turn_e(i):
                    pe.wait_ge(e_ready, GS * i + GS)
                    pe.wait_ge(eT_ready, i)
                    for j in range(GS):
                        t = pe.transpose(psE[:, j * P:(j + 1) * P], E[:, j, :], idf[:, :])
                    t.then_inc(eT_psum, 1)

                def attended(i):
                    pe.wait_ge(eT_ready, i + 1)
                    pe.wait_ge(v_ready, i + 1)
                    for j in range(GS):
                        t = pe.matmul(psS[0:DCMP, j * P:(j + 1) * P], V[:, j, :], ET[:, j, :], start=True, stop=True)
                    t.then_inc(oT_psum, 1)

                def outputs(i, last=False):
                    pe.wait_ge(oT_ready, i + 1)
                    pe.wait_ge(xT_ready, DC * i + DC * (1 if last else 2))
                    for j in range(GS):
                        if j >= 2:
                            pe.wait_ge(norm.rows_ready, GS * i + j - 1)
                        pe.matmul(psT[j % 2][:, :], OT[:, j * P:(j + 1) * P], Wout[:, :], start=True, stop=True)\
                          .then_inc(out_psum, 1)

                pe.wait_ge(zeros_set, 3)
                weights_products()
                turn_x(0)
                pe.wait_ge(win_ready, 1)
                compressed(0)
                turn_c(0)
                queries_keys(0)
                pe.wait_ge(wout_ready, 1)

                def turn(i):
                    scores(i)
                    turn_x(i + 1)
                    compressed(i + 1)
                    turn_e(i)
                    attended(i)
                    outputs(i)
                    turn_c(i + 1)
                    queries_keys(i + 1)

                turn(0)
                with pe.Fori(0, NG - 2) as r:
                    turn(r + 1)
                scores(NG - 1)
                turn_e(NG - 1)
                attended(NG - 1)
                outputs(NG - 1, last=True)

            @block.scalar
            def _(act):

                def x_out(i):
                    act.wait_ge(c_psum, i)
                    for c in range(DC):
                        act.wait_ge(xT_psum, DC * i + c + 1)
                        act.activation(XT[:, c, :], psT[c % 2][:, :], ACT.Copy).then_inc(xT_ready, 1)

                def c_out(i):
                    act.wait_ge(cT_psum, i + 1)
                    act.wait_ge(v_psum, i)
                    act.activation(CT[0:DCMP, :], psCT[0:DCMP, :], ACT.Identity, bias=gb[:, 1:2], scale=gb[:, 0:1])\
                       .then_inc(cT_ready, 1)

                def v_out(i):
                    act.wait_ge(v_psum, i + 1)
                    act.wait_ge(oT_psum, i)
                    act.activation(V[:, :, :].rearrange("p j n -> p (j n)"), psC[:, GS * DCMP:2 * GS * DCMP], ACT.Copy)\
                       .then_inc(v_ready, 1)

                def exps(i):
                    act.wait_ge(nmx_ready, i + 1)
                    act.wait_ge(eT_psum, i)
                    act.wait_ge(rinv_ready, i)
                    for j in range(GS):
                        act.activation(E[:, j, :], S[:, j, :], ACT.Exp, bias=nmx[:, j:j + 1], scale=0.125,
                                       accum_out=rs[:, j:j + 1]).then_inc(e_ready, 1)

                def e_out(i):
                    act.wait_ge(eT_psum, i + 1)
                    act.wait_ge(oT_psum, i)
                    act.activation(ET[:, :, :].rearrange("p j n -> p (j n)"), psE[:, :], ACT.Copy).then_inc(eT_ready, 1)

                def o_out(i):
                    act.wait_ge(oT_psum, i + 1)
                    act.wait_ge(out_psum, GS * i)
                    act.activation(OT[0:DCMP, :], psS[0:DCMP, :], ACT.Copy).then_inc(oT_ready, 1)

                def up_his(i, h, k):
                    c = slice(k * UW, (k + 1) * UW)
                    act.wait_ge(u_loaded[h], (i - h) * 8 + 16)
                    act.activation(U[:, h, c], U[:, h, c], ACT.Copy, scale=WS).then_inc(u_scaled, 1)
                    act.wait_ge(u_scaled, 2 * i + k + 1)
                    act.activation(up_hi[:, ds((2 * i + k) * UW, UW)], U[:, h, c], ACT.Copy).then_inc(uh_made, 1)

                act.wait_ge(loaded, LA_LOADS)
                act.wait_ge(win_psum, 1)
                act.activation(Win[:, :, :].rearrange("p c n -> p (c n)"), psC[:, 0:DC * DCMP], ACT.Copy).then_inc(win_ready, 1)
                act.wait_ge(wout_psum, 1)
                act.activation(Wout[0:DCMP, :], psS[0:DCMP, :], ACT.Copy).then_inc(wout_ready, 1)
                x_out(0)
                c_out(0)
                v_out(0)

                def turn(i, h):
                    x_out(i + 1)
                    exps(i)
                    e_out(i)
                    o_out(i)
                    up_his(i, h, 0)
                    c_out(i + 1)
                    up_his(i, h, 1)
                    v_out(i + 1)

                turn(0, 0)
                with act.Fori(0, NG // 2 - 1) as r:
                    for h in range(2):
                        turn(r * 2 + (1 + h), 1 - h)
                for k in range(2):
                    up_his(NG - 1, 1, k)
                exps(NG - 1)
                e_out(NG - 1)
                o_out(NG - 1)

            @block.vector
            def _(dve):

                def compressed_norm(i):
                    wait_apart(dve, cn.waits_apart, c_psum, i + 1)
                    for j in range(GS):
                        dve.bn_stats(cn.stats[:, j, :], psC[:, j * DCMP:(j + 1) * DCMP]).then_inc(cn.stats_ready, 1)
                    for j in range(GS):
                        norm_aggr(dve, cn, i, j)
                    dve.wait_ge(cn.rstd_ready, i + 1)
                    dve.wait_ge(cT_psum, i)
                    for j in range(GS):
                        dve.tensor_scalar(CN[:, j, :], psC[:, j * DCMP:(j + 1) * DCMP], cn.mv[:, j, 0:1],
                                          cn.rstd[:, j:j + 1], ALU.subtract, ALU.mult).then_inc(cn_ready, 1)

                def apply_rope(i):
                    dve.wait_ge(s_psum, i)
                    for n in range(3):
                        dve.wait_ge(qk_psum, 3 * i + n + 1)
                        dve.tensor_tensor(RT[:, n, :], psQ[n % 2][:, :], rope[:, n // 2, :], ALU.mult).then_inc(roped, 1)

                def masked(i):
                    dve.wait_ge(s_psum, i + 1)
                    dve.wait_ge(e_ready, GS * i)
                    dve.tensor_tensor(S[:, :, :], j4(psS[:, :]), mask[:, :].unsqueeze(1).to_broadcast([P, GS, P]), ALU.add)\
                       .then_inc(s_masked, 1)
                    dve.wait_ge(s_masked, i + 1)
                    dve.tensor_reduce(mx[:, :], S[:, :, :], AX.X, ALU.max).then_inc(mx_ready, 1)
                    dve.wait_ge(mx_ready, i + 1)
                    dve.tensor_scalar(nmx[:, :], mx[:, :], -0.125, None, ALU.mult).then_inc(nmx_ready, 1)

                def add(i):
                    dve.wait_ge(e_ready, GS * i + GS)
                    dve.reciprocal(rinv[:, :], rs[:, :]).then_inc(rinv_ready, 1)
                    dve.wait_ge(rinv_ready, i + 1)
                    for j in range(GS):
                        dve.wait_ge(out_psum, GS * i + j + 1)
                        dve.wait_ge(biased, GS * i + j + 1)
                        x = tile(X, GS * i + j)
                        dve.scalar_tensor_tensor(x, psT[j % 2][:, :], rinv[:, j:j + 1], x, ALU.mult, ALU.add)\
                           .then_inc(norm.rows_ready, 1)

                def stats(i):
                    for j in range(GS):
                        norm_stats(dve, norm, X, i, j)
                    for j in range(GS):
                        norm_aggr(dve, norm, i, j)

                def apply(i):
                    for j in range(GS):
                        norm_apply(dve, norm, X, i, j)

                for z in (CT, OT, Wout):
                    dve.memset(z[DCMP:P, :], 0.0).then_inc(zeros_set, 1)
                dve.wait_ge(loaded, LA_LOADS)
                compressed_norm(0)
                apply_rope(0)
                masked(0)
                compressed_norm(1)
                add(0)
                apply_rope(1)
                with dve.Fori(0, NG - 2) as r:
                    masked(r + 1)
                    stats(r)
                    compressed_norm(r + 2)
                    add(r + 1)
                    apply_rope(r + 2)
                    apply(r)
                masked(NG - 1)
                stats(NG - 2)
                apply(NG - 2)
                add(NG - 1)
                stats(NG - 1)
                apply(NG - 1)


CT = 16
NCT = P // CT
LC = 2 * P


WQ = 3 * DC * P


PIECES = [(n * WQ, (n + 1) * WQ) for n in range(DC)] + [(DC * WQ, DC * WQ + DC * D)]


def hyena_taps(nc, kerT, dskip, taps, wqkv, wo, wpair):
    with ExitStack() as ctx:
        sb = lambda n, s, d=F32: ctx.enter_context(nc.sbuf_tensor(f"ht_{n}", s, d))
        sem = lambda n: nc.alloc_semaphore(f"ht_{n}")
        E = sb("E", [P, 2, D])
        Dk = sb("Dk", [P, D])
        H = [sb("Eh", [P, 2, D], F16), sb("El", [P, 2, D], F16)]
        W = sb("W", [P, PIECES[-1][1]])
        Wp = [sb("Wh", [P, PIECES[-1][1]], F16), sb("Wl", [P, PIECES[-1][1]], F16)]
        w_loaded = [sem(f"w_loaded{k}") for k in range(len(PIECES))]
        wh_made, wl_made, w_stored = sem("wh_made"), sem("wl_made"), sem("w_stored")
        loaded, added, hi_made, lo_made, stored = sem("loaded"), sem("added"), sem("hi_made"), sem("lo_made"), sem("stored")
        with nc.Block() as block:

            @block.sync
            def _(sp):
                sp.dma_start(E[:, :, :].rearrange("p a c -> p (a c)"), kerT).then_inc(loaded, 16)
                sp.dma_start(Dk[:, :], dskip).then_inc(loaded, 16)
                for n, (a, b) in enumerate(PIECES):
                    sp.dma_start(W[:, a:b], wqkv[:, a:b] if n < DC else wo).then_inc(w_loaded[n], 16)
                for k, made in enumerate((hi_made, lo_made)):
                    sp.wait_ge(made, 1)
                    for a in range(2):
                        sp.dma_start(taps[k, :, a * P:(a + 1) * P, :].rearrange("n i c -> i n c"),
                                     H[k][:, a, :].rearrange("p (n c) -> p n c", c=CT)).then_inc(stored, 16)
                for n, (a, b) in enumerate(PIECES):
                    for k, made in enumerate((wh_made, wl_made)):
                        sp.wait_ge(made, n + 1)
                        sp.dma_start(wpair[k, :, a:b], Wp[k][:, a:b]).then_inc(w_stored, 16)
                sp.wait_ge(stored, 64)
                sp.wait_ge(w_stored, 32 * len(PIECES))

            @block.scalar
            def _(act):
                for n, (a, b) in enumerate(PIECES):
                    act.wait_ge(w_loaded[n], 16)
                    act.activation(Wp[0][:, a:b], W[:, a:b], ACT.Copy, scale=WS).then_inc(wh_made, 1)

            @block.vector
            def _(dve):
                dve.wait_ge(loaded, 32)
                dve.tensor_tensor(E[:, 0, :], E[:, 0, :], Dk[:, :], ALU.add).then_inc(added, 1)
                dve.wait_ge(added, 1)
                dve.tensor_scalar(H[0][:, :, :], E[:, :, :], WS, None, ALU.mult).then_inc(hi_made, 1)
                dve.wait_ge(hi_made, 1)
                flat = lambda t: t[:, :, :].rearrange("p a c -> p (a c)")
                dve.scalar_tensor_tensor(flat(H[1]), flat(E), WS, flat(H[0]), ALU.mult, ALU.subtract).then_inc(lo_made, 1)
                for n, (a, b) in enumerate(PIECES):
                    dve.wait_ge(wh_made, n + 1)
                    dve.wait_ge(w_loaded[n], 16)
                    dve.scalar_tensor_tensor(Wp[1][:, a:b], W[:, a:b], WS, Wp[0][:, a:b], ALU.mult, ALU.subtract)\
                       .then_inc(wl_made, 1)


def hyena(nc, X, w, taps, wpair, idf, flip):
    with ExitStack() as ctx:
        sb = lambda n, s, d=F32: ctx.enter_context(nc.sbuf_tensor(f"hy_{n}", s, d))
        sem = lambda n: nc.alloc_semaphore(f"hy_{n}")
        bank = [ctx.enter_context(nc.psum_tensor(f"hy_bank{k}", [P, GT], F32)) for k in range(8)]
        T = B * P
        xflat = X[:, :, :].rearrange("p b n -> p (b n)").bitcast(F16)
        XT = [xflat[:, k * DC * T:(k + 1) * DC * T] for k in range(2)]
        XT = [x.rearrange("p (c t) -> p c t", c=DC) for x in XT]
        Y = sb("Y", [P, DC, T])
        cst = sb("cst", [P, DC, 11])
        with ExitStack() as ctx1:
            sb1 = lambda n, s, d=F32: ctx1.enter_context(nc.sbuf_tensor(f"hy_{n}", s, d))
            Wq = [sb1("Wh", [P, DC, 3, P], F16), sb1("Wl", [P, DC, 3, P], F16)]
            pad = sb1("pad", [P, 2, GS, P + 2])
            K = sb1("K", [P, GT])
            Vv = sb1("Vv", [P, GT])
            KVh, KVl = sb1("KVh", [P, 2, P, B], F16), sb1("KVl", [P, 2, P, B], F16)
            NQ = 2
            TP = sb1("TP", [P, NQ, 2, P, CT], F16)
            C = sb1("C", [P, B, P])
            stage = C[:, :, :].rearrange("p b n -> p (b n)").rearrange("p (h c t) -> p h c t", h=2, c=DC)
            xT = w["xT"].rearrange("p (c t) -> p c t", c=DC)
            xT_loaded, xh_ready, xl_ready = [sem(f"xT_loaded{h}") for h in range(2)], sem("xh_ready"), sem("xl_ready")
            loaded, w_loaded, zeros_set = sem("loaded"), sem("w_loaded"), sem("zeros_set")
            waits_apart = sem("waits_apart")
            qkv_psum, qk_padded, v_ready = sem("qkv_psum"), sem("qk_padded"), sem("v_ready")
            q_tap, k_tap, kv_ready = sem("q_tap"), sem("k_tap"), sem("kv_ready")
            kvT_psum, kvh_ready, kvl_ready = sem("kvT_psum"), sem("kvh_ready"), sem("kvl_ready")
            t_loaded = [sem(f"t_loaded{u}") for u in range(NQ)]
            c_psum, c_ready, cT_psum, gated = sem("c_psum"), sem("c_ready"), sem("cT_psum"), sem("gated")
            cs = lambda cc, n: cst[:, cc, n:n + 1]

            with nc.Block() as block:
                HALF = NG // 2

                def half(eng, part):
                    if eng is nc.tensor:
                        for i in range(HALF):
                            part(i)
                    else:
                        part(0)
                        with eng.Fori(0, HALF - 1) as i:
                            part(i + 1)

                def groups(eng, cc, work, convolve, gate):
                    if cc == 0:
                        work(0, lambda: None)
                        work(1, lambda: None)
                        with eng.Fori(0, NG // 2 - 2) as i:
                            for u in range(2):
                                work(i * 2 + (2 + u), lambda: None, u)
                        work(NG - 2, lambda: None)
                        work(NG - 1, lambda: None)
                    else:
                        half(eng, lambda i: work(i, lambda: [convolve(cc - 1, i, u) for u in range(NQ)]))
                        half(eng, lambda i: work(i + HALF, lambda: [gate(cc - 1, i, u) for u in range(2)]))

                def group_before(cc, i):
                    if type(i) is int and i == 0:
                        return (cc - 1, NG - 1) if cc else None
                    return cc, i - 1

                def x_ahead(i, u, split):
                    if type(i) is not int:
                        split(i + 2, u)
                    elif i + 2 < NG:
                        split(i + 2, i % 2)

                def last_chunk(eng, convolve, gate):
                    half(eng, lambda i: [convolve(DC - 1, i, u) for u in range(NQ)])
                    half(eng, lambda i: [gate(DC - 1, i, u) for u in range(2)])

                @block.sync
                def _(sp):

                    def load_w(cc):
                        for k in range(2):
                            sp.dma_start(Wq[k][:, :, :, :].rearrange("p c m n -> p (c m n)"),
                                         wpair[k, :, cc * WQ:(cc + 1) * WQ]).then_inc(w_loaded, 16)

                    def load_t(cc, i, u):
                        for k in range(2):
                            src = bass.AP(tensor=taps.tensor, offset=taps.offset + ((k * DC + cc) * NCT + NQ * i + u) * (LC * CT),
                                          ap=[[CT, P], [1, P * CT]])
                            sp.dma_start(TP[:, u, k, :, :].rearrange("p t c -> p (t c)"), src).then_inc(t_loaded[u], 16)

                    sp.dma_start(cst[:, :, :].rearrange("p a n -> p (a n)"), w["cst"]).then_inc(loaded, 16)
                    load_w(0)

                    def load_x(i, h):
                        sp.dma_start(stage[:, h, :, :], xT[:, :, ds(i * GT, GT)]).then_inc(xT_loaded[h], 16)

                    load_x(0, 0)
                    load_x(1, 1)
                    for u in range(NQ):
                        load_t(0, 0, u)
                    with sp.Fori(0, NG // 2 - 1) as i:
                        for h in range(2):
                            sp.wait_ge(xl_ready, 2 * i + h + 1)
                            load_x(i * 2 + (2 + h), h)
                    for cc in range(DC):
                        if cc + 1 < DC:
                            sp.wait_ge(qkv_psum, 3 * NG * (cc + 1))
                            load_w(cc + 1)
                        with sp.Fori(0, NCT // NQ - 1) as i:
                            for u in range(NQ):
                                sp.wait_ge(c_psum, NCT * cc + NQ * i + u + 1)
                                load_t(cc, i + 1, u)
                        if cc + 1 < DC:
                            for u in range(NQ):
                                sp.wait_ge(c_psum, NCT * (cc + 1) - NQ + u + 1)
                                load_t(cc + 1, 0, u)

                @block.tensor
                def _(pe):

                    def convolve(cc, i, u):
                        q = NQ * i + u
                        if q == 0:
                            pe.wait_ge(kvl_ready, NG * (cc + 1))
                        pe.wait_ge(t_loaded[u], (NCT // NQ * cc + i + 1) * 32)
                        if cc or q >= 2:
                            pe.wait_ge(c_ready, NCT * cc + q - 1)
                        for c in range(CT):
                            out = bank[4 + u % 2][:, c * B:(c + 1) * B]
                            h, l = (kv[:, cc % 2, q * CT + c, :] for kv in (KVh, KVl))
                            pe.matmul(out, TP[:, u, 0, :, c], h, start=True, stop=False)
                            pe.matmul(out, TP[:, u, 1, :, c], h, start=False, stop=False)
                            t = pe.matmul(out, TP[:, u, 0, :, c], l, start=False, stop=True)
                        t.then_inc(c_psum, 1)

                    def turn_kv(n):
                        pe.wait_ge(kv_ready, n + 1)
                        pe.wait_ge(kvl_ready, n)
                        for j in range(GS):
                            t = pe.transpose(bank[3][:, j * P:(j + 1) * P], K[:, j * P:(j + 1) * P], idf[:, :])
                        t.then_inc(kvT_psum, 1)

                    def turn_back(cc, i, u):
                        g = 2 * i + u
                        pe.wait_ge(c_ready, NCT * cc + NCT)
                        if cc or g >= 2:
                            pe.wait_ge(gated, NG * cc + g - 1)
                        for j in range(GS):
                            t = pe.transpose(bank[6 + u][:, j * P:(j + 1) * P], C[:, GS * g + j, :], flip[:, :])
                        t.then_inc(cT_psum, 1)

                    for cc in range(DC):
                        wait_apart(pe, waits_apart, w_loaded, 32 * cc + 32)

                        def work(i, beside, u=None):
                            n = cc * NG + i
                            if cc == 0:
                                wait_apart(pe, waits_apart, xh_ready, i + 1)
                                wait_apart(pe, waits_apart, xl_ready, i + 1)
                            for m in range(3):
                                pe.wait_ge(v_ready, n) if m == 2 else pe.wait_ge(qk_padded, 2 * n)
                                k = 0
                                for c in range(DC):
                                    for ww, x in ((Wq[0], XT[0]), (Wq[0], XT[1]), (Wq[1], XT[0])):
                                        t = pe.matmul(bank[m][:, :], ww[:, c, m, :], x[:, c, ds(i * GT, GT)], start=(k == 0),
                                                      stop=(k == 3 * DC - 1))
                                        k += 1
                                t.then_inc(qkv_psum, 1)
                                if m == 0 and group_before(cc, i):
                                    turn_kv(n - 1)
                            beside()

                        groups(pe, cc, work, convolve, turn_back)
                    turn_kv(DC * NG - 1)
                    last_chunk(pe, convolve, turn_back)

                @block.scalar
                def _(act):

                    def c_out(cc, i, u):
                        q = NQ * i + u
                        act.wait_ge(c_psum, NCT * cc + q + 1)
                        act.wait_ge(cT_psum, NG * cc)
                        act.activation(C[:, :, ds(q * CT, CT)].rearrange("p b c -> p c b"),
                                       bank[4 + u % 2][:, 0:CT * B].rearrange("p (c b) -> p c b", c=CT), ACT.Copy,
                                       scale=1.0 / WS).then_inc(c_ready, 1)

                    def x_hi(i, h):
                        act.wait_ge(xT_loaded[h], (i - h) * 8 + 16)
                        act.activation(XT[0][:, :, ds(i * GT, GT)], stage[:, h, :, :], ACT.Copy).then_inc(xh_ready, 1)

                    def kv_hi(cc, i):
                        act.wait_ge(kvT_psum, NG * cc + i + 1)
                        if cc >= 2:
                            act.wait_ge(c_psum, NCT * (cc - 1))
                        act.activation(KVh[:, cc % 2, :, ds(i * GS, GS)].rearrange("p c j -> p j c"),
                                       bank[3][:, :].rearrange("p (j c) -> p j c", j=GS), ACT.Copy).then_inc(kvh_ready, 1)

                    act.wait_ge(loaded, 16)
                    act.wait_ge(zeros_set, 1)
                    x_hi(0, 0)
                    x_hi(1, 1)
                    for cc in range(DC):

                        def work(i, beside, u=None):
                            n = cc * NG + i
                            for m, taken in enumerate((q_tap, k_tap)):
                                act.wait_ge(qkv_psum, 3 * n + m + 1)
                                act.wait_ge(taken, 3 * n)
                                act.activation(pad[:, m, :, 2:P + 2], bank[m][:, :].rearrange("p (j t) -> p j t", j=GS),
                                               ACT.Identity, bias=cs(cc, m), scale=1.0 / WS).then_inc(qk_padded, 1)
                                if m == 0 and group_before(cc, i):
                                    kv_hi(*group_before(cc, i))
                            act.wait_ge(qkv_psum, 3 * n + 3)
                            act.wait_ge(kv_ready, n)
                            act.activation(Vv[:, :], bank[2][:, :], ACT.Identity, bias=cs(cc, 2), scale=1.0 / WS)\
                               .then_inc(v_ready, 1)
                            beside()
                            if cc == 0:
                                x_ahead(i, u, x_hi)

                        groups(act, cc, work, c_out, lambda cc, i, u: None)
                    kv_hi(DC - 1, NG - 1)
                    with act.Fori(0, HALF) as i:
                        for u in range(NQ):
                            c_out(DC - 1, i, u)

                @block.vector
                def _(dve):

                    def gate(cc, i, u):
                        g = 2 * i + u
                        dve.wait_ge(cT_psum, NG * cc + g + 1)
                        y = Y[:, cc, ds(g * GT, GT)]
                        dve.tensor_tensor(y, bank[6 + u][:, :], y, ALU.mult).then_inc(gated, 1)

                    def x_lo(i, h):
                        dve.wait_ge(xh_ready, i + 1)
                        dve.wait_ge(xT_loaded[h], (i - h) * 8 + 16)
                        dve.tensor_tensor(XT[1][:, :, ds(i * GT, GT)], stage[:, h, :, :], XT[0][:, :, ds(i * GT, GT)], ALU.subtract)\
                           .then_inc(xl_ready, 1)

                    def kv_lo(cc, i):
                        n = NG * cc + i
                        dve.wait_ge(kvT_psum, n + 1)
                        dve.wait_ge(kvh_ready, n + 1)
                        b4 = ds(i * GS, GS)
                        dve.tensor_tensor(KVl[:, cc % 2, :, b4].rearrange("p c j -> p j c"),
                                          bank[3][:, :].rearrange("p (j c) -> p j c", j=GS),
                                          KVh[:, cc % 2, :, b4].rearrange("p c j -> p j c"), ALU.subtract).then_inc(kvl_ready, 1)

                    dve.memset(pad[:, :, :, 0:2], 0.0).then_inc(zeros_set, 1)
                    dve.wait_ge(loaded, 16)
                    x_lo(0, 0)
                    x_lo(1, 1)
                    for cc in range(DC):

                        def work(i, beside, u=None):
                            n = cc * NG + i
                            yq = Y[:, cc, ds(i * GT, GT)].rearrange("p (j t) -> p j t", j=GS)
                            for m, (to, taken) in enumerate(((yq, q_tap), (K[:, :].rearrange("p (j t) -> p j t", j=GS), k_tap))):
                                dve.wait_ge(qk_padded, 2 * n + m + 1)
                                if m:
                                    if group_before(cc, i):
                                        kv_lo(*group_before(cc, i))
                                    dve.wait_ge(kvT_psum, n)
                                dve.tensor_scalar(to, pad[:, m, :, 2:P + 2], cs(cc, 3 + 4 * m + 2), cs(cc, 3 + 4 * m + 3),
                                                  ALU.mult, ALU.add).then_inc(taken, 1)
                                for s in (1, 0):
                                    dve.wait_ge(taken, 3 * n + 2 - s)
                                    dve.scalar_tensor_tensor(to, pad[:, m, :, s:P + s], cs(cc, 3 + 4 * m + s), to,
                                                             ALU.mult, ALU.add).then_inc(taken, 1)
                            dve.wait_ge(k_tap, 3 * n + 3)
                            dve.wait_ge(v_ready, n + 1)
                            dve.tensor_tensor(K[:, :], K[:, :], Vv[:, :], ALU.mult).then_inc(kv_ready, 1)
                            beside()
                            if cc == 0:
                                x_ahead(i, u, x_lo)

                        groups(dve, cc, work, lambda cc, i, u: None, gate)
                    kv_lo(DC - 1, NG - 1)
                    with dve.Fori(0, HALF) as i:
                        for u in range(2):
                            gate(DC - 1, i, u)

        with ExitStack() as ctx2:
            sb2 = lambda n, s, d=F32: ctx2.enter_context(nc.sbuf_tensor(f"hy_{n}", s, d))
            Woh, Wol = sb2("Woh", [P, DC * D], F16), sb2("Wol", [P, DC * D], F16)
            bo = sb2("bo", [P, D])
            Yh, Yl = sb2("Yh", [P, 2, DC, GT], F16), sb2("Yl", [P, 2, DC, GT], F16)
            norm = Norm(nc, ctx2, "hy_norm")
            x_loaded = [sem(f"x_loaded{k}") for k in range(NG)]
            wo_loaded, bo_loaded, biased = sem("wo_loaded"), sem("bo_loaded"), sem("biased")
            yh_ready, yl_ready, o_psum = sem("yh_ready"), sem("yl_ready"), sem("o_psum")

            with nc.Block() as block:

                @block.sync
                def _(sp):
                    for k, to in enumerate((Woh, Wol)):
                        sp.dma_start(to[:, :], wpair[k, :, PIECES[DC][0]:PIECES[DC][1]]).then_inc(wo_loaded, 16)
                    sp.dma_start(bo[:, :], w["bo"].partition_broadcast(P)).then_inc(bo_loaded, 16)
                    for k in range(NG):
                        sp.dma_start(X[:, GS * k:GS * k + GS, :].rearrange("p b n -> p (b n)"),
                                     w["x"][:, GS * k * D:(GS * k + GS) * D]).then_inc(x_loaded[k], 16)

                @block.gpsimd
                def _(pool):
                    norm_consts(pool, norm)
                    pool.wait_ge(bo_loaded, 16)
                    for i in range(NG):
                        pool.wait_ge(x_loaded[i], 16)
                        for j in range(GS):
                            x = X[:, GS * i + j, :]
                            pool.tensor_tensor(x, x, bo[:, :], ALU.add).then_inc(biased, 1)
                        norm_rstd(pool, norm, i)

                @block.scalar
                def _(act):
                    for i in range(NG):
                        if i >= 2:
                            act.wait_ge(o_psum, GS * (i - 1))
                        act.activation(Yh[:, i % 2, :, :], Y[:, :, i * GT:(i + 1) * GT], ACT.Copy).then_inc(yh_ready, 1)

                @block.tensor
                def _(pe):
                    pe.wait_ge(wo_loaded, 32)
                    for i in range(NG):
                        pe.wait_ge(yh_ready, i + 1)
                        pe.wait_ge(yl_ready, i + 1)
                        for j in range(GS):
                            if i:
                                pe.wait_ge(norm.rows_ready, GS * (i - 1) + j + 1)
                            k = 0
                            for c in range(DC):
                                for y, ww in ((Yh, Woh), (Yl, Woh), (Yh, Wol)):
                                    t = pe.matmul(bank[j][:, :], y[:, i % 2, c, j * P:(j + 1) * P], ww[:, c * D:(c + 1) * D],
                                                  start=(k == 0), stop=(k == 3 * DC - 1))
                                    k += 1
                            t.then_inc(o_psum, 1)

                @block.vector
                def _(dve):

                    def split(i):
                        dve.wait_ge(yh_ready, i + 1)
                        if i >= 2:
                            dve.wait_ge(o_psum, GS * (i - 1))
                        dve.tensor_tensor(Yl[:, i % 2, :, :], Y[:, :, i * GT:(i + 1) * GT], Yh[:, i % 2, :, :], ALU.subtract)\
                           .then_inc(yl_ready, 1)

                    split(0)
                    for i in range(NG):
                        if i + 1 < NG:
                            split(i + 1)
                        for j in range(GS):
                            dve.wait_ge(o_psum, GS * i + j + 1)
                            dve.wait_ge(biased, GS * i + j + 1)
                            x = X[:, GS * i + j, :]
                            dve.scalar_tensor_tensor(x, bank[j][:, :], 1.0 / WS, x, ALU.mult, ALU.add).then_inc(norm.rows_ready, 1)
                        for j in range(GS):
                            norm_stats(dve, norm, X, i, j)
                        for j in range(GS):
                            norm_aggr(dve, norm, i, j)
                        for j in range(GS):
                            norm_apply(dve, norm, X, i, j)


def load_consts(nc, ctx, name, arrays, wanted):
    tiles = {n: ctx.enter_context(nc.sbuf_tensor(f"{name}_{n}", list(arrays[n].shape), arrays[n].dtype)) for n in wanted}
    loaded = nc.alloc_semaphore(f"{name}_tiles_loaded")
    with nc.Block() as block:

        @block.sync
        def _(sp):
            for n in wanted:
                sp.dma_start(tiles[n][:, :], arrays[n]).then_inc(loaded, 16)
            sp.wait_ge(loaded, 16 * len(wanted))

    return tiles


def decoder(nc, a, out):
    with ExitStack() as ctx:
        X = ctx.enter_context(nc.sbuf_tensor("X", [P, B, D], F32))
        taps = nc.dram_tensor("taps", [2, D // CT, LC, CT], F16, kind="Internal").ap()
        wpair = nc.dram_tensor("wpair", [2, P, PIECES[-1][1]], F16, kind="Internal").ap()
        kv = nc.dram_tensor("kv", [P, B, KVW], F16, kind="Internal").ap()

        with nc.cleanup_on_exit(), ExitStack() as stage:
            hyena_taps(nc, a["kerT"], a["dskip"], taps, a["wqkv"], a["WoT_hy"], wpair)
            c = load_consts(nc, stage, "hy", a, ("idf", "flip"))
            hyena(nc, X, a, taps, wpair, c["idf"], c["flip"])
        c = load_consts(nc, ctx, "all", a, ("idh", "idf", "nsel", "gmask", "tri", "mc"))
        idh, idf, nsel, gmask = c["idh"], c["idf"], c["nsel"], c["gmask"][:, :].rearrange("p (g t) -> p g t", g=QG)
        with nc.cleanup_on_exit():
            context(nc, a["ctx"], kv, idh)
        with ExitStack() as weights:
            raw = weights.enter_context(nc.sbuf_tensor("ffn_raw", [P, 2, DC * FF], F32))
            with nc.cleanup_on_exit():
                cross_attention(nc, "xa", X, kv, idh, nsel, gmask, prefetch=[(raw[:, 0, :], a["w0T"]), (raw[:, 1, :], a["w1T"])])
            with nc.cleanup_on_exit():
                ffn(nc, X, raw, a["bias0"], a["bias1"], idh)
        with ExitStack() as weights:
            W12h, W12l = (weights.enter_context(nc.sbuf_tensor(n, [P, NE * W12E], F16)) for n in ("W12h", "W12l"))
            with nc.cleanup_on_exit():
                latent_attention(nc, X, a, idf, (a["mw12"], W12h, W12l))
            with nc.cleanup_on_exit():
                cross_attention(nc, "xb", X, kv, idh, nsel, gmask)
            with nc.cleanup_on_exit():
                moe(nc, X, W12h, W12l, a["mw3"], a["rw"], idh, idf, c["tri"], c["mc"], out)



def _layout(np, i):
    c = np.ascontiguousarray

    def rows(w):
        n = w.shape[0] // P
        return c(w.reshape(n, P, -1).transpose(1, 0, 2).reshape(P, -1))

    def by_channel(v):
        return v.reshape(DC, P).T

    a = {}
    x = i["x"]
    a["x"] = c(x.transpose(1, 0, 2).reshape(P, -1))
    a["xT"] = rows(c(x.transpose(2, 0, 1)).reshape(D, -1))
    a["ctx"] = c(i["ctx_512"].transpose(1, 0, 2).reshape(P, -1))
    w = np.stack([i["L0_attn_Wq"].T, i["L0_attn_Wk"].T, i["L0_attn_Wv"].T], 1)
    a["wqkv"] = c(w.reshape(DC, P, 3, DC, P).transpose(1, 3, 0, 2, 4).reshape(P, -1))
    qw, kw = i["L0_attn_convq_w"], i["L0_attn_convk_w"]
    per_channel = [i["L0_attn_bq"], i["L0_attn_bk"], i["L0_attn_bv"], qw[:, 0, 0], qw[:, 0, 1], qw[:, 0, 2],
                   i["L0_attn_convq_b"], kw[:, 0, 0], kw[:, 0, 1], kw[:, 0, 2], i["L0_attn_convk_b"]]
    a["cst"] = c(np.stack([by_channel(v) for v in per_channel], 2).reshape(P, -1))
    ker = i["L0_attn_ssm_kernel"]
    a["kerT"] = rows(np.concatenate([ker[:, :P][:, ::-1], ker[:, P:LC][:, ::-1]], 1).T)
    a["dskip"] = np.zeros((P, D), x.dtype)
    a["dskip"][P - 1] = i["L0_attn_D_skip"]
    a["WoT_hy"] = rows(i["L0_attn_Wo"].T)
    a["bo"] = i["L0_attn_bo"]
    a["w0T"] = rows(i["L0_ffn_W0"].T)
    a["w1T"] = rows(i["L0_ffn_W1"].T)
    a["bias0"] = c(i["L0_ffn_bias0"].reshape(FC, P).T)
    a["bias1"] = i["L0_ffn_bias1"]
    q, kv = i["L1_attn_W_q_comp"], i["L1_attn_W_kv_comp"]

    def halves_swapped(m):
        return np.concatenate([m[DCMP // 2:], m[:DCMP // 2]], 0)

    k = kv[:DCMP]
    a["Wkv"] = i["L1_attn_W_to_kv"]
    a["WoT"] = c(i["L1_attn_W_out_res"].T)
    a["WcT"] = c(i["L1_attn_W_compress"].T)
    qs, ks = halves_swapped(q), halves_swapped(k)

    def zeros_below(m):
        return np.concatenate([m, np.zeros_like(m)], 0)

    a["Wqk"] = zeros_below(np.concatenate([q.T, qs.T, k.T, ks.T, ks.T, k.T], 1))
    a["WvT"] = zeros_below(kv[DCMP:].T)
    a["Wl"] = i["L1_attn_W_comp2lat"]
    a["gb"] = c(np.stack([i["L1_attn_ln_gamma"], i["L1_attn_ln_beta"]], 1))
    a["bout"] = i["L1_attn_b_out_res"]
    up = np.stack([i["L1_ffn_w1"], i["L1_ffn_w2"]], 2)
    a["mw12"] = c(up.reshape(NE, DC, P, 2 * FE).transpose(2, 0, 1, 3).reshape(P, -1))
    a["mw3"] = c(i["L1_ffn_w3"].reshape(NE, FE // P, P, D).transpose(2, 0, 1, 3).reshape(P, -1))
    a["rw"] = rows(i["L1_ffn_router_w"].T)
    f32, f16 = np.float32, np.float16
    a["idf"], a["idh"], a["flip"] = np.eye(P, dtype=f32), np.eye(P, dtype=f16), c(np.eye(P, dtype=f32)[:, ::-1])
    inv = (1.0 / (10000.0 ** (np.arange(0, DCMP, 2, dtype=f32) / DCMP))).astype(f32)
    angle = np.arange(P, dtype=f32)[:, None] * inv[None, :]
    cos = np.concatenate([np.cos(angle), np.cos(angle)], 1).T
    sin = np.concatenate([-np.sin(angle), np.sin(angle)], 1).T
    cos, sin = np.tile(cos, (1, GS)), np.tile(sin, (1, GS))
    a["rope"] = np.concatenate([np.concatenate([cos, sin], 1), np.concatenate([sin, cos], 1)], 0).astype(f32)
    a["mask"] = np.where(np.tril(np.ones((P, P), bool)), 0, -1e30).astype(f32)
    nsel, gmask = np.zeros((QH, KH, P), f16), np.zeros((QH, QG, P), f16)
    for h in range(QH):
        nsel[h, h // QG] = -1
        gmask[h, ORDER.index(h % QG)] = 1
    a["nsel"], a["gmask"] = nsel.reshape(QH, -1), gmask.reshape(QH, -1)
    t = np.arange(P)
    a["tri"] = np.concatenate([t[:, None] < t[None, :], np.ones((P, P), bool)], 1).astype(f16)
    e = np.arange(NE)
    row = np.concatenate([e, e * EROWS, np.arange(B) * P, (e[None, :] <= e[:, None]).reshape(-1), np.arange(NTILE)])
    a["mc"] = np.concatenate([np.tile(row, (P, 1)), t[:, None]], 1).astype(f32)
    return a


def kernel(**inputs):
    import numpy as np
    import concourse.bacc as bacc
    from concourse.bass_utils import run_bass_kernel_spmd

    nc = bacc.Bacc("TRN2", target_bir_lowering=False, num_devices=1)
    arrays = _layout(np, {n: np.asarray(v) for n, v in inputs.items()})
    aps = {n: nc.dram_tensor(f"in_{n}", v.shape, mybir.dt.from_np(v.dtype), kind="ExternalInput").ap()
           for n, v in arrays.items()}
    out = nc.dram_tensor("out_0", (P, B * D), F32, kind="ExternalOutput").ap()
    decoder(nc, aps, out)
    r = run_bass_kernel_spmd(nc, [{f"in_{n}": v for n, v in arrays.items()}], core_ids=[0])
    y = r.results[0]["out_0"]
    return np.ascontiguousarray(y.reshape(P, B, D).transpose(1, 0, 2))
```

```python
from contextlib import ExitStack

import concourse.bass as bass
from concourse import mybir

F32 = mybir.dt.float32
F16 = mybir.dt.float16
U32 = mybir.dt.uint32
ALU = mybir.AluOpType
ACT = mybir.ActivationFunctionType
AX = mybir.AxisListType

P = 128
B = 32
D = 512
DC = D // P
GS = 4
GT = GS * P
NG = B // GS
FF = 2048
FC = FF // P
NE = 8
FE = 256
WS = 256.0
EPS = 1e-5
ds = bass.ds


def tile(X, i):
    return X[:, ds(i, 1), :].rearrange("p a n -> p (a n)")


def group(X, i, n=GS):
    return X[:, ds(i, n), :]


class Norm:

    def __init__(self, nc, ctx, name, n=GS):
        self.n = n
        self.stats = ctx.enter_context(nc.sbuf_tensor(f"{name}_stats", [P, n, 6], F32))
        self.mv = ctx.enter_context(nc.sbuf_tensor(f"{name}_mv", [P, n, 2], F32))
        self.rstd = ctx.enter_context(nc.sbuf_tensor(f"{name}_rstd", [P, n], F32))
        self.consts = ctx.enter_context(nc.sbuf_tensor(f"{name}_consts", [P, 2 * n], F32))
        s = lambda n: nc.alloc_semaphore(f"{name}_{n}")
        self.rows_ready = s("rows_ready")
        self.stats_ready = s("stats_ready")
        self.mv_ready = s("mv_ready")
        self.var_eps = s("var_eps")
        self.rstd_ready = s("rstd_ready")
        self.normed = s("normed")
        self.consts_set = s("consts_set")
        self.waits_apart = s("waits_apart")


def norm_consts(pool, n):
    pool.memset(n.consts[:, 0:n.n], EPS).then_inc(n.consts_set, 1)
    pool.memset(n.consts[:, n.n:2 * n.n], -0.5).then_inc(n.consts_set, 1)


def norm_rstd(pool, n, i):
    pool.wait_ge(n.consts_set, 2)
    pool.wait_ge(n.mv_ready, n.n * i + n.n)
    pool.tensor_tensor(n.rstd[:, :], n.mv[:, :, 1], n.consts[:, 0:n.n], ALU.add).then_inc(n.var_eps, 1)
    pool.wait_ge(n.var_eps, i + 1)
    pool.tensor_tensor(n.rstd[:, :], n.rstd[:, :], n.consts[:, n.n:2 * n.n], ALU.pow).then_inc(n.rstd_ready, 1)


def wait_apart(eng, apart, sem, value):
    eng.wait_ge(sem, value)
    eng.sem_inc(apart, 1)


def norm_stats(dve, n, X, i, j, at=None):
    wait_apart(dve, n.waits_apart, n.rows_ready, n.n * i + j + 1)
    dve.bn_stats(n.stats[:, j, :], tile(X, n.n * i + j if at is None else at)).then_inc(n.stats_ready, 1)


def norm_aggr(dve, n, i, j):
    wait_apart(dve, n.waits_apart, n.stats_ready, n.n * i + j + 1)
    dve.bn_aggr(n.mv[:, j, :], n.stats[:, j, :]).then_inc(n.mv_ready, 1)


def norm_apply(dve, n, X, i, j, at=None):
    dve.wait_ge(n.rstd_ready, i + 1)
    x = tile(X, n.n * i + j if at is None else at)
    dve.tensor_scalar(x, x, n.mv[:, j, 0:1], n.rstd[:, j:j + 1], ALU.subtract, ALU.mult).then_inc(n.normed, 1)


def ffn(nc, X, raw, bias0, bias1, idh):
    with ExitStack() as ctx:
        sb = lambda n, s, d=F32: ctx.enter_context(nc.sbuf_tensor(f"ffn_{n}", s, d))
        ps = lambda n, s, d=F32: ctx.enter_context(nc.psum_tensor(f"ffn_{n}", s, d))
        sem = lambda n: nc.alloc_semaphore(f"ffn_{n}")
        W0h, W0l = sb("W0h", [P, FC, DC * P], F16), sb("W0l", [P, FC, DC * P], F16)
        W1h, W1l = sb("W1h", [P, FC, D], F16), sb("W1l", [P, FC, D], F16)
        flat = lambda t: t[:, :, :].rearrange("p a n -> p (a n)")
        X16 = sb("X16", [P, GS, D], F16)
        XT = sb("XT", [P, DC, GT], F16)
        DT = raw[:, 0, :].bitcast(F16)[:, 0:FC * GT].rearrange("p (n t) -> p n t", n=FC)
        E16 = raw[:, 1, :].bitcast(F16)[:, 0:GS * D].rearrange("p (j n) -> p j n", j=GS)
        b0 = sb("b0", [P, FC])
        b1 = sb("b1", [P, D])
        psT = [ps(f"psT{k}", [P, GT], F16) for k in range(2)]
        psD = [ps(f"psD{k}", [P, GT]) for k in range(2)]
        psE = [ps(f"psE{k}", [P, D]) for k in range(GS)]
        norm = Norm(nc, ctx, "ffn_norm")
        consts_loaded, wh_made, wl_made = sem("consts_loaded"), sem("wh_made"), sem("wl_made")
        NQ = 4
        QW = FF * DC // NQ
        pieces = [(raw[:, k, a:a + QW], flat(h)[:, a:a + QW], flat(l)[:, a:a + QW])
                  for k, (h, l) in enumerate(((W0h, W0l), (W1h, W1l))) for a in range(0, NQ * QW, QW)]
        x16_ready, xT_psum, xT_ready = sem("x16_ready"), sem("xT_psum"), sem("xT_ready")
        d_psum, dT_ready, e_psum, e16_ready = sem("d_psum"), sem("dT_ready"), sem("e_psum"), sem("e16_ready")

        with nc.Block() as block:

            @block.sync
            def _(sp):
                sp.dma_start(b0[:, :], bias0).then_inc(consts_loaded, 16)
                sp.dma_start(b1[:, :], bias1.partition_broadcast(P)).then_inc(consts_loaded, 16)

            @block.gpsimd
            def _(pool):
                norm_consts(pool, norm)

                def cast(i):
                    pool.wait_ge(xT_psum, DC * i)
                    for j in range(GS):
                        pool.tensor_copy(X16[:, j, :], tile(X, GS * i + j)).then_inc(x16_ready, 1)

                with pool.Fori(0, NG - 1) as i:
                    cast(i + 1)
                    norm_rstd(pool, norm, i)
                norm_rstd(pool, norm, NG - 1)

            @block.tensor
            def _(pe):

                def turn_x(i):
                    pe.wait_ge(x16_ready, GS * i + GS)
                    for c in range(DC):
                        pe.wait_ge(xT_ready, DC * i + max(0, c - 1))
                        for j in range(GS):
                            t = pe.transpose(psT[c % 2][:, j * P:(j + 1) * P], X16[:, j, c * P:(c + 1) * P], idh[:, :])
                        t.then_inc(xT_psum, 1)

                def up(i):
                    pe.wait_ge(xT_ready, DC * i + DC)
                    for n in range(FC):
                        if n % (FC // NQ) == 0:
                            pe.wait_ge(wl_made, n // (FC // NQ) + 1)
                        pe.wait_ge(dT_ready, FC * i + max(0, n - 1))
                        for c in range(DC):
                            for w in (W0h, W0l):
                                t = pe.matmul(psD[n % 2][:, :], w[:, n, c * P:(c + 1) * P], XT[:, c, :],
                                              start=(c == 0 and w is W0h), stop=(c == DC - 1 and w is W0l))
                        t.then_inc(d_psum, 1)

                def down(i):
                    pe.wait_ge(dT_ready, FC * i + FC)
                    pe.wait_ge(wl_made, 2 * NQ)
                    pe.wait_ge(e16_ready, GS * i)
                    for j in range(GS):
                        for n in range(FC):
                            for w in (W1h, W1l):
                                t = pe.matmul(psE[j][:, :], DT[:, n, j * P:(j + 1) * P], w[:, n, :],
                                              start=(n == 0 and w is W1h), stop=(n == FC - 1 and w is W1l))
                        t.then_inc(e_psum, 1)

                turn_x(0)
                with pe.Fori(0, NG - 1) as i:
                    up(i)
                    turn_x(i + 1)
                    down(i)
                up(NG - 1)
                down(NG - 1)

            @block.scalar
            def _(act):
                def hi(k):
                    w, h, _ = pieces[k]
                    act.activation(h, w, ACT.Copy, scale=WS).then_inc(wh_made, 1)

                def gelu(i, between):
                    act.wait_ge(e_psum, GS * i)
                    for n in range(FC):
                        act.wait_ge(d_psum, FC * i + n + 1)
                        if between:
                            act.wait_ge(wl_made, n * NQ // (2 * FC) + 1)
                        act.activation(DT[:, n, :], psD[n % 2][:, :], ACT.Gelu, bias=b0[:, n:n + 1],
                                       scale=1.0 / WS).then_inc(dT_ready, 1)
                        if n in between:
                            hi(between[n])

                for k in range(NQ):
                    hi(k)
                act.wait_ge(consts_loaded, 32)
                gelu(0, {1: NQ, 4: NQ + 1, 7: NQ + 2, 10: NQ + 3})
                with act.Fori(0, NG - 1) as i:
                    gelu(i + 1, {})

            @block.vector
            def _(dve):

                def x_out(i):
                    for c in range(DC):
                        dve.wait_ge(xT_psum, DC * i + c + 1)
                        if c == 0:
                            dve.wait_ge(d_psum, FC * i)
                        dve.tensor_copy(XT[:, c, :], psT[c % 2][:, :]).then_inc(xT_ready, 1)

                def add(i):
                    for j in range(GS):
                        dve.wait_ge(e_psum, GS * i + j + 1)
                        dve.scalar_tensor_tensor(E16[:, j, :], psE[j][:, :], 1.0 / WS, b1[:, :], ALU.mult, ALU.add)\
                           .then_inc(e16_ready, 1)
                        dve.wait_ge(e16_ready, GS * i + j + 1)
                        x = tile(X, GS * i + j)
                        dve.tensor_tensor(x, x, E16[:, j, :], ALU.add).then_inc(norm.rows_ready, 1)
                        norm_stats(dve, norm, X, i, j)
                        norm_aggr(dve, norm, i, j)
                    for j in range(GS):
                        norm_apply(dve, norm, X, i, j)

                for j in range(GS):
                    dve.tensor_copy(X16[:, j, :], tile(X, j)).then_inc(x16_ready, 1)
                x_out(0)
                for n, (w, h, l) in enumerate(pieces):
                    dve.wait_ge(wh_made, n + 1)
                    dve.scalar_tensor_tensor(l, w, WS, h, ALU.mult, ALU.subtract).then_inc(wl_made, 1)
                dve.wait_ge(consts_loaded, 32)
                dve.wait_ge(wl_made, 2 * NQ)
                with dve.Fori(0, NG - 1) as i:
                    x_out(i + 1)
                    add(i)
                add(NG - 1)


NR = 2
TT = 4
EROWS = B * P + P
NTILE = B * NR + NE
ETILE = EROWS // P
ZTILE = 3 * P
EMPTY = NE + NTILE
W12E = DC * 2 * FE
W3E = FE // P * D
MC_IOTA = 0
MC_ZONE = MC_IOTA + NE
MC_FULL = MC_ZONE + NE
MC_UPTO = MC_FULL + B
MC_TILE = MC_UPTO + NE * NE
MC_P = MC_TILE + NTILE
MC_P2 = MC_P + 1
MC_W = MC_P2 + 1


def moe(nc, X, W12h, W12l, w3, rw, idh, idf, tri, mc, empty, out):
    xs = nc.dram_tensor("moe_xs", [B * P, 2 * D], F16, kind="Internal").ap()
    inv = nc.dram_tensor("moe_inv", [ZTILE * P, 1], F32, kind="Internal").ap()
    ys = nc.dram_tensor("moe_ys", [NR * B * P + EMPTY * P, D], F32, kind="Internal").ap()
    with ExitStack() as ctx:
        sb = lambda n, s, d=F32: ctx.enter_context(nc.sbuf_tensor(f"moe_{n}", s, d))
        gap = sb("gap", [P, B])
        tokens = sb("tokens", [P, ZTILE], U32)
        targets = sb("targets", [P, ZTILE], U32)
        zone_tile = sb("zone_tile", [P, NTILE], U32)
        expert_at = sb("expert_at", [P, NTILE], U32)
        with ExitStack() as weights:
            wsb = lambda n, s, d=F16: weights.enter_context(nc.sbuf_tensor(f"moe_{n}", s, d))
            W3h, W3l = wsb("W3h", [P, NE * W3E]), wsb("W3l", [P, NE * W3E])
            RWh, RWl = wsb("RWh", [P, DC * NE]), wsb("RWl", [P, DC * NE])
            moe_route(nc, X, rw, RWh, RWl, idh, idf, tri, mc, empty, xs, inv, gap, tokens, targets, zone_tile, expert_at,
                      (w3, W3h, W3l))
            moe_experts(nc, W12h, W12l, W3h, W3l, idh, xs, ys, tokens, targets, zone_tile, expert_at)
        moe_combine(nc, X, ys, gap, out)


def moe_route(nc, X, rw, RWh, RWl, idh, idf, tri, mc, empty, xs, inv, gap, tokens, targets, zone_tile, expert_at, down):
    with ExitStack() as ctx:
        sb = lambda n, s, d=F32: ctx.enter_context(nc.sbuf_tensor(f"route_{n}", s, d))
        ps = lambda n, s, d=F32: ctx.enter_context(nc.psum_tensor(f"route_{n}", s, d))
        sem = lambda n: nc.alloc_semaphore(f"route_{n}")
        R = sb("R", [P, 2, TT, 2 * D], F16)
        XT = sb("XT", [P, TT, 2 * D], F16)
        entry = sb("entry", [P, 2, NR, TT])
        I = sb("I", [P, TT, NR])
        second = sb("second", [P, ZTILE])
        lst = sb("list", [P, 3, P])
        L = sb("L", [P, TT, NE])
        V8 = sb("V8", [P, TT, 8])
        I8 = sb("I8", [P, TT, 8], U32)
        pick = sb("pick", [P, TT, NR, NE])
        both = sb("both", [P, TT, NE], F16)
        next_row = sb("next_row", [P, NE])
        row = sb("row", [P, TT, NE])
        prow = sb("prow", [P, TT, NR, NE])
        rowf = sb("rowf", [P, TT * NR])
        J = sb("J", [P, 2, TT * NR], U32)
        n_of = sb("n_of", [P, NE])
        room = XT[:, :, :].rearrange("p j n -> p (j n)").bitcast(F32)
        full = room[:, 0:NE * B].rearrange("p (e k) -> p e k", e=NE)
        tiles = sb("tiles", [P, NE])
        upto = sb("upto", [P, NE, NE])
        end = sb("end", [P, NE])
        past = room[:, 0:NTILE * NE].rearrange("p (t e) -> p t e", e=NE)
        et, before, base = sb("et", [P, NTILE]), sb("before", [P, NTILE]), sb("base", [P, NTILE])
        down_dram, down_hi, down_lo = down
        DW = NE * W3E // (B // TT)
        Dn = sb("Dn", [P, 2, DW])
        d_loaded, dh_made, dl_made = [sem(f"d_loaded{h}") for h in range(2)], sem("dh_made"), sem("dl_made")
        T = [ps(f"T{k}", [P, D]) for k in range(4)]
        T16 = [t[:, :].bitcast(F16) for t in T]
        M = [ps(f"M{k}", [P, TT * NE]) for k in range(2)]
        C = [ps(f"C{k}", [P, (TT + 1) * NE]) for k in range(2)]
        hi_ready, lo_ready, xT_psum, xT_ready = sem("hi_ready"), sem("lo_ready"), sem("xT_psum"), sem("xT_ready")
        logits_psum, logits_ready, best_ready = sem("logits_psum"), sem("logits_ready"), sem("best_ready")
        gap_ready, index_ready, indexf_ready = sem("gap_ready"), sem("index_ready"), sem("indexf_ready")
        pick_ready, both_ready, counts_psum, row_ready = (sem("pick_ready"), sem("both_ready"), sem("counts_psum"),
                                                          sem("row_ready"))
        next_ready, prow_ready, rowf_ready, rows_ready = (sem("next_ready"), sem("prow_ready"), sem("rowf_ready"),
                                                          sem("rows_ready"))
        first_set, zone_emptied, apart = sem("first_set"), sem("zone_emptied"), sem("apart")
        table, rw_hi_made, rw_lo_made = sem("table"), sem("rw_hi_made"), sem("rw_lo_made")
        entry_ready, list_loaded, list_psum = sem("entry_ready"), sem("list_loaded"), sem("list_psum")
        targets_ready = sem("targets_ready")
        scattered, xs_stored = [sem(f"scattered{k}") for k in range(2)], [sem(f"xs_stored{k}") for k in range(2)]
        NI = B // (2 * TT)
        cols = lambda k, n: mc[:, k:k + n]

        with nc.Block() as block:

            @block.gpsimd
            def _(pool):
                pool.wait_ge(zone_emptied, 16)
                with pool.Fori(0, NI) as i:
                    for h in range(2):
                        wait_apart(pool, apart, entry_ready, NR * (2 * i + h) + NR)
                        wait_apart(pool, apart, rows_ready, 2 * i + h + 1)
                        for j in range(TT):
                            for r in range(NR):
                                pool.indirect_dma_start(inv, bass.IndirectOffsetOnAxis(ap=J[:, h, NR * j + r:NR * j + r + 1], axis=0),
                                                        entry[:, h, r, j:j + 1], None).then_inc(scattered[h], 16)

            @block.sync
            def _(sp):
                sp.dma_start(inv.rearrange("(p n) o -> p (n o)", p=P), empty[:, :]).then_inc(zone_emptied, 16)

                def load_down(g, h):
                    sp.dma_start(Dn[:, h, :], down_dram[:, ds(g * DW, DW)]).then_inc(d_loaded[h], 16)

                def store_x(i, h):
                    sp.wait_ge(hi_ready, TT * (2 * i + h) + TT)
                    sp.wait_ge(lo_ready, TT * (2 * i + h) + TT)
                    sp.dma_start(xs[ds((8 * i + 4 * h) * P, TT * P), :].rearrange("(j p) n -> p j n", p=P), R[:, h, :, :])\
                      .then_inc(xs_stored[h], 16)

                for h in range(2):
                    load_down(h, h)
                with sp.Fori(0, NI - 1) as i:
                    for h in range(2):
                        store_x(i, h)
                        sp.wait_ge(dl_made, 2 * i + h + 1)
                        load_down(2 * i + (h + 2), h)
                for h in range(2):
                    store_x(NI - 1, h)
                for h in range(2):
                    sp.wait_ge(scattered[h], 16 * TT * NR * NI)
                sp.dma_start(lst[:, :, :], inv.rearrange("(k q p) o -> q k (p o)", k=3, p=P)).then_inc(list_loaded, 16)
                for h in range(2):
                    sp.wait_ge(xs_stored[h], 16 * NI)

            @block.scalar
            def _(act):
                act.activation(RWh[:, :], rw, ACT.Copy, scale=WS).then_inc(rw_hi_made, 1)
                with act.Fori(0, NI) as i:
                    for h in range(2):
                        act.wait_ge(xs_stored[h], 16 * i)
                        act.wait_ge(xT_psum, TT * (2 * i + h))
                        for j in range(TT):
                            act.activation(R[:, h, j, 0:D], tile(X, 8 * i + TT * h + j), ACT.Copy).then_inc(hi_ready, 1)
                        act.wait_ge(logits_psum, 2 * i + h)
                        for j in range(TT):
                            act.wait_ge(xT_psum, TT * (2 * i + h) + j + 1)
                            act.activation(XT[:, j, :], T16[j], ACT.Copy).then_inc(xT_ready, 1)
                        act.wait_ge(d_loaded[h], 16 * i + 16)
                        act.activation(down_hi[:, ds((2 * i + h) * DW, DW)], Dn[:, h, :], ACT.Copy, scale=WS).then_inc(dh_made, 1)
                act.wait_ge(list_psum, 1)
                act.activation(targets[:, :], T[0][:, 0:ZTILE], ACT.Copy).then_inc(targets_ready, 1)

            @block.tensor
            def _(pe):

                def turn(g, h):
                    for j in range(TT):
                        pe.wait_ge(hi_ready, TT * g + j + 1)
                        pe.wait_ge(xT_ready, TT * g)
                        for c in range(DC):
                            pe.transpose(T16[j][:, c * P:(c + 1) * P], R[:, h, j, c * P:(c + 1) * P], idh[:, :])
                        pe.wait_ge(lo_ready, TT * g + j + 1)
                        for c in range(DC, 2 * DC):
                            t = pe.transpose(T16[j][:, c * P:(c + 1) * P], R[:, h, j, c * P:(c + 1) * P], idh[:, :])
                        t.then_inc(xT_psum, 1)

                def logits(g, h):
                    pe.wait_ge(logits_ready, g)
                    for j in range(TT):
                        pe.wait_ge(xT_ready, TT * g + j + 1)
                        for c in range(DC):
                            for k, (x, w) in enumerate(((c, RWh), (DC + c, RWh), (c, RWl))):
                                t = pe.matmul(M[h][:, j * NE:(j + 1) * NE], XT[:, j, x * P:(x + 1) * P],
                                              w[:, c * NE:(c + 1) * NE],
                                              start=(c == 0 and k == 0), stop=(c == DC - 1 and k == 2))
                    t.then_inc(logits_psum, 1)

                def counts(g, h):
                    pe.wait_ge(both_ready, g + 1)
                    pe.wait_ge(next_ready, g)
                    for j in range(TT + 1):
                        for b in range(min(j + 1, TT)):
                            last = b == min(j, TT - 1)
                            lhs = tri[:, 0:P] if b == j else tri[:, P:2 * P]
                            t = pe.matmul(C[h][:, j * NE:(j + 1) * NE], lhs, both[:, b, :], start=(b == 0), stop=last)
                    t.then_inc(counts_psum, 1)

                turn(0, 0)
                pe.wait_ge(rw_hi_made, 1)
                pe.wait_ge(rw_lo_made, 1)
                logits(0, 0)
                with pe.Fori(0, NI - 1) as i:
                    for h in range(2):
                        turn(2 * i + h + 1, 1 - h)
                        counts(2 * i + h, h)
                        logits(2 * i + h + 1, 1 - h)
                turn(2 * NI - 1, 1)
                counts(2 * NI - 2, 0)
                logits(2 * NI - 1, 1)
                counts(2 * NI - 1, 1)
                pe.wait_ge(list_loaded, 16)
                for k in range(3):
                    t = pe.transpose(T[0][:, k * P:(k + 1) * P], lst[:, k, :], idf[:, :])
                t.then_inc(list_psum, 1)

            @block.vector
            def _(dve):
                dve.tensor_copy(next_row[:, :], cols(MC_ZONE, NE)).then_inc(first_set, 1)
                dve.wait_ge(first_set, 1)

                def lo(g, h):
                    for j in range(TT):
                        dve.wait_ge(hi_ready, TT * g + j + 1)
                        dve.tensor_tensor(R[:, h, j, D:2 * D], tile(X, TT * g + j), R[:, h, j, 0:D], ALU.subtract)\
                           .then_inc(lo_ready, 1)

                def route(i, h):
                    g = 2 * i + h
                    dve.wait_ge(logits_psum, g + 1)
                    dve.tensor_scalar(L[:, :, :].rearrange("p j e -> p (j e)"), M[h][:, :], 1.0 / WS, None, ALU.mult)\
                       .then_inc(logits_ready, 1)
                    for j in range(TT):
                        wait_apart(dve, apart, logits_ready, g + 1)
                        dve.max(V8[:, j, :], L[:, j, :]).then_inc(best_ready, 1)
                    dve.wait_ge(best_ready, TT * g + TT)
                    dve.tensor_tensor(gap[:, ds(TT * g, TT)], V8[:, :, 0], V8[:, :, 1], ALU.subtract).then_inc(gap_ready, 1)
                    for j in range(TT):
                        dve.max_index(I8[:, j, :], V8[:, j, :], L[:, j, :]).then_inc(index_ready, 1)
                    dve.wait_ge(index_ready, TT * g + TT)
                    dve.tensor_copy(I[:, :, :], I8[:, :, 0:NR]).then_inc(indexf_ready, 1)
                    dve.wait_ge(indexf_ready, g + 1)
                    iota = cols(MC_IOTA, NE).unsqueeze(1).to_broadcast([P, TT * NR, NE])
                    index = I[:, :, :].rearrange("p j r -> p (j r)").unsqueeze(2).to_broadcast([P, TT * NR, NE])
                    dve.tensor_tensor(pick[:, :, :, :].rearrange("p j r e -> p (j r) e"), iota, index, ALU.is_equal)\
                       .then_inc(pick_ready, 1)
                    dve.wait_ge(pick_ready, g + 1)
                    dve.wait_ge(counts_psum, g)
                    dve.tensor_tensor(both[:, :, :], pick[:, :, 0, :], pick[:, :, 1, :], ALU.add).then_inc(both_ready, 1)
                    dve.wait_ge(counts_psum, g + 1)
                    c = C[h][:, 0:TT * NE].rearrange("p (j e) -> p j e", e=NE)
                    dve.tensor_tensor(row[:, :, :], c, next_row[:, :].unsqueeze(1).to_broadcast([P, TT, NE]), ALU.add)\
                       .then_inc(row_ready, 1)
                    dve.wait_ge(row_ready, g + 1)
                    dve.tensor_tensor(next_row[:, :], next_row[:, :], C[h][:, TT * NE:(TT + 1) * NE], ALU.add)\
                       .then_inc(next_ready, 1)
                    for r in range(NR):
                        dve.tensor_tensor(prow[:, :, r, :], pick[:, :, r, :], row[:, :, :], ALU.mult).then_inc(prow_ready, 1)
                    dve.wait_ge(prow_ready, NR * g + NR)
                    dve.tensor_reduce(rowf[:, :], prow[:, :, :, :].rearrange("p j r e -> p (j r) e"), AX.X, ALU.add)\
                       .then_inc(rowf_ready, 1)
                    dve.wait_ge(rowf_ready, g + 1)
                    dve.wait_ge(scattered[h], 16 * TT * NR * i)
                    dve.tensor_copy(J[:, h, :], rowf[:, :]).then_inc(rows_ready, 1)
                    for r, number in enumerate((MC_P, MC_P2)):
                        dve.tensor_scalar(entry[:, h, r, :], mc[:, ds(MC_FULL + TT * g, TT)], cols(number, 1), None, ALU.add)\
                           .then_inc(entry_ready, 1)

                def down_piece(i, h):
                    g = 2 * i + h
                    dve.wait_ge(dh_made, g + 1)
                    dve.wait_ge(d_loaded[h], 16 * i + 16)
                    at = ds(g * DW, DW)
                    dve.scalar_tensor_tensor(down_lo[:, at], Dn[:, h, :], WS, down_hi[:, at], ALU.mult, ALU.subtract)\
                       .then_inc(dl_made, 1)

                dve.wait_ge(rw_hi_made, 1)
                dve.scalar_tensor_tensor(RWl[:, :], rw, WS, RWh[:, :], ALU.mult, ALU.subtract).then_inc(rw_lo_made, 1)
                lo(0, 0)
                with dve.Fori(0, NI - 1) as i:
                    for h in range(2):
                        lo(2 * i + h + 1, 1 - h)
                        route(i, h)
                        down_piece(i, h)
                lo(2 * NI - 1, 1)
                for h in range(2):
                    route(NI - 1, h)
                    down_piece(NI - 1, h)
                dve.wait_ge(next_ready, 2 * NI)
                n = 0

                def step(t):
                    nonlocal n
                    n += 1
                    t.then_inc(table, 1)
                    dve.wait_ge(table, n)

                step(dve.tensor_tensor(n_of[:, :], next_row[:, :], cols(MC_ZONE, NE), ALU.subtract))
                step(dve.tensor_tensor(full[:, :, :], n_of[:, :].unsqueeze(2).to_broadcast([P, NE, B]),
                                       cols(MC_FULL, B).unsqueeze(1).to_broadcast([P, NE, B]), ALU.is_gt))
                step(dve.tensor_reduce(tiles[:, :], full[:, :, :], AX.X, ALU.add))
                step(dve.tensor_tensor(upto[:, :, :], cols(MC_UPTO, NE * NE).rearrange("p (e f) -> p e f", e=NE),
                                       tiles[:, :].unsqueeze(1).to_broadcast([P, NE, NE]), ALU.mult))
                step(dve.tensor_reduce(end[:, :], upto[:, :, :], AX.X, ALU.add))
                step(dve.tensor_tensor(past[:, :, :], end[:, :].unsqueeze(1).to_broadcast([P, NTILE, NE]),
                                       cols(MC_TILE, NTILE).unsqueeze(2).to_broadcast([P, NTILE, NE]), ALU.is_le))
                step(dve.tensor_reduce(et[:, :], past[:, :, :], AX.X, ALU.add))
                step(dve.tensor_tensor(past[:, :, :], past[:, :, :], tiles[:, :].unsqueeze(1).to_broadcast([P, NTILE, NE]),
                                       ALU.mult))
                step(dve.tensor_reduce(before[:, :], past[:, :, :], AX.X, ALU.add))
                step(dve.tensor_tensor(before[:, :], cols(MC_TILE, NTILE), before[:, :], ALU.subtract))
                step(dve.scalar_tensor_tensor(base[:, :], et[:, :], float(ETILE), before[:, :], ALU.mult, ALU.add))
                step(dve.tensor_copy(zone_tile[:, :], base[:, :]))
                step(dve.tensor_scalar(et[:, :], et[:, :], float(NE - 1), float(W3E), ALU.min, ALU.mult))
                step(dve.tensor_copy(expert_at[:, :], et[:, :]))
                dve.wait_ge(targets_ready, 1)
                entries = T[0][:, 0:ZTILE]
                step(dve.tensor_scalar(second[:, :], entries, float(B * P), float(-B * P), ALU.is_ge, ALU.mult))
                step(dve.tensor_tensor(second[:, :], second[:, :], entries, ALU.add))
                step(dve.tensor_scalar(second[:, :], second[:, :], float(B * P - 1), None, ALU.min))
                step(dve.tensor_copy(tokens[:, :], second[:, :]))


def moe_experts(nc, W12h, W12l, W3h, W3l, idh, xs, ys, tokens, targets, zone_tile, expert_at):
    with ExitStack() as ctx:
        sb = lambda n, s, d=F32: ctx.enter_context(nc.sbuf_tensor(f"ex_{n}", s, d))
        ps = lambda n: ctx.enter_context(nc.psum_tensor(f"ex_{n}", [P, D], F32))
        sem = lambda n: nc.alloc_semaphore(f"ex_{n}")
        K = 4
        NS = NTILE // K
        G = sb("G", [P, K, 2 * D], F16)
        J = sb("J", [P, K], U32)
        JY = sb("JY", [P, K], U32)
        XT = sb("XT", [P, 2, 2 * D], F16)
        S = sb("S", [P, 2, FE])
        H = sb("H", [P, 2, 2 * FE], F16)
        HT = sb("HT", [P, 2, 2 * FE], F16)
        Y = sb("Y", [P, K, D])
        TB = [ps(f"TB{k}") for k in range(2)]
        UB = [ps(f"UB{k}") for k in range(2)]
        HB = [ps(f"HB{k}") for k in range(2)]
        DB = [ps(f"DB{k}") for k in range(2)]
        T16 = [t[:, :].bitcast(F16) for t in TB]
        H16 = [t[:, :].bitcast(F16)[:, 0:2 * FE] for t in HB]
        gathered, written = [sem(f"gathered{k}") for k in range(K)], [sem(f"written{k}") for k in range(K)]
        j_ready, jy_ready, xT_psum, xT_ready = sem("j_ready"), sem("jy_ready"), sem("xT_psum"), sem("xT_ready")
        up_psum, silu_ready, prod_ready, hi_ready, lo_ready = (sem("up_psum"), sem("silu_ready"), sem("prod_ready"),
                                                               sem("hi_ready"), sem("lo_ready"))
        hT_psum, hT_ready, down_psum, y_ready, apart = (sem("hT_psum"), sem("hT_ready"), sem("down_psum"), sem("y_ready"),
                                                        sem("apart"))

        with nc.Block() as block:

            @block.gpsimd
            def _(pool):

                def fetch(i, k):
                    column = pool.value_load(zone_tile[0:1, ds(K * i + k, 1)], min_val=0, max_val=ZTILE - 1)
                    pool.wait_ge(gathered[k], 16 * i)
                    pool.tensor_copy(J[:, k:k + 1], tokens[:, ds(column, 1)]).then_inc(j_ready, 1)
                    wait_apart(pool, apart, j_ready, K * i + k + 1)
                    if type(i) is not int or i > 0:
                        wait_apart(pool, apart, xT_psum, K * i + k + 1 - K)
                    pool.indirect_dma_start(G[:, k, :], None, xs, bass.IndirectOffsetOnAxis(ap=J[:, k:k + 1], axis=0))\
                        .then_inc(gathered[k], 16)

                def put(i, k):
                    column = pool.value_load(zone_tile[0:1, ds(K * i + k, 1)], min_val=0, max_val=ZTILE - 1)
                    pool.wait_ge(written[k], 16 * i)
                    pool.tensor_copy(JY[:, k:k + 1], targets[:, ds(column, 1)]).then_inc(jy_ready, 1)
                    wait_apart(pool, apart, jy_ready, K * i + k + 1)
                    wait_apart(pool, apart, y_ready, K * i + k + 1)
                    pool.indirect_dma_start(ys, bass.IndirectOffsetOnAxis(ap=JY[:, k:k + 1], axis=0), Y[:, k, :], None)\
                        .then_inc(written[k], 16)

                for i in range(2):
                    for k in range(K):
                        fetch(i, k)
                with pool.Fori(0, NS - 2) as i:
                    for k in range(K):
                        fetch(i + 2, k)
                        put(i, k)
                for i in range(NS - 2, NS):
                    for k in range(K):
                        put(i, k)

            @block.sync
            def _(sp):
                for k in range(K):
                    sp.wait_ge(written[k], 16 * NS)

            @block.tensor
            def _(pe):

                def turn_x(t, i, k):
                    pe.wait_ge(gathered[k], 16 * i + 16)
                    if type(t) is not int or t >= 2:
                        pe.wait_ge(xT_ready, t - 1)
                    for c in range(2 * DC):
                        m = pe.transpose(T16[k % 2][:, c * P:(c + 1) * P], G[:, k, c * P:(c + 1) * P], idh[:, :])
                    m.then_inc(xT_psum, 1)

                def up(t, k):
                    e = pe.value_load(expert_at[0:1, ds(t, 1)], min_val=0, max_val=(NE - 1) * W3E)
                    pe.wait_ge(xT_ready, t + 1)
                    if type(t) is not int or t >= 2:
                        pe.wait_ge(prod_ready, t - 1)
                    for c in range(DC):
                        for n, (x, w) in enumerate(((c, W12h), (DC + c, W12h), (c, W12l))):
                            m = pe.matmul(UB[k % 2][:, :], XT[:, k % 2, x * P:(x + 1) * P],
                                          w[:, ds(e * (W12E // W3E) + c * 2 * FE, 2 * FE)],
                                          start=(c == 0 and n == 0), stop=(c == DC - 1 and n == 2))
                    m.then_inc(up_psum, 1)

                def turn_h(t, k):
                    pe.wait_ge(lo_ready, t + 1)
                    pe.wait_ge(hi_ready, t + 1)
                    if type(t) is not int or t >= 2:
                        pe.wait_ge(hT_ready, t - 1)
                    for c in range(4):
                        m = pe.transpose(H16[k % 2][:, c * P:(c + 1) * P], H[:, k % 2, c * P:(c + 1) * P], idh[:, :])
                    m.then_inc(hT_psum, 1)

                def down(t, k):
                    e = pe.value_load(expert_at[0:1, ds(t, 1)], min_val=0, max_val=(NE - 1) * W3E)
                    pe.wait_ge(hT_ready, t + 1)
                    if type(t) is not int or t >= 2:
                        pe.wait_ge(y_ready, t - 1)
                    for f in range(2):
                        for n, (h, w) in enumerate(((f, W3h), (2 + f, W3h), (f, W3l))):
                            m = pe.matmul(DB[k % 2][:, :], HT[:, k % 2, h * P:(h + 1) * P], w[:, ds(e + f * D, D)],
                                          start=(f == 0 and n == 0), stop=(f == 1 and n == 2))
                    m.then_inc(down_psum, 1)

                def step(i, k, first=False, last=False):
                    s = K * i + k
                    if not last:
                        turn_x(s, i, k)
                    if not (first and s < 1) and not (last and s - 1 >= NTILE):
                        up(s - 1, (k - 1) % K)
                    if not (first and s < 2) and not (last and s - 2 >= NTILE):
                        turn_h(s - 2, (k - 2) % K)
                    if not (first and s < 3):
                        down(s - 3, (k - 3) % K)

                for k in range(K):
                    step(0, k, first=True)
                with pe.Fori(0, NS - 1) as r:
                    for k in range(K):
                        step(r + 1, k)
                for k in range(3):
                    step(NS, k, last=True)

            @block.scalar
            def _(act):

                def turned_x(t, k):
                    act.wait_ge(xT_psum, t + 1)
                    if type(t) is not int or t >= 2:
                        act.wait_ge(up_psum, t - 1)
                    act.activation(XT[:, k % 2, :], T16[k % 2], ACT.Copy).then_inc(xT_ready, 1)

                def silu(t, k):
                    act.wait_ge(up_psum, t + 1)
                    if type(t) is not int or t >= 2:
                        act.wait_ge(lo_ready, t - 1)
                    act.activation(S[:, k % 2, :], UB[k % 2][:, 0:FE], ACT.Silu, scale=1.0 / WS).then_inc(silu_ready, 1)

                turned_x(0, 0)
                turned_x(1, 1)
                silu(0, 0)
                turned_x(2, 2)
                silu(1, 1)
                with act.Fori(0, (NTILE - 4) // 2) as i:
                    for k in range(2):
                        turned_x(2 * i + 3 + k, k + 1)
                        silu(2 * i + 2 + k, k)
                turned_x(NTILE - 1, 1)
                silu(NTILE - 2, 0)
                silu(NTILE - 1, 1)

            @block.vector
            def _(dve):

                def split(t, k):
                    s = S[:, k % 2, :]
                    dve.wait_ge(silu_ready, t + 1)
                    dve.scalar_tensor_tensor(s, UB[k % 2][:, FE:2 * FE], 1.0 / WS, s, ALU.mult, ALU.mult).then_inc(prod_ready, 1)
                    dve.wait_ge(prod_ready, t + 1)
                    if type(t) is not int or t >= 2:
                        dve.wait_ge(hT_psum, t - 1)
                    dve.tensor_copy(H[:, k % 2, 0:FE], s).then_inc(hi_ready, 1)
                    dve.wait_ge(hi_ready, t + 1)
                    dve.tensor_tensor(H[:, k % 2, FE:2 * FE], s, H[:, k % 2, 0:FE], ALU.subtract).then_inc(lo_ready, 1)

                def turned_h(t, k):
                    dve.wait_ge(hT_psum, t + 1)
                    if type(t) is not int or t >= 2:
                        dve.wait_ge(down_psum, t - 1)
                    dve.tensor_copy(HT[:, k % 2, :], H16[k % 2]).then_inc(hT_ready, 1)

                def outputs(t, i, k):
                    dve.wait_ge(down_psum, t + 1)
                    dve.wait_ge(written[k], 16 * i)
                    dve.tensor_scalar(Y[:, k, :], DB[k % 2][:, :], 1.0 / WS, None, ALU.mult).then_inc(y_ready, 1)

                split(0, 0)
                split(1, 1)
                turned_h(0, 0)
                with dve.Fori(0, NS - 1) as i:
                    for k in range(K):
                        t = K * i + k
                        split(t + 2, k)
                        turned_h(t + 1, k + 1)
                        outputs(t, i, k)
                for k in range(K):
                    t = NTILE - K + k
                    if t + 2 < NTILE:
                        split(t + 2, k)
                    if t + 1 < NTILE:
                        turned_h(t + 1, k + 1)
                    outputs(t, NS - 1, k)


def moe_combine(nc, X, ys, gap, out):
    with ExitStack() as ctx:
        sb = lambda n, s, d=F32: ctx.enter_context(nc.sbuf_tensor(f"comb_{n}", s, d))
        sem = lambda n: nc.alloc_semaphore(f"comb_{n}")
        th = sb("th", [P, B])
        wt = sb("wt", [P, NR, B])
        Y = sb("Y", [P, 2, TT, NR, D])
        rows = ys[0:NR * B * P, :].rearrange("(r b p) n -> p b r n", r=NR, p=P)
        norms = [Norm(nc, ctx, f"moe_norm{h}") for h in range(2)]
        tanh_ready, weights_ready, first_added, stored = (sem("tanh_ready"), sem("weights_ready"), sem("first_added"),
                                                          sem("stored"))
        fetched = [[sem(f"fetched{h}{j}") for j in range(TT)] for h in range(2)]
        NI = B // (2 * TT)

        with nc.Block() as block:

            @block.scalar
            def _(act):

                def fetch(i, h):
                    for j in range(TT):
                        if type(i) is not int:
                            act.wait_ge(norms[h].rows_ready, TT * (i - 1) + j + 1)
                        act.dma_start(Y[:, h, j, :, :], rows[:, ds(TT * (2 * i + h) + j, 1), :, :].rearrange("p b r n -> p (b r) n"))\
                           .then_inc(fetched[h][j], 16)

                fetch(0, 0)
                fetch(0, 1)
                act.activation(th[:, :], gap[:, :], ACT.Tanh, scale=0.5).then_inc(tanh_ready, 1)
                with act.Fori(0, NI - 1) as i:
                    for h in range(2):
                        fetch(i + 1, h)

            @block.gpsimd
            def _(pool):
                for n in norms:
                    norm_consts(pool, n)
                with pool.Fori(0, NI - 1) as i:
                    for h in range(2):
                        norm_rstd(pool, norms[h], i)
                for h in range(2):
                    norm_rstd(pool, norms[h], NI - 1)

            @block.vector
            def _(dve):
                dve.wait_ge(tanh_ready, 1)
                dve.tensor_scalar(wt[:, 0, :], th[:, :], 0.5, 0.5, ALU.mult, ALU.add).then_inc(weights_ready, 1)
                dve.tensor_scalar(wt[:, 1, :], th[:, :], -0.5, 0.5, ALU.mult, ALU.add).then_inc(weights_ready, 1)
                dve.wait_ge(weights_ready, 2)

                def add(i, h):
                    g = 2 * i + h
                    for j in range(TT):
                        x = tile(X, TT * g + j)
                        dve.wait_ge(fetched[h][j], 16 * (i + 1))
                        dve.scalar_tensor_tensor(x, Y[:, h, j, 0, :], wt[:, 0, ds(TT * g + j, 1)], x, ALU.mult, ALU.add)\
                           .then_inc(first_added, 1)
                    for j in range(TT):
                        x = tile(X, TT * g + j)
                        dve.wait_ge(first_added, TT * g + j + 1)
                        dve.scalar_tensor_tensor(x, Y[:, h, j, 1, :], wt[:, 1, ds(TT * g + j, 1)], x, ALU.mult, ALU.add)\
                           .then_inc(norms[h].rows_ready, 1)
                    for j in range(TT):
                        norm_stats(dve, norms[h], X, i, j, TT * g + j)
                    for j in range(TT):
                        norm_aggr(dve, norms[h], i, j)

                def apply(i, h):
                    for j in range(TT):
                        norm_apply(dve, norms[h], X, i, j, TT * (2 * i + h) + j)

                add(0, 0)
                add(0, 1)
                apply(0, 0)
                with dve.Fori(0, NI - 1) as i:
                    add(i + 1, 0)
                    apply(i, 1)
                    add(i + 1, 1)
                    apply(i + 1, 0)
                apply(NI - 1, 1)

            @block.sync
            def _(sp):
                n = TT * D
                with sp.Fori(0, NI) as i:
                    for h in range(2):
                        sp.wait_ge(norms[h].normed, TT * i + TT)
                        sp.dma_start(out[:, ds(n * (2 * i + h), n)], group(X, TT * (2 * i + h), TT).rearrange("p b n -> p (b n)"))\
                          .then_inc(stored, 16)
                sp.wait_ge(stored, 16 * (B // TT))


KH = 8
HD = 16
QH = 32
QG = QH // KH
SL = 4
ORDER = (0, 2, 1, 3)
VW = HD + 1


VG = KH // 4
VP = VG * 2 * 3 * VW
VF = 2 * VG * VW
VS = (VP + VF) // 2


def cross_attention(nc, name, X, k_dram, v_dram, idh, nsel_dram, gmask_dram, prefetch=()):
    with ExitStack() as ctx:
        sb = lambda n, s, d=F32: ctx.enter_context(nc.sbuf_tensor(f"{name}_{n}", s, d))
        ps = lambda n, s, d=F32: ctx.enter_context(nc.psum_tensor(f"{name}_{n}", s, d))
        sem = lambda n: nc.alloc_semaphore(f"{name}_{n}")
        LAG = 3
        KT = sb("KT", [P, 3, 2, KH, P], F16)
        nsel = sb("nsel", [QH, KH * P], F16)
        gm = sb("gmask", [QG * KH, QG * P], F16)
        gmask = gm[:, :].rearrange("p (g t) -> p g t", g=QG)
        Vt = sb("V", [P, 3, VS])
        V = Vt[:, :, 0:VP // 2].bitcast(F16).rearrange("p u (g a h d) -> p u g a h d", g=VG, a=2, h=3)
        V32 = Vt[:, :, VP // 2:VS].rearrange("p u (g d) -> p u g d", g=VG)
        Q = sb("Q", [P, QH, SL, HD], F16)
        QT = sb("QT", [P, 3, 16, P], F16)
        Mx = sb("Mx", [P, QH], F16)
        MD = sb("MD", [QH, 3, QG, P], F16)
        W32, Wh, Wl = sb("W32", [P, KH, GT]), sb("Wh", [P, KH, GT], F16), sb("Wl", [P, KH, GT], F16)
        rinv = sb("rinv", [P, QH])
        O = sb("O", [P, D])
        psQ = ps("psQ", [P, 8, P], F16)
        psM = ps("psM", [QH, P], F16)
        psS = [ps(f"psS{k}", [P, QG, P]) for k in range(2)]
        psW = [ps(f"psW{k}", [P, GT]) for k in range(2)]
        psO = [ps(f"psO{k}", [P, 16, VW]) for k in range(2)]
        norm = Norm(nc, ctx, f"{name}_norm", 1)
        qh_ready, ql_ready, q_psum, q_ready = sem("qh_ready"), sem("ql_ready"), sem("q_psum"), sem("q_ready")
        s_psum, max_ready, m_psum, md_ready = sem("s_psum"), sem("max_ready"), sem("m_psum"), sem("md_ready")
        w_psum, w32_ready, wh_ready, wl_dve, wl_pool = (sem("w_psum"), sem("w32_ready"), sem("wh_ready"), sem("wl_dve"),
                                                        sem("wl_pool"))
        kv_loaded = [sem(f"kv_loaded{u}") for u in range(3)]
        zeros_set, pv_done, rinv_ready, o_ready = sem("zeros_set"), sem("pv_done"), sem("rinv_ready"), sem("o_ready")
        qh2_ready, prefetched, masks_loaded = sem("qh2_ready"), sem("prefetched"), sem("masks_loaded")
        more_zeros_set = sem("more_zeros_set")


        FLOAT = [k for k in range(KH) if k % 4 == 3]
        PAIRS = [k for k in range(KH) if k % 4 != 3]
        LO_DVE = (0, 4)

        def first(b):
            return type(b) is int and b == 0

        def lo_count(k):
            mine = [j for j in PAIRS if (j in LO_DVE) == (k in LO_DVE)]
            return (wl_dve if k in LO_DVE else wl_pool), len(mine), mine.index(k) + 1

        def wait_exps(eng, b, k):
            if k in FLOAT:
                eng.wait_ge(w32_ready, KH * b + k + 1)
            else:
                eng.wait_ge(wh_ready, len(PAIRS) * b + PAIRS.index(k) + 1)


        def q_hi(eng, b):
            eng.wait_ge(q_psum, 2 * b)
            eng.tensor_copy(Q[:, :, 0, :], tile(X, b).rearrange("p (h d) -> p h d", d=HD)).then_inc(qh_ready, 1)

        def q_hi_again(act, b):
            act.wait_ge(q_psum, 2 * b)
            act.activation(Q[:, :, 1, :], tile(X, b).rearrange("p (h d) -> p h d", d=HD), ACT.Copy).then_inc(qh2_ready, 1)

        def q_lo(eng, b):
            wait_apart(eng, norm.waits_apart, qh_ready, b + 1)
            x = tile(X, b).rearrange("p (h d) -> p h d", d=HD)
            eng.tensor_tensor(Q[:, :, 2, :], x, Q[:, :, 0, :], ALU.subtract).then_inc(ql_ready, 1)

        def turn_q(pe, b, half):
            if half == 0:
                pe.wait_ge(ql_ready, b + 1)
                pe.wait_ge(qh_ready, b + 1)
                pe.wait_ge(qh2_ready, b + 1)
            pe.wait_ge(q_ready, 2 * b + half)
            for n in range(8):
                h = 2 * (8 * half + n)
                q = Q[:, h:h + 2, :, :].rearrange("p h s d -> p (h s d)")
                t = pe.transpose(psQ[:, n, :], q, idh[:, :])
            t.then_inc(q_psum, 1)

        def q_out(act, b, u, half):
            act.wait_ge(q_psum, 2 * b + half + 1)
            act.activation(QT[:, u, 8 * half:8 * half + 8, :].rearrange("p a t -> p (a t)"),
                           psQ[:, :, :].rearrange("p a t -> p (a t)"), ACT.Copy).then_inc(q_ready, 1)

        def scores(pe, b, u, k):
            if k == 0:
                pe.wait_ge(kv_loaded[u], 16 * (b - u) + 48)
            pe.wait_ge(q_ready, 2 * b + 1 + k // 4)
            if not (first(b) and k < 2):
                pe.wait_ge(max_ready, KH * b + k - 1)
            if k == 0:
                pe.wait_ge(zeros_set, 3)
                if not first(b):
                    pe.wait_ge(more_zeros_set, 4)
            for a in range(2):
                t = pe.matmul(psS[k % 2][:, 2 * a:2 * a + 2, :], QT[:, u, 2 * k + a, :], KT[:, u, :, k, :], start=True, stop=True)
            t.then_inc(s_psum, 1)

        def load(sp, b, u):
            for e in range(2):
                r = slice(64 * e, 64 * e + 64)
                sp.dma_start(KT[r, u, e, :, :].rearrange("p k t -> p (k t)"),
                             k_dram[:, ds(b, 1), :].rearrange("p a n -> p (a n)")).then_inc(kv_loaded[u], 16)
            sp.dma_start(Vt[:, u, :],
                         v_dram[:, ds(b, 1), :].rearrange("p a n -> p (a n)")).then_inc(kv_loaded[u], 16)

        def maxima(dve, b, k):
            dve.wait_ge(s_psum, KH * b + k + 1)
            if k == 0:
                dve.wait_ge(m_psum, b)
            dve.tensor_reduce(Mx[:, QG * k:QG * k + QG], psS[k % 2][:, :, :], AX.X, ALU.max).then_inc(max_ready, 1)

        def turn_max(pe, b):
            pe.wait_ge(max_ready, KH * b + KH)
            pe.wait_ge(md_ready, b)
            pe.transpose(psM[:, :], Mx[:, :], idh[:, :]).then_inc(m_psum, 1)

        def spread_max(dve, b, u):
            dve.wait_ge(m_psum, b + 1)
            dve.tensor_tensor(MD[:, u, :, :], psM[:, :].unsqueeze(1).to_broadcast([QH, QG, P]), gmask, ALU.mult)\
               .then_inc(md_ready, 1)

        def turned_scores(pe, b, u, k):
            if k >= 2:
                wait_exps(pe, b, k - 2)
            elif not first(b):
                wait_exps(pe, b - 1, KH + k - 2)
            if k == 0:
                pe.wait_ge(md_ready, b + 1)
            pe.matmul(psW[k % 2][:, :], nsel[:, k * P:(k + 1) * P], MD[:, u, :, :].rearrange("p g t -> p (g t)"),
                      start=True, stop=False)
            for e in range(2):
                t = pe.matmul(psW[k % 2][:, 2 * P * e:2 * P * e + 2 * P], KT[:, u, e, k, :],
                              QT[:, u, 2 * k:2 * k + 2, :].rearrange("p a t -> p (a t)"), start=False, stop=(e == 1))
            t.then_inc(w_psum, 1)

        def weights(act, b, k):
            act.wait_ge(w_psum, KH * b + k + 1)
            if not first(b) and k in PAIRS:
                wl, n, m = lo_count(k)
                act.wait_ge(wl, n * (b - 1) + m)
            elif not first(b):
                act.wait_ge(pv_done, KH * (b - 1) + k + 1)
            act.activation(W32[:, k, :], psW[k % 2][:, :], ACT.Exp, scale=0.25).then_inc(w32_ready, 1)
            if k in FLOAT:
                return
            if not first(b):
                act.wait_ge(pv_done, KH * (b - 1) + k + 1)
            act.activation(Wh[:, k, :], psW[k % 2][:, :], ACT.Exp, scale=0.25).then_inc(wh_ready, 1)

        def weights_lo(eng, b, k):
            eng.wait_ge(w32_ready, KH * b + k + 1)
            wait_exps(eng, b, k)
            if not first(b):
                eng.wait_ge(pv_done, KH * (b - 1) + k + 1)
            eng.tensor_tensor(Wl[:, k, :], W32[:, k, :], Wh[:, k, :], ALU.subtract)\
               .then_inc(lo_count(k)[0], 1)

        def values(pe, b, u, k):
            wait_exps(pe, b, k)
            if k in PAIRS:
                wl, n, m = lo_count(k)
                pe.wait_ge(wl, n * b + m)
            if k % 4 == 0 and not first(b):
                pe.wait_ge(o_ready, 2 * (b - 1) + k // 4 + 1)
            for g in range(QG):
                h = QG * k + g
                at = ORDER.index(g) * P
                w = slice(at, at + P)
                out = psO[h // 16][:, h % 16, :]
                if k in FLOAT:
                    t = pe.matmul(out, W32[:, k, w], V32[:, u, k // 4, :], start=True, stop=True)
                else:
                    v = [V[:, u, k // 4, h, k % 4, :] for h in range(2)]
                    pe.matmul(out, Wh[:, k, w], v[0], start=True, stop=False)
                    pe.matmul(out, Wh[:, k, w], v[1], start=False, stop=False)
                    t = pe.matmul(out, Wl[:, k, w], v[0], start=False, stop=True)
            t.then_inc(pv_done, 1)

        def divide(dve, b, a):
            r = rinv[:, 16 * a:16 * a + 16]
            dve.wait_ge(pv_done, KH * b + 4 * a + 4)
            dve.reciprocal(r, psO[a][:, :, HD]).then_inc(rinv_ready, 1)
            dve.wait_ge(rinv_ready, 2 * b + a + 1)
            dve.tensor_tensor(O[:, 256 * a:256 * a + 256].rearrange("p (h d) -> p h d", d=HD), psO[a][:, :, 0:HD],
                              r.unsqueeze(2).to_broadcast([P, 16, HD]), ALU.mult).then_inc(o_ready, 1)

        def add(dve, b):
            dve.wait_ge(o_ready, 2 * b + 2)
            x = tile(X, b)
            dve.tensor_tensor(x, x, O[:, :], ALU.add).then_inc(norm.rows_ready, 1)

        def every_sequence(eng, sequence):
            for b in range(2):
                sequence(b, b, lambda d: b + d >= 0)
            with eng.Fori(0, (B - 5) // 3) as r:
                for v in range(3):
                    sequence(r * 3 + (v + 2), (v + 2) % 3, lambda d: True)
            for b in range(B - 3, B):
                sequence(b, b % 3, lambda d: b + d < B)

        with nc.Block() as block:

            @block.sync
            def _(sp):
                for b in range(3):
                    load(sp, b, b)
                for to, of in ((nsel, nsel_dram), (gm, gmask_dram)):
                    sp.dma_start(to[:, :], of).then_inc(masks_loaded, 16)
                for to, of in prefetch:
                    sp.dma_start(to, of).then_inc(prefetched, 16)

                def reload(b, u):
                    sp.wait_ge(w_psum, KH * (b + 1))
                    sp.wait_ge(pv_done, KH * (b + 1))
                    load(sp, b + 3, u)

                with sp.Fori(0, (B - 5) // 3) as r:
                    for v in range(3):
                        reload(r * 3 + v, v)
                for b in range(B - 5, B - 3):
                    reload(b, b % 3)
                if prefetch:
                    sp.wait_ge(prefetched, 16 * len(prefetch))

            @block.gpsimd
            def _(pool):
                for n, (u, e) in enumerate(((1, 0), (1, 1), (2, 0), (2, 1))):
                    pool.memset(KT[64 - 64 * e:128 - 64 * e, u, e, :, :], 0.0).then_inc(more_zeros_set, 1)
                    pool.wait_ge(more_zeros_set, n + 1)
                norm_consts(pool, norm)
                for b in range(1, 3):
                    q_hi(pool, b)
                    q_lo(pool, b)

                def sequence(b, u, has):
                    weights_lo(pool, b, 1)
                    weights_lo(pool, b, 2)
                    weights_lo(pool, b, 5)
                    weights_lo(pool, b, 6)
                    if has(3):
                        q_hi(pool, b + 3)
                    if has(-1):
                        norm_rstd(pool, norm, b - 1)
                    if has(3):
                        q_lo(pool, b + 3)

                every_sequence(pool, sequence)
                norm_rstd(pool, norm, B - 1)

            @block.tensor
            def _(pe):

                def sequence(b, u, has):
                    for k in range(KH):
                        turned_scores(pe, b, u, k)
                        if k < KH - 1 and has(1):
                            scores(pe, b + 1, (u + 1) % 3, k + 1)
                        if k >= LAG:
                            values(pe, b, u, k - LAG)
                        elif has(-1):
                            values(pe, b - 1, (u + 2) % 3, KH + k - LAG)
                        if k in (3, 5) and has(2):
                            turn_q(pe, b + 2, k // 4)
                    if has(1):
                        turn_max(pe, b + 1)
                    if has(2):
                        scores(pe, b + 2, (u + 2) % 3, 0)

                pe.wait_ge(zeros_set, 1)
                for half in range(2):
                    turn_q(pe, 0, half)
                for k in range(KH):
                    scores(pe, 0, 0, k)
                turn_max(pe, 0)
                for half in range(2):
                    turn_q(pe, 1, half)
                scores(pe, 1, 1, 0)
                pe.wait_ge(masks_loaded, 32)
                every_sequence(pe, sequence)
                for k in range(KH - LAG, KH):
                    values(pe, B - 1, (B - 1) % 3, k)

            @block.scalar
            def _(act):

                def sequence(b, u, has):
                    for k in range(KH):
                        weights(act, b, k)
                        if k in (3, 5) and has(2):
                            q_out(act, b + 2, (u + 2) % 3, k // 4)
                    if has(3):
                        q_hi_again(act, b + 3)

                for b in range(2):
                    q_hi_again(act, b)
                    for half in range(2):
                        q_out(act, b, b, half)
                q_hi_again(act, 2)
                every_sequence(act, sequence)

            @block.vector
            def _(dve):

                def sequence(b, u, has):
                    for k in range(KH):
                        if k < KH - 1 and has(1):
                            maxima(dve, b + 1, k + 1)
                        if k - 1 in LO_DVE:
                            weights_lo(dve, b, k - 1)
                        if k == 2 and has(-2):
                            norm_apply(dve, norm, X, b - 2, 0)
                        if k == 3 and has(-1):
                            divide(dve, b - 1, 1)
                        if k == 4 and has(-1):
                            add(dve, b - 1)
                        if k == 5 and has(-1):
                            norm_stats(dve, norm, X, b - 1, 0)
                        if k == 6 and has(-1):
                            norm_aggr(dve, norm, b - 1, 0)
                    if has(1):
                        spread_max(dve, b + 1, (u + 1) % 3)
                    divide(dve, b, 0)
                    if has(2):
                        maxima(dve, b + 2, 0)

                dve.memset(Q[:, :, 3, :], 0.0).then_inc(zeros_set, 1)
                q_hi(dve, 0)
                q_lo(dve, 0)
                for e in range(2):
                    dve.memset(KT[64 - 64 * e:128 - 64 * e, 0, e, :, :], 0.0).then_inc(zeros_set, 1)
                for k in range(KH):
                    maxima(dve, 0, k)
                dve.wait_ge(masks_loaded, 32)
                spread_max(dve, 0, 0)
                maxima(dve, 1, 0)
                every_sequence(dve, sequence)
                norm_apply(dve, norm, X, B - 2, 0)
                divide(dve, B - 1, 1)
                add(dve, B - 1)
                norm_stats(dve, norm, X, B - 1, 0)
                norm_aggr(dve, norm, B - 1, 0)
                norm_apply(dve, norm, X, B - 1, 0)


LAT = 128
LA_LOADS = 16 * 10
DCMP = 64


def latent_attention(nc, X, w, idf, up):
    with ExitStack() as ctx:
        sb = lambda n, s, d=F32: ctx.enter_context(nc.sbuf_tensor(f"la_{n}", s, d))
        sem = lambda n: nc.alloc_semaphore(f"la_{n}")
        ps = lambda n: ctx.enter_context(nc.psum_tensor(f"la_{n}", [P, GT], F32))
        psT = [ps(f"psT{k}") for k in range(2)]
        psC = ps("psC")
        psCT = ps("psCT")
        psQ = [ps(f"psQ{k}") for k in range(2)]
        psS = ps("psS")
        psE = ps("psE")
        psX = psT + psQ
        psQK = psQ + [psCT]
        psO = psT + [psE, psS]
        Wkv = sb("Wkv", [P, D])
        Wsum = sb("Wsum", [P, D])
        WcT = sb("WcT", [P, DCMP])
        Wl = sb("Wl", [P, DCMP])
        Win = sb("Win", [P, DC, DCMP])
        Wout = sb("Wout", [P, D])
        Wqk = sb("Wqk", [P, 3, P])
        WvT = sb("WvT", [P, DCMP])
        gb = sb("gb", [DCMP, 2])
        rope = sb("rope", [P, 2, GT])
        mask = sb("mask", [P, P])
        bout = sb("bout", [P, D])
        X4 = sb("X4", [P, GS, D])
        XT = sb("XT", [P, DC, GT])
        x_copied = sem("x_copied")
        CN = sb("CN", [P, GS, DCMP])
        CT = sb("CT", [P, GT])
        RT = sb("RT", [P, 3, GT])
        V = sb("V", [P, GS, DCMP])
        S = sb("S", [P, GS, P])
        E = sb("E", [P, GS, P])
        ET = sb("ET", [P, GS, P])
        OT = sb("OT", [P, GT])
        up_dram, up_hi, up_lo = up
        UW = NE * W12E // (2 * NG)
        U = sb("U", [P, 2, 2 * UW])
        mx, nmx = sb("mx", [P, GS]), sb("nmx", [P, GS])
        rs, rinv = sb("rs", [P, GS]), sb("rinv", [P, GS])
        norm = Norm(nc, ctx, "la_norm")
        cn = Norm(nc, ctx, "la_cnorm")
        loaded, w_summed = sem("loaded"), sem("w_summed")
        u_loaded, u_scaled, uh_made, ul_made = ([sem(f"u_loaded{h}") for h in range(2)], sem("u_scaled"), sem("uh_made"),
                                                  sem("ul_made"))
        xT_psum, xT_ready, win_psum, win_ready = sem("xT_psum"), sem("xT_ready"), sem("win_psum"), sem("win_ready")
        c_psum, cn_ready, cT_psum, cT_ready = sem("c_psum"), sem("cn_ready"), sem("cT_psum"), sem("cT_ready")
        qk_psum, roped, zeros_set, v_psum, v_ready = (sem("qk_psum"), sem("roped"), sem("zeros_set"), sem("v_psum"),
                                                      sem("v_ready"))
        s_psum, s_masked, mx_ready, nmx_ready, e_ready = (sem("s_psum"), sem("s_masked"), sem("mx_ready"), sem("nmx_ready"),
                                                          sem("e_ready"))
        eT_psum, eT_ready, oT_psum, oT_ready = sem("eT_psum"), sem("eT_ready"), sem("oT_psum"), sem("oT_ready")
        wout_psum, wout_ready, out_psum, rinv_ready, biased = (sem("wout_psum"), sem("wout_ready"), sem("out_psum"),
                                                               sem("rinv_ready"), sem("biased"))
        j4 = lambda t: t.rearrange("p (j n) -> p j n", j=GS)

        with nc.Block() as block:

            @block.sync
            def _(sp):
                pairs = [(Wkv[:, :], w["Wkv"]), (Wsum[:, :], w["WoT"]), (WcT[:, :], w["WcT"]),
                         (Wqk[:, :, :].rearrange("p c n -> p (c n)"), w["Wqk"]), (WvT[:, :], w["WvT"]),
                         (Wl[:, :], w["Wl"]), (gb[:, :], w["gb"]), (rope[:, :, :].rearrange("p c n -> p (c n)"), w["rope"]),
                         (mask[:, :], w["mask"]), (bout[:, :], w["bout"].partition_broadcast(P))]

                def copy(i):
                    sp.dma_start(X4[:, :, :], group(X, GS * i)).then_inc(x_copied, 16)

                def load_up(g, h):
                    sp.dma_start(U[:, h, :], up_dram[:, ds(g * (2 * UW), 2 * UW)]).then_inc(u_loaded[h], 16)

                copy(0)
                for to, of in pairs:
                    sp.dma_start(to, of).then_inc(loaded, 16)
                for h in range(2):
                    load_up(h, h)

                def next_copy(i):
                    sp.wait_ge(xT_psum, DC * i)
                    copy(i)

                def next_up(i, h):
                    sp.wait_ge(ul_made, 2 * i - 2)
                    load_up(i, h)

                next_copy(1)
                next_copy(2)
                with sp.Fori(0, NG // 2 - 2) as r:
                    for h in range(2):
                        next_copy(r * 2 + (h + 3))
                        next_up(r * 2 + (h + 2), h)
                next_copy(NG - 1)
                for h in range(2):
                    next_up(NG - 2 + h, h)
                sp.wait_ge(x_copied, 16 * NG)

            @block.gpsimd
            def _(pool):
                norm_consts(pool, norm)
                norm_consts(pool, cn)
                pool.wait_ge(loaded, LA_LOADS)
                pool.tensor_tensor(Wsum[:, :], Wsum[:, :], Wkv[:, :], ALU.add).then_inc(w_summed, 1)
                norm_rstd(pool, cn, 0)

                def bias(i):
                    wait_apart(pool, norm.waits_apart, xT_psum, DC * i + DC)
                    for j in range(GS):
                        x = tile(X, GS * i + j)
                        pool.tensor_tensor(x, x, bout[:, :], ALU.add).then_inc(biased, 1)

                bias(0)
                norm_rstd(pool, cn, 1)
                bias(1)

                def up_los(i, h):
                    for k in range(2):
                        pool.wait_ge(uh_made, 2 * i + k + 1)
                        at = ds((2 * i + k) * UW, UW)
                        pool.tensor_tensor(up_lo[:, at], U[:, h, k * UW:(k + 1) * UW], up_hi[:, at], ALU.subtract)\
                            .then_inc(ul_made, 1)

                with pool.Fori(0, NG // 2 - 1) as r:
                    for h in range(2):
                        i = r * 2 + h
                        bias(i + 2)
                        norm_rstd(pool, cn, i + 2)
                        norm_rstd(pool, norm, i)
                        up_los(i, h)
                for i in range(NG - 2, NG):
                    up_los(i, i % 2)
                norm_rstd(pool, norm, NG - 2)
                norm_rstd(pool, norm, NG - 1)

            @block.tensor
            def _(pe):

                def weights_products():
                    pe.wait_ge(loaded, LA_LOADS)
                    for c in range(DC):
                        m = pe.matmul(psC[:, c * DCMP:(c + 1) * DCMP], Wkv[:, c * P:(c + 1) * P], WcT[:, :], start=True, stop=True)
                    m.then_inc(win_psum, 1)
                    pe.wait_ge(w_summed, 1)
                    pe.matmul(psS[0:DCMP, :], Wl[:, :], Wsum[:, :], start=True, stop=True).then_inc(wout_psum, 1)

                def turn_x(i):
                    pe.wait_ge(x_copied, 16 * i + 16)
                    if type(i) is not int or i > 0:
                        pe.wait_ge(norm.rows_ready, GS * (i - 1))
                    for c in range(DC):
                        for j in range(GS):
                            x = X4[:, j, c * P:(c + 1) * P]
                            t = pe.transpose(psX[c][:, j * P:(j + 1) * P], x, idf[:, :])
                        t.then_inc(xT_psum, 1)

                def compressed(i, part):
                    if part == 0:
                        pe.wait_ge(xT_ready, DC * i + DC)
                        pe.wait_ge(cn_ready, GS * i)
                    for j in range(part * GS // 2, (part + 1) * GS // 2):
                        for c in range(DC):
                            t = pe.matmul(psC[:, j * DCMP:(j + 1) * DCMP], XT[:, c, j * P:(j + 1) * P], Win[:, c, :],
                                          start=(c == 0), stop=(c == DC - 1))
                    t.then_inc(c_psum, 1)

                def turn_c(i):
                    wait_apart(pe, cn.waits_apart, cT_ready, i)
                    wait_apart(pe, cn.waits_apart, cn_ready, GS * i + GS)
                    for j in range(GS):
                        t = pe.transpose(psCT[0:DCMP, j * P:(j + 1) * P], CN[:, j, :], idf[:, :])
                    t.then_inc(cT_psum, 1)

                def queries_keys(i):
                    wait_apart(pe, norm.waits_apart, cT_ready, i + 1)
                    for n in range(3):
                        if n == 0 and (type(i) is not int or i > 0):
                            wait_apart(pe, norm.waits_apart, roped, 3 * i)
                        pe.matmul(psQK[n][:, :], Wqk[:, n, :], CT[:, :], start=True, stop=True).then_inc(qk_psum, 1)
                    wait_apart(pe, norm.waits_apart, v_ready, i)
                    for j in range(GS):
                        t = pe.matmul(psC[:, (GS + j) * DCMP:(GS + j + 1) * DCMP], CT[:, j * P:(j + 1) * P], WvT[:, :],
                                      start=True, stop=True)
                    t.then_inc(v_psum, 1)

                def scores(i):
                    pe.wait_ge(roped, 3 * i + 3)
                    pe.wait_ge(norm.rows_ready, GS * i)
                    for j in range(GS):
                        c = slice(j * P, (j + 1) * P)
                        pe.matmul(psS[:, c], RT[:, 0, c], RT[:, 1, c], start=True, stop=False)
                        t = pe.matmul(psS[:, c], RT[:, 0, c], RT[:, 2, c], start=False, stop=True)
                    t.then_inc(s_psum, 1)

                def turn_e(i):
                    pe.wait_ge(e_ready, GS * i + GS)
                    pe.wait_ge(eT_ready, i)
                    for j in range(GS):
                        t = pe.transpose(psE[:, j * P:(j + 1) * P], E[:, j, :], idf[:, :])
                    t.then_inc(eT_psum, 1)

                def attended(i):
                    pe.wait_ge(eT_ready, i + 1)
                    pe.wait_ge(v_ready, i + 1)
                    for j in range(GS):
                        t = pe.matmul(psS[0:DCMP, j * P:(j + 1) * P], V[:, j, :], ET[:, j, :], start=True, stop=True)
                    t.then_inc(oT_psum, 1)

                def outputs(i, js, last=False):
                    pe.wait_ge(oT_ready, i + 1)
                    pe.wait_ge(xT_ready, DC * i + DC * (1 if last else 2))
                    for j in js:
                        pe.matmul(psO[j][:, :], OT[:, j * P:(j + 1) * P], Wout[:, :], start=True, stop=True)\
                          .then_inc(out_psum, 1)

                pe.wait_ge(zeros_set, 3)
                turn_x(0)
                weights_products()
                pe.wait_ge(win_ready, 1)
                compressed(0, 0)
                compressed(0, 1)
                turn_c(0)
                queries_keys(0)
                pe.wait_ge(wout_ready, 1)

                def turn(i):
                    scores(i)
                    turn_x(i + 1)
                    compressed(i + 1, 0)
                    turn_e(i)
                    compressed(i + 1, 1)
                    attended(i)
                    outputs(i, range(3))
                    turn_c(i + 1)
                    outputs(i, range(3, GS))
                    queries_keys(i + 1)

                turn(0)
                with pe.Fori(0, NG - 2) as r:
                    turn(r + 1)
                scores(NG - 1)
                turn_e(NG - 1)
                attended(NG - 1)
                outputs(NG - 1, range(GS), last=True)

            @block.scalar
            def _(act):

                def x_out(i):
                    act.wait_ge(c_psum, 2 * i)
                    for c in range(DC):
                        act.wait_ge(xT_psum, DC * i + c + 1)
                        act.activation(XT[:, c, :], psX[c][:, :], ACT.Copy).then_inc(xT_ready, 1)

                def c_out(i):
                    act.wait_ge(cT_psum, i + 1)
                    act.wait_ge(v_psum, i)
                    act.activation(CT[0:DCMP, :], psCT[0:DCMP, :], ACT.Identity, bias=gb[:, 1:2], scale=gb[:, 0:1])\
                       .then_inc(cT_ready, 1)

                def v_out(i):
                    act.wait_ge(v_psum, i + 1)
                    act.wait_ge(oT_psum, i)
                    act.activation(V[:, :, :].rearrange("p j n -> p (j n)"), psC[:, GS * DCMP:2 * GS * DCMP], ACT.Copy)\
                       .then_inc(v_ready, 1)

                def exps(i):
                    act.wait_ge(nmx_ready, i + 1)
                    act.wait_ge(eT_psum, i)
                    act.wait_ge(rinv_ready, i)
                    for j in range(GS):
                        act.activation(E[:, j, :], S[:, j, :], ACT.Exp, bias=nmx[:, j:j + 1], scale=0.125,
                                       accum_out=rs[:, j:j + 1]).then_inc(e_ready, 1)

                def e_out(i):
                    act.wait_ge(eT_psum, i + 1)
                    act.wait_ge(oT_psum, i)
                    act.activation(ET[:, :, :].rearrange("p j n -> p (j n)"), psE[:, :], ACT.Copy).then_inc(eT_ready, 1)

                def o_out(i):
                    act.wait_ge(oT_psum, i + 1)
                    act.wait_ge(out_psum, GS * i)
                    act.activation(OT[0:DCMP, :], psS[0:DCMP, :], ACT.Copy).then_inc(oT_ready, 1)

                def up_his(i, h, k):
                    c = slice(k * UW, (k + 1) * UW)
                    act.wait_ge(u_loaded[h], (i - h) * 8 + 16)
                    act.activation(U[:, h, c], U[:, h, c], ACT.Copy, scale=WS).then_inc(u_scaled, 1)
                    act.wait_ge(u_scaled, 2 * i + k + 1)
                    act.activation(up_hi[:, ds((2 * i + k) * UW, UW)], U[:, h, c], ACT.Copy).then_inc(uh_made, 1)

                x_out(0)
                act.wait_ge(loaded, LA_LOADS)
                act.wait_ge(win_psum, 1)
                act.activation(Win[:, :, :].rearrange("p c n -> p (c n)"), psC[:, 0:DC * DCMP], ACT.Copy).then_inc(win_ready, 1)
                act.wait_ge(wout_psum, 1)
                act.activation(Wout[0:DCMP, :], psS[0:DCMP, :], ACT.Copy).then_inc(wout_ready, 1)
                c_out(0)
                v_out(0)

                def turn(i, h):
                    x_out(i + 1)
                    exps(i)
                    e_out(i)
                    o_out(i)
                    up_his(i, h, 0)
                    c_out(i + 1)
                    up_his(i, h, 1)
                    v_out(i + 1)

                turn(0, 0)
                with act.Fori(0, NG // 2 - 1) as r:
                    for h in range(2):
                        turn(r * 2 + (1 + h), 1 - h)
                for k in range(2):
                    up_his(NG - 1, 1, k)
                exps(NG - 1)
                e_out(NG - 1)
                o_out(NG - 1)

            @block.vector
            def _(dve):

                def compressed_norm(i):
                    wait_apart(dve, cn.waits_apart, c_psum, 2 * i + 2)
                    for j in range(GS):
                        dve.bn_stats(cn.stats[:, j, :], psC[:, j * DCMP:(j + 1) * DCMP]).then_inc(cn.stats_ready, 1)
                    for j in range(GS):
                        norm_aggr(dve, cn, i, j)
                    dve.wait_ge(cn.rstd_ready, i + 1)
                    dve.wait_ge(cT_psum, i)
                    for j in range(GS):
                        dve.tensor_scalar(CN[:, j, :], psC[:, j * DCMP:(j + 1) * DCMP], cn.mv[:, j, 0:1],
                                          cn.rstd[:, j:j + 1], ALU.subtract, ALU.mult).then_inc(cn_ready, 1)

                def apply_rope(i):
                    dve.wait_ge(s_psum, i)
                    for n in range(3):
                        dve.wait_ge(qk_psum, 3 * i + n + 1)
                        dve.tensor_tensor(RT[:, n, :], psQK[n][:, :], rope[:, n // 2, :], ALU.mult).then_inc(roped, 1)

                def masked(i):
                    dve.wait_ge(s_psum, i + 1)
                    dve.wait_ge(e_ready, GS * i)
                    dve.tensor_tensor(S[:, :, :], j4(psS[:, :]), mask[:, :].unsqueeze(1).to_broadcast([P, GS, P]), ALU.add)\
                       .then_inc(s_masked, 1)
                    dve.wait_ge(s_masked, i + 1)
                    dve.tensor_reduce(mx[:, :], S[:, :, :], AX.X, ALU.max).then_inc(mx_ready, 1)
                    dve.wait_ge(mx_ready, i + 1)
                    dve.tensor_scalar(nmx[:, :], mx[:, :], -0.125, None, ALU.mult).then_inc(nmx_ready, 1)

                def add(i):
                    dve.wait_ge(e_ready, GS * i + GS)
                    dve.reciprocal(rinv[:, :], rs[:, :]).then_inc(rinv_ready, 1)
                    dve.wait_ge(rinv_ready, i + 1)
                    for j in range(GS):
                        dve.wait_ge(out_psum, GS * i + j + 1)
                        dve.wait_ge(biased, GS * i + j + 1)
                        x = tile(X, GS * i + j)
                        dve.scalar_tensor_tensor(x, psO[j][:, :], rinv[:, j:j + 1], x, ALU.mult, ALU.add)\
                           .then_inc(norm.rows_ready, 1)

                def stats(i):
                    for j in range(GS):
                        norm_stats(dve, norm, X, i, j)
                    for j in range(GS):
                        norm_aggr(dve, norm, i, j)

                def apply(i):
                    for j in range(GS):
                        norm_apply(dve, norm, X, i, j)

                for z in (CT, OT, Wout):
                    dve.memset(z[DCMP:P, :], 0.0).then_inc(zeros_set, 1)
                dve.wait_ge(loaded, LA_LOADS)
                compressed_norm(0)
                apply_rope(0)
                masked(0)
                compressed_norm(1)
                add(0)
                apply_rope(1)
                with dve.Fori(0, NG - 2) as r:
                    masked(r + 1)
                    stats(r)
                    compressed_norm(r + 2)
                    add(r + 1)
                    apply_rope(r + 2)
                    apply(r)
                masked(NG - 1)
                stats(NG - 2)
                apply(NG - 2)
                add(NG - 1)
                stats(NG - 1)
                apply(NG - 1)


CT = 16
NCT = P // CT
LC = 2 * P


WQ = 3 * DC * P


PIECES = [(n * WQ, (n + 1) * WQ) for n in range(DC)] + [(DC * WQ, DC * WQ + DC * D)]


def prepare(nc, X, a, groups, taps, Wq, k_dram, v_dram, consts):
    with ExitStack() as ctx:
        sb = lambda n, s, d=F32: ctx.enter_context(nc.sbuf_tensor(f"pre_{n}", s, d))
        sem = lambda n: nc.alloc_semaphore(f"pre_{n}")
        E = sb("E", [P, 2, D])
        Dk = sb("Dk", [P, D])
        H = [sb("Eh", [P, 2, D], F16), sb("El", [P, 2, D], F16)]
        W = sb("W", [P, WQ])
        w_loaded, wh_made, wl_made, x_loaded = sem("w_loaded"), sem("wh_made"), sem("wl_made"), sem("x_loaded")
        loaded, added, hi_made, lo_made, stored = sem("loaded"), sem("added"), sem("hi_made"), sem("lo_made"), sem("stored")
        NB = 4
        BB = B // NB
        C = sb("C", [P, B * P])
        K = sb("K", [P, B * KH, SL, HD], F16)
        KT = X[0:SL * HD, :, :].rearrange("p b n -> p (b n)").bitcast(F16).rearrange("p (b a t) -> p b a t", b=B, a=KH)
        Vt = sb("V", [P, B, VS])
        V = [Vt[:, :, g * VP // VG // 2:(g + 1) * VP // VG // 2].bitcast(F16).rearrange("p b (a h d) -> p b a h d", a=2, h=3)
             for g in range(VG)]
        V32 = Vt[:, :, VP // 2:VS].rearrange("p b (g d) -> p b g d", g=VG)
        psK = [ctx.enter_context(nc.psum_tensor(f"pre_psK{k}", [SL * HD, KH * P], F16)) for k in range(4)]
        c_loaded = [sem(f"c_loaded{n}") for n in range(NB)]
        zeros_set, khi_made, klo_made, copied = sem("zeros_set"), sem("khi_made"), sem("klo_made"), sem("copied")
        vhi_made, v_made, turned, out_act, out_dve = (sem("vhi_made"), sem("v_made"), sem("turned"), sem("out_act"),
                                                      sem("out_dve"))
        kv_stored, consts_loaded = sem("kv_stored"), [sem(f"consts_loaded{k}") for k in range(2)]
        c = C[:, :].rearrange("p (h d) -> p h d", d=HD)
        c4 = C[:, :].rearrange("p (b h d) -> p b h d", d=HD, h=KH)

        idh = consts[0][0]

        with nc.Block() as block:

            @block.sync
            def _(sp):
                for n, (to, of) in enumerate(consts):
                    sp.dma_start(to, of).then_inc(consts_loaded[min(n, 1)], 16)
                sp.dma_start(E[:, :, :].rearrange("p a c -> p (a c)"), a["kerT"]).then_inc(loaded, 16)
                sp.dma_start(Dk[:, :], a["dskip"]).then_inc(loaded, 16)
                sp.dma_start(W[:, :], a["wqkv"][:, 0:WQ]).then_inc(w_loaded, 16)
                for k, made in enumerate((hi_made, lo_made)):
                    sp.wait_ge(made, 1)
                    for h in range(2):
                        sp.dma_start(taps[k, :, h * P:(h + 1) * P, :].rearrange("n i c -> i n c"),
                                     H[k][:, h, :].rearrange("p (n c) -> p n c", c=CT)).then_inc(stored, 16)
                xT = a["xT"].rearrange("p (c t) -> p c t", c=DC)
                for h in range(2):
                    sp.dma_start(groups[:, h, :, :], xT[:, :, h * GT:(h + 1) * GT]).then_inc(x_loaded, 16)
                sp.wait_ge(x_loaded, 32)
                sp.wait_ge(stored, 64)
                sp.wait_ge(consts_loaded[1], 16 * (len(consts) - 1))

            @block.gpsimd
            def _(pool):
                for n in range(NB):
                    w = slice(n * BB * P, (n + 1) * BB * P)
                    pool.dma_start(C[:, w], a["ctx"][:, w]).then_inc(c_loaded[n], 16)
                pool.memset(K[:, :, 3, :], 0.0).then_inc(zeros_set, 1)
                for g in range(VG):
                    pool.memset(V[g][:, :, 0, :, HD:VW], 1.0).then_inc(zeros_set, 1)
                    pool.memset(V[g][:, :, 1, :, HD:VW], 0.0).then_inc(zeros_set, 1)
                pool.memset(V32[:, :, :, HD:VW], 1.0).then_inc(zeros_set, 1)
                pool.wait_ge(zeros_set, 2 + 2 * VG)
                for n in range(NB):
                    w = slice(n * BB, (n + 1) * BB)
                    pool.wait_ge(vhi_made, VG * n + VG)
                    for g in range(VG):
                        pool.tensor_tensor(V[g][:, w, 1, :, 0:HD], c4[:, w, 4 * g:4 * g + 3, :], V[g][:, w, 0, :, 0:HD],
                                           ALU.subtract).then_inc(v_made, 1)
                        pool.tensor_copy(V32[:, w, g, 0:HD], c4[:, w, 4 * g + 3, :]).then_inc(v_made, 1)
                    pool.wait_ge(v_made, 2 * VG * (n + 1))
                    pool.dma_start(v_dram[:, w, :], Vt[:, w, :])\
                        .then_inc(kv_stored, 16)
                for n in range(NB):
                    w = slice(n * BB, (n + 1) * BB)
                    pool.wait_ge(out_act, BB // 2 * (n + 1))
                    pool.wait_ge(out_dve, BB // 2 * (n + 1))
                    pool.dma_start(k_dram[:, w, :], KT[:, w, :, :].rearrange("p b a t -> p b (a t)"))\
                        .then_inc(kv_stored, 16)
                pool.wait_ge(kv_stored, 32 * NB)

            @block.scalar
            def _(act):

                def keys_out(n):
                    for b in range(n * BB, (n + 1) * BB, 2):
                        act.wait_ge(turned, b + 1)
                        act.activation(KT[:, b, :, :].rearrange("p a t -> p (a t)"), psK[b % 4][:, :], ACT.Copy).then_inc(out_act, 1)

                for n in range(NB):
                    w, h = slice(n * BB, (n + 1) * BB), slice(n * BB * KH, (n + 1) * BB * KH)
                    act.wait_ge(c_loaded[n], 16)
                    act.activation(K[:, h, 2, :], c[:, h], ACT.Copy).then_inc(copied, 1)
                    for g in range(VG):
                        act.activation(V[g][:, w, 0, :, 0:HD], c4[:, w, 4 * g:4 * g + 3, :], ACT.Copy).then_inc(vhi_made, 1)
                    if n:
                        keys_out(n - 1)
                keys_out(NB - 1)
                act.wait_ge(w_loaded, 16)
                act.activation(Wq[0][:, :], W[:, :], ACT.Copy, scale=WS).then_inc(wh_made, 1)

            @block.vector
            def _(dve):

                def keys_out(n):
                    for b in range(n * BB + 1, (n + 1) * BB, 2):
                        dve.wait_ge(turned, b + 1)
                        dve.tensor_copy(KT[:, b, :, :].rearrange("p a t -> p (a t)"), psK[b % 4][:, :]).then_inc(out_dve, 1)

                dve.wait_ge(loaded, 32)
                dve.tensor_tensor(E[:, 0, :], E[:, 0, :], Dk[:, :], ALU.add).then_inc(added, 1)
                dve.wait_ge(added, 1)
                dve.tensor_scalar(H[0][:, :, :], E[:, :, :], WS, None, ALU.mult).then_inc(hi_made, 1)
                dve.wait_ge(hi_made, 1)
                flat = lambda t: t[:, :, :].rearrange("p a c -> p (a c)")
                dve.scalar_tensor_tensor(flat(H[1]), flat(E), WS, flat(H[0]), ALU.mult, ALU.subtract).then_inc(lo_made, 1)
                for n in range(NB):
                    h = slice(n * BB * KH, (n + 1) * BB * KH)
                    dve.wait_ge(c_loaded[n], 16)
                    dve.tensor_copy(K[:, h, 0, :], c[:, h]).then_inc(khi_made, 1)
                    dve.wait_ge(khi_made, n + 1)
                    dve.tensor_tensor(K[:, h, 1, :], c[:, h], K[:, h, 0, :], ALU.subtract).then_inc(klo_made, 1)
                    if n:
                        keys_out(n - 1)
                keys_out(NB - 1)
                dve.wait_ge(wh_made, 1)
                dve.wait_ge(w_loaded, 16)
                dve.scalar_tensor_tensor(Wq[1][:, :], W[:, :], WS, Wq[0][:, :], ALU.mult, ALU.subtract).then_inc(wl_made, 1)

            @block.tensor
            def _(pe):
                pe.wait_ge(consts_loaded[0], 16)
                pe.wait_ge(zeros_set, 2 + 2 * VG)
                for b in range(B):
                    if b % BB == 0:
                        pe.wait_ge(klo_made, b // BB + 1)
                        pe.wait_ge(copied, b // BB + 1)
                    if b >= 4:
                        pe.wait_ge(out_dve if b % 2 else out_act, (b - 4) // 2 + 1)
                    for a in range(KH):
                        k = K[:, b * KH + a, :, :].rearrange("p s d -> p (s d)")
                        t = pe.transpose(psK[b % 4][:, a * P:(a + 1) * P], k, idh)
                    t.then_inc(turned, 1)


def hyena(nc, X, w, C, stage, taps, Wq, wpair, idf, flip):
    with ExitStack() as ctx:
        sb = lambda n, s, d=F32: ctx.enter_context(nc.sbuf_tensor(f"hy_{n}", s, d))
        sem = lambda n: nc.alloc_semaphore(f"hy_{n}")
        bank = [ctx.enter_context(nc.psum_tensor(f"hy_bank{k}", [P, GT], F32)) for k in range(8)]
        T = B * P
        xflat = X[:, :, :].rearrange("p b n -> p (b n)").bitcast(F16)
        XT = [xflat[:, k * DC * T:(k + 1) * DC * T] for k in range(2)]
        XT = [x.rearrange("p (c t) -> p c t", c=DC) for x in XT]
        Y = sb("Y", [P, DC, T])
        cst = sb("cst", [P, DC, 11])
        with ExitStack() as ctx1:
            sb1 = lambda n, s, d=F32: ctx1.enter_context(nc.sbuf_tensor(f"hy_{n}", s, d))
            pad = sb1("pad", [P, 2, GS, P + 2])
            K = sb1("K", [P, GT])
            Vv = sb1("Vv", [P, GT])
            KVh, KVl = sb1("KVh", [P, 2, P, B], F16), sb1("KVl", [P, 2, P, B], F16)
            W4 = [t[:, :].rearrange("p (c m n) -> p c m n", c=DC, m=3) for t in Wq]
            RAW = KVh[:, 1, :, :].rearrange("p c b -> p (c b)").bitcast(F32)
            PAIR = KVl[:, 1, :, :].rearrange("p c b -> p (c b)").rearrange("p (k n) -> p k n", k=2)
            AT_GROUP = {0: 1, 1: 2, NG - 2: 3, NG - 1: 4}
            piece_loaded, ph_made, pl_made, w_stored = sem("piece_loaded"), sem("ph_made"), sem("pl_made"), sem("w_stored")
            NQ = 2
            TP = sb1("TP", [P, NQ, 2, P, CT], F16)
            xT = w["xT"].rearrange("p (c t) -> p c t", c=DC)
            xT_loaded, xh_ready, xl_ready = [sem(f"xT_loaded{h}") for h in range(2)], sem("xh_ready"), sem("xl_ready")
            loaded, w_loaded, zeros_set = sem("loaded"), sem("w_loaded"), sem("zeros_set")
            waits_apart = sem("waits_apart")
            qkv_psum, qk_padded, v_ready = sem("qkv_psum"), sem("qk_padded"), sem("v_ready")
            q_tap, k_tap, kv_ready = sem("q_tap"), sem("k_tap"), sem("kv_ready")
            kvT_psum, kvh_ready, kvl_ready = sem("kvT_psum"), sem("kvh_ready"), sem("kvl_ready")
            t_loaded = [sem(f"t_loaded{u}") for u in range(NQ)]
            c_psum, c_ready, cT_psum, gated = sem("c_psum"), sem("c_ready"), sem("cT_psum"), sem("gated")
            cs = lambda cc, n: cst[:, cc, n:n + 1]

            with nc.Block() as block:
                HALF = NG // 2

                def half(eng, part):
                    if eng is nc.tensor:
                        for i in range(HALF):
                            part(i)
                    else:
                        part(0)
                        with eng.Fori(0, HALF - 1) as i:
                            part(i + 1)

                def groups(eng, cc, work, convolve, gate):
                    if cc == 0:
                        work(0, lambda: None)
                        work(1, lambda: None)
                        with eng.Fori(0, NG // 2 - 2) as i:
                            for u in range(2):
                                work(i * 2 + (2 + u), lambda: None, u)
                        work(NG - 2, lambda: None)
                        work(NG - 1, lambda: None)
                    else:
                        half(eng, lambda i: work(i, lambda: [convolve(cc - 1, i, u) for u in range(NQ)]))
                        half(eng, lambda i: work(i + HALF, lambda: [gate(cc - 1, i, u) for u in range(2)]))

                def group_before(cc, i):
                    if type(i) is int and i == 0:
                        return (cc - 1, NG - 1) if cc else None
                    return cc, i - 1

                def x_ahead(i, u, split):
                    if type(i) is not int:
                        split(i + 2, u)
                    elif i + 2 < NG:
                        split(i + 2, i % 2)

                def last_chunk(eng, convolve, gate):
                    half(eng, lambda i: [convolve(DC - 1, i, u) for u in range(NQ)])
                    half(eng, lambda i: [gate(DC - 1, i, u) for u in range(2)])

                @block.gpsimd
                def _(pool):
                    for n in range(1, DC + 1):
                        p, q = PIECES[n]
                        if n > 1:
                            pool.wait_ge(pl_made, n - 1)
                        pool.dma_start(RAW[:, 0:q - p], w["wqkv"][:, p:q] if n < DC else w["WoT_hy"]).then_inc(piece_loaded, 16)
                        for k, made in enumerate((ph_made, pl_made)):
                            pool.wait_ge(made, n)
                            pool.dma_start(wpair[k, :, p:q], PAIR[:, k, 0:q - p]).then_inc(w_stored, 16)
                    pool.wait_ge(w_stored, 32 * DC)

                @block.sync
                def _(sp):

                    def load_w(cc):
                        for k in range(2):
                            sp.dma_start(Wq[k][:, :], wpair[k, :, cc * WQ:(cc + 1) * WQ]).then_inc(w_loaded, 16)

                    def load_t(cc, i, u):
                        for k in range(2):
                            src = bass.AP(tensor=taps.tensor, offset=taps.offset + ((k * DC + cc) * NCT + NQ * i + u) * (LC * CT),
                                          ap=[[CT, P], [1, P * CT]])
                            sp.dma_start(TP[:, u, k, :, :].rearrange("p t c -> p (t c)"), src).then_inc(t_loaded[u], 16)

                    sp.dma_start(cst[:, :, :].rearrange("p a n -> p (a n)"), w["cst"]).then_inc(loaded, 16)

                    def load_x(i, h):
                        sp.dma_start(stage[:, h, :, :], xT[:, :, ds(i * GT, GT)]).then_inc(xT_loaded[h], 16)

                    for u in range(NQ):
                        load_t(0, 0, u)
                    with sp.Fori(0, NG // 2 - 1) as i:
                        for h in range(2):
                            sp.wait_ge(xl_ready, 2 * i + h + 1)
                            load_x(i * 2 + (2 + h), h)
                    for cc in range(DC):
                        if cc + 1 < DC:
                            sp.wait_ge(qkv_psum, 3 * NG * (cc + 1))
                            sp.wait_ge(w_stored, 32 * (cc + 1))
                            load_w(cc + 1)
                        with sp.Fori(0, NCT // NQ - 1) as i:
                            for u in range(NQ):
                                sp.wait_ge(c_psum, NCT * cc + NQ * i + u + 1)
                                load_t(cc, i + 1, u)
                        if cc + 1 < DC:
                            for u in range(NQ):
                                sp.wait_ge(c_psum, NCT * (cc + 1) - NQ + u + 1)
                                load_t(cc + 1, 0, u)

                @block.tensor
                def _(pe):

                    def convolve(cc, i, u):
                        q = NQ * i + u
                        if q == 0:
                            pe.wait_ge(kvl_ready, NG * (cc + 1))
                        pe.wait_ge(t_loaded[u], (NCT // NQ * cc + i + 1) * 32)
                        if cc or q >= 2:
                            pe.wait_ge(c_ready, NCT * cc + q - 1)
                        for c in range(CT):
                            out = bank[4 + u % 2][:, c * B:(c + 1) * B]
                            h, l = (kv[:, cc % 2, q * CT + c, :] for kv in (KVh, KVl))
                            pe.matmul(out, TP[:, u, 0, :, c], h, start=True, stop=False)
                            pe.matmul(out, TP[:, u, 1, :, c], h, start=False, stop=False)
                            t = pe.matmul(out, TP[:, u, 0, :, c], l, start=False, stop=True)
                        t.then_inc(c_psum, 1)

                    def turn_kv(n):
                        pe.wait_ge(kv_ready, n + 1)
                        pe.wait_ge(kvl_ready, n)
                        for j in range(GS):
                            t = pe.transpose(bank[3][:, j * P:(j + 1) * P], K[:, j * P:(j + 1) * P], idf[:, :])
                        t.then_inc(kvT_psum, 1)

                    def turn_back(cc, i, u):
                        g = 2 * i + u
                        pe.wait_ge(c_ready, NCT * cc + NCT)
                        if cc or g >= 2:
                            pe.wait_ge(gated, NG * cc + g - 1)
                        for j in range(GS):
                            t = pe.transpose(bank[6 + u][:, j * P:(j + 1) * P], C[:, GS * g + j, :], flip[:, :])
                        t.then_inc(cT_psum, 1)

                    for cc in range(DC):
                        if cc:
                            wait_apart(pe, waits_apart, w_loaded, 32 * cc)

                        def work(i, beside, u=None):
                            n = cc * NG + i
                            if cc == 0:
                                wait_apart(pe, waits_apart, xh_ready, i + 1)
                                wait_apart(pe, waits_apart, xl_ready, i + 1)
                            for m in range(3):
                                pe.wait_ge(v_ready, n) if m == 2 else pe.wait_ge(qk_padded, 2 * n)
                                k = 0
                                for c in range(DC):
                                    for ww, x in ((W4[0], XT[0]), (W4[0], XT[1]), (W4[1], XT[0])):
                                        t = pe.matmul(bank[m][:, :], ww[:, c, m, :], x[:, c, ds(i * GT, GT)], start=(k == 0),
                                                      stop=(k == 3 * DC - 1))
                                        k += 1
                                t.then_inc(qkv_psum, 1)
                                if m == 0 and group_before(cc, i):
                                    turn_kv(n - 1)
                            beside()

                        groups(pe, cc, work, convolve, turn_back)
                    turn_kv(DC * NG - 1)
                    last_chunk(pe, convolve, turn_back)

                @block.scalar
                def _(act):

                    def c_out(cc, i, u):
                        q = NQ * i + u
                        act.wait_ge(c_psum, NCT * cc + q + 1)
                        act.wait_ge(cT_psum, NG * cc)
                        act.activation(C[:, :, ds(q * CT, CT)].rearrange("p b c -> p c b"),
                                       bank[4 + u % 2][:, 0:CT * B].rearrange("p (c b) -> p c b", c=CT), ACT.Copy,
                                       scale=1.0 / WS).then_inc(c_ready, 1)

                    def x_hi(i, h):
                        if type(i) is not int or i >= 2:
                            act.wait_ge(xT_loaded[h], (i - h) * 8)
                        act.activation(XT[0][:, :, ds(i * GT, GT)], stage[:, h, :, :], ACT.Copy).then_inc(xh_ready, 1)

                    def kv_hi(cc, i):
                        act.wait_ge(kvT_psum, NG * cc + i + 1)
                        if cc >= 2:
                            act.wait_ge(c_psum, NCT * (cc - 1))
                        elif cc == 1:
                            act.wait_ge(w_stored, 32 * DC)
                        act.activation(KVh[:, cc % 2, :, ds(i * GS, GS)].rearrange("p c j -> p j c"),
                                       bank[3][:, :].rearrange("p (j c) -> p j c", j=GS), ACT.Copy).then_inc(kvh_ready, 1)

                    act.wait_ge(loaded, 16)
                    act.wait_ge(zeros_set, 1)
                    x_hi(0, 0)
                    x_hi(1, 1)
                    for cc in range(DC):

                        def work(i, beside, u=None):
                            n = cc * NG + i
                            for m, taken in enumerate((q_tap, k_tap)):
                                act.wait_ge(qkv_psum, 3 * n + m + 1)
                                act.wait_ge(taken, 3 * n)
                                act.activation(pad[:, m, :, 2:P + 2], bank[m][:, :].rearrange("p (j t) -> p j t", j=GS),
                                               ACT.Identity, bias=cs(cc, m), scale=1.0 / WS).then_inc(qk_padded, 1)
                                if m == 0 and group_before(cc, i):
                                    kv_hi(*group_before(cc, i))
                            act.wait_ge(qkv_psum, 3 * n + 3)
                            act.wait_ge(kv_ready, n)
                            act.activation(Vv[:, :], bank[2][:, :], ACT.Identity, bias=cs(cc, 2), scale=1.0 / WS)\
                               .then_inc(v_ready, 1)
                            beside()
                            if cc == 0:
                                x_ahead(i, u, x_hi)
                            if cc == 0 and type(i) is int and i in AT_GROUP:
                                n = AT_GROUP[i]
                                c = PIECES[n][1] - PIECES[n][0]
                                act.wait_ge(piece_loaded, 16 * n)
                                if n > 1:
                                    act.wait_ge(w_stored, 32 * (n - 1))
                                act.activation(PAIR[:, 0, 0:c], RAW[:, 0:c], ACT.Copy, scale=WS).then_inc(ph_made, 1)

                        groups(act, cc, work, c_out, lambda cc, i, u: None)
                    kv_hi(DC - 1, NG - 1)
                    with act.Fori(0, HALF) as i:
                        for u in range(NQ):
                            c_out(DC - 1, i, u)

                @block.vector
                def _(dve):

                    def gate(cc, i, u):
                        g = 2 * i + u
                        dve.wait_ge(cT_psum, NG * cc + g + 1)
                        y = Y[:, cc, ds(g * GT, GT)]
                        dve.tensor_tensor(y, bank[6 + u][:, :], y, ALU.mult).then_inc(gated, 1)

                    def x_lo(i, h):
                        dve.wait_ge(xh_ready, i + 1)
                        if type(i) is not int or i >= 2:
                            dve.wait_ge(xT_loaded[h], (i - h) * 8)
                        dve.tensor_tensor(XT[1][:, :, ds(i * GT, GT)], stage[:, h, :, :], XT[0][:, :, ds(i * GT, GT)], ALU.subtract)\
                           .then_inc(xl_ready, 1)

                    def kv_lo(cc, i):
                        n = NG * cc + i
                        dve.wait_ge(kvT_psum, n + 1)
                        dve.wait_ge(kvh_ready, n + 1)
                        b4 = ds(i * GS, GS)
                        dve.tensor_tensor(KVl[:, cc % 2, :, b4].rearrange("p c j -> p j c"),
                                          bank[3][:, :].rearrange("p (j c) -> p j c", j=GS),
                                          KVh[:, cc % 2, :, b4].rearrange("p c j -> p j c"), ALU.subtract).then_inc(kvl_ready, 1)

                    dve.memset(pad[:, :, :, 0:2], 0.0).then_inc(zeros_set, 1)
                    dve.wait_ge(loaded, 16)
                    x_lo(0, 0)
                    x_lo(1, 1)
                    for cc in range(DC):

                        def work(i, beside, u=None):
                            n = cc * NG + i
                            yq = Y[:, cc, ds(i * GT, GT)].rearrange("p (j t) -> p j t", j=GS)
                            for m, (to, taken) in enumerate(((yq, q_tap), (K[:, :].rearrange("p (j t) -> p j t", j=GS), k_tap))):
                                dve.wait_ge(qk_padded, 2 * n + m + 1)
                                if m:
                                    if group_before(cc, i):
                                        kv_lo(*group_before(cc, i))
                                    dve.wait_ge(kvT_psum, n)
                                dve.tensor_scalar(to, pad[:, m, :, 2:P + 2], cs(cc, 3 + 4 * m + 2), cs(cc, 3 + 4 * m + 3),
                                                  ALU.mult, ALU.add).then_inc(taken, 1)
                                for s in (1, 0):
                                    dve.wait_ge(taken, 3 * n + 2 - s)
                                    dve.scalar_tensor_tensor(to, pad[:, m, :, s:P + s], cs(cc, 3 + 4 * m + s), to,
                                                             ALU.mult, ALU.add).then_inc(taken, 1)
                            dve.wait_ge(k_tap, 3 * n + 3)
                            dve.wait_ge(v_ready, n + 1)
                            dve.tensor_tensor(K[:, :], K[:, :], Vv[:, :], ALU.mult).then_inc(kv_ready, 1)
                            beside()
                            if cc == 0:
                                x_ahead(i, u, x_lo)
                            if cc == 0 and type(i) is int and i in AT_GROUP:
                                n = AT_GROUP[i]
                                c = PIECES[n][1] - PIECES[n][0]
                                dve.wait_ge(ph_made, n)
                                if n > 1:
                                    dve.wait_ge(w_stored, 32 * (n - 1))
                                dve.scalar_tensor_tensor(PAIR[:, 1, 0:c], RAW[:, 0:c], WS, PAIR[:, 0, 0:c], ALU.mult, ALU.subtract)\
                                   .then_inc(pl_made, 1)

                        groups(dve, cc, work, lambda cc, i, u: None, gate)
                    kv_lo(DC - 1, NG - 1)
                    with dve.Fori(0, HALF) as i:
                        for u in range(2):
                            gate(DC - 1, i, u)

        with ExitStack() as ctx2:
            sb2 = lambda n, s, d=F32: ctx2.enter_context(nc.sbuf_tensor(f"hy_{n}", s, d))
            Woh, Wol = sb2("Woh", [P, DC * D], F16), sb2("Wol", [P, DC * D], F16)
            bo = sb2("bo", [P, D])
            Yh, Yl = sb2("Yh", [P, 2, DC, GT], F16), sb2("Yl", [P, 2, DC, GT], F16)
            norm = Norm(nc, ctx2, "hy_norm")
            x_loaded = [sem(f"x_loaded{k}") for k in range(NG)]
            wo_loaded, bo_loaded, biased = sem("wo_loaded"), sem("bo_loaded"), sem("biased")
            yh_ready, yl_ready, o_psum = sem("yh_ready"), sem("yl_ready"), sem("o_psum")

            with nc.Block() as block:

                @block.sync
                def _(sp):
                    for k, to in enumerate((Woh, Wol)):
                        sp.dma_start(to[:, :], wpair[k, :, PIECES[DC][0]:PIECES[DC][1]]).then_inc(wo_loaded, 16)
                    sp.dma_start(bo[:, :], w["bo"].partition_broadcast(P)).then_inc(bo_loaded, 16)
                    for k in range(NG):
                        sp.dma_start(X[:, GS * k:GS * k + GS, :].rearrange("p b n -> p (b n)"),
                                     w["x"][:, GS * k * D:(GS * k + GS) * D]).then_inc(x_loaded[k], 16)

                @block.gpsimd
                def _(pool):
                    norm_consts(pool, norm)
                    pool.wait_ge(bo_loaded, 16)
                    for i in range(NG):
                        pool.wait_ge(x_loaded[i], 16)
                        for j in range(GS):
                            x = X[:, GS * i + j, :]
                            pool.tensor_tensor(x, x, bo[:, :], ALU.add).then_inc(biased, 1)
                        norm_rstd(pool, norm, i)

                @block.scalar
                def _(act):
                    for i in range(NG):
                        if i >= 2:
                            act.wait_ge(o_psum, GS * (i - 1))
                        act.activation(Yh[:, i % 2, :, :], Y[:, :, i * GT:(i + 1) * GT], ACT.Copy).then_inc(yh_ready, 1)

                @block.tensor
                def _(pe):
                    pe.wait_ge(wo_loaded, 32)
                    for i in range(NG):
                        pe.wait_ge(yh_ready, i + 1)
                        pe.wait_ge(yl_ready, i + 1)
                        for j in range(GS):
                            if i:
                                pe.wait_ge(norm.rows_ready, GS * (i - 1) + j + 1)
                            k = 0
                            for c in range(DC):
                                for y, ww in ((Yh, Woh), (Yl, Woh), (Yh, Wol)):
                                    t = pe.matmul(bank[j][:, :], y[:, i % 2, c, j * P:(j + 1) * P], ww[:, c * D:(c + 1) * D],
                                                  start=(k == 0), stop=(k == 3 * DC - 1))
                                    k += 1
                            t.then_inc(o_psum, 1)

                @block.vector
                def _(dve):

                    def split(i):
                        dve.wait_ge(yh_ready, i + 1)
                        if i >= 2:
                            dve.wait_ge(o_psum, GS * (i - 1))
                        dve.tensor_tensor(Yl[:, i % 2, :, :], Y[:, :, i * GT:(i + 1) * GT], Yh[:, i % 2, :, :], ALU.subtract)\
                           .then_inc(yl_ready, 1)

                    split(0)
                    for i in range(NG):
                        if i + 1 < NG:
                            split(i + 1)
                        for j in range(GS):
                            dve.wait_ge(o_psum, GS * i + j + 1)
                            dve.wait_ge(biased, GS * i + j + 1)
                            x = X[:, GS * i + j, :]
                            dve.scalar_tensor_tensor(x, bank[j][:, :], 1.0 / WS, x, ALU.mult, ALU.add).then_inc(norm.rows_ready, 1)
                        for j in range(GS):
                            norm_stats(dve, norm, X, i, j)
                        for j in range(GS):
                            norm_aggr(dve, norm, i, j)
                        for j in range(GS):
                            norm_apply(dve, norm, X, i, j)


def decoder(nc, a, out):
    with ExitStack() as ctx:
        X = ctx.enter_context(nc.sbuf_tensor("X", [P, B, D], F32))
        taps = nc.dram_tensor("taps", [2, D // CT, LC, CT], F16, kind="Internal").ap()
        wpair = nc.dram_tensor("wpair", [2, P, PIECES[-1][1]], F16, kind="Internal").ap()
        kd = nc.dram_tensor("k", [SL * HD, B, KH * P], F16, kind="Internal").ap()
        vd = nc.dram_tensor("v", [P, B, VS], F32, kind="Internal").ap()

        idh = ctx.enter_context(nc.sbuf_tensor("idh", [P, P], F16))
        idf = ctx.enter_context(nc.sbuf_tensor("idf", [P, P], F32))
        with nc.cleanup_on_exit(), ExitStack() as stage:
            flip = stage.enter_context(nc.sbuf_tensor("flip", [P, P], F32))
            Wq = [stage.enter_context(nc.sbuf_tensor(n, [P, WQ], F16)) for n in ("Wq_hi", "Wq_lo")]
            C = stage.enter_context(nc.sbuf_tensor("hy_C", [P, B, P], F32))
            groups = C[:, :, :].rearrange("p b n -> p (b n)").rearrange("p (h c t) -> p h c t", h=2, c=DC)
            prepare(nc, X, a, groups, taps, Wq, kd, vd, [(idh[:, :], a["idh"]), (idf[:, :], a["idf"]), (flip[:, :], a["flip"])])
            hyena(nc, X, a, C, groups, taps, Wq, wpair, idf, flip)
        with ExitStack() as weights:
            raw = weights.enter_context(nc.sbuf_tensor("ffn_raw", [P, 2, DC * FF], F32))
            with nc.cleanup_on_exit():
                cross_attention(nc, "xa", X, kd, vd, idh, a["nsel"], a["gmask"], prefetch=[(raw[:, 0, :], a["w0T"]), (raw[:, 1, :], a["w1T"])])
            with nc.cleanup_on_exit():
                ffn(nc, X, raw, a["bias0"], a["bias1"], idh)
        with ExitStack() as weights:
            W12h, W12l = (weights.enter_context(nc.sbuf_tensor(n, [P, NE * W12E], F16)) for n in ("W12h", "W12l"))
            with nc.cleanup_on_exit():
                latent_attention(nc, X, a, idf, (a["mw12"], W12h, W12l))
            tri, mc, rw, empty = (weights.enter_context(nc.sbuf_tensor(f"moe_{n}", list(a[n].shape), a[n].dtype))
                           for n in ("tri", "mc", "rw", "empty"))
            with nc.cleanup_on_exit():
                cross_attention(nc, "xb", X, kd, vd, idh, a["nsel"], a["gmask"],
                                prefetch=[(tri[:, :], a["tri"]), (mc[:, :], a["mc"]), (rw[:, :], a["rw"]),
                                          (empty[:, :], a["empty"])])
            with nc.cleanup_on_exit():
                moe(nc, X, W12h, W12l, a["mw3"], rw[:, :], idh, idf, tri, mc, empty, out)



def _layout(np, i):
    c = np.ascontiguousarray

    def rows(w):
        n = w.shape[0] // P
        return c(w.reshape(n, P, -1).transpose(1, 0, 2).reshape(P, -1))

    def by_channel(v):
        return v.reshape(DC, P).T

    a = {}
    x = i["x"]
    a["x"] = c(x.transpose(1, 0, 2).reshape(P, -1))
    a["xT"] = rows(c(x.transpose(2, 0, 1)).reshape(D, -1))
    a["ctx"] = c(i["ctx_512"].transpose(1, 0, 2).reshape(P, -1))
    w = np.stack([i["L0_attn_Wq"].T, i["L0_attn_Wk"].T, i["L0_attn_Wv"].T], 1)
    a["wqkv"] = c(w.reshape(DC, P, 3, DC, P).transpose(1, 3, 0, 2, 4).reshape(P, -1))
    qw, kw = i["L0_attn_convq_w"], i["L0_attn_convk_w"]
    per_channel = [i["L0_attn_bq"], i["L0_attn_bk"], i["L0_attn_bv"], qw[:, 0, 0], qw[:, 0, 1], qw[:, 0, 2],
                   i["L0_attn_convq_b"], kw[:, 0, 0], kw[:, 0, 1], kw[:, 0, 2], i["L0_attn_convk_b"]]
    a["cst"] = c(np.stack([by_channel(v) for v in per_channel], 2).reshape(P, -1))
    ker = i["L0_attn_ssm_kernel"]
    a["kerT"] = rows(np.concatenate([ker[:, :P][:, ::-1], ker[:, P:LC][:, ::-1]], 1).T)
    a["dskip"] = np.zeros((P, D), x.dtype)
    a["dskip"][P - 1] = i["L0_attn_D_skip"]
    a["WoT_hy"] = rows(i["L0_attn_Wo"].T)
    a["bo"] = i["L0_attn_bo"]
    a["w0T"] = c(rows(i["L0_ffn_W0"].T).reshape(P, DC, FC, P).transpose(0, 2, 1, 3).reshape(P, -1))
    a["w1T"] = rows(i["L0_ffn_W1"].T)
    a["bias0"] = c(i["L0_ffn_bias0"].reshape(FC, P).T)
    a["bias1"] = i["L0_ffn_bias1"]
    q, kv = i["L1_attn_W_q_comp"], i["L1_attn_W_kv_comp"]

    def halves_swapped(m):
        return np.concatenate([m[DCMP // 2:], m[:DCMP // 2]], 0)

    k = kv[:DCMP]
    a["Wkv"] = i["L1_attn_W_to_kv"]
    a["WoT"] = c(i["L1_attn_W_out_res"].T)
    a["WcT"] = c(i["L1_attn_W_compress"].T)
    qs, ks = halves_swapped(q), halves_swapped(k)

    def zeros_below(m):
        return np.concatenate([m, np.zeros_like(m)], 0)

    a["Wqk"] = zeros_below(np.concatenate([q.T, qs.T, k.T, ks.T, ks.T, k.T], 1))
    a["WvT"] = zeros_below(kv[DCMP:].T)
    a["Wl"] = i["L1_attn_W_comp2lat"]
    a["gb"] = c(np.stack([i["L1_attn_ln_gamma"], i["L1_attn_ln_beta"]], 1))
    a["bout"] = i["L1_attn_b_out_res"]
    up = np.stack([i["L1_ffn_w1"], i["L1_ffn_w2"]], 2)
    a["mw12"] = c(up.reshape(NE, DC, P, 2 * FE).transpose(2, 0, 1, 3).reshape(P, -1))
    a["mw3"] = c(i["L1_ffn_w3"].reshape(NE, FE // P, P, D).transpose(2, 0, 1, 3).reshape(P, -1))
    a["rw"] = rows(i["L1_ffn_router_w"].T)
    f32, f16 = np.float32, np.float16
    a["idf"], a["idh"], a["flip"] = np.eye(P, dtype=f32), np.eye(P, dtype=f16), c(np.eye(P, dtype=f32)[:, ::-1])
    inv = (1.0 / (10000.0 ** (np.arange(0, DCMP, 2, dtype=f32) / DCMP))).astype(f32)
    angle = np.arange(P, dtype=f32)[:, None] * inv[None, :]
    cos = np.concatenate([np.cos(angle), np.cos(angle)], 1).T
    sin = np.concatenate([-np.sin(angle), np.sin(angle)], 1).T
    cos, sin = np.tile(cos, (1, GS)), np.tile(sin, (1, GS))
    a["rope"] = np.concatenate([np.concatenate([cos, sin], 1), np.concatenate([sin, cos], 1)], 0).astype(f32)
    a["mask"] = np.where(np.tril(np.ones((P, P), bool)), 0, -1e30).astype(f32)
    nsel, gmask = np.zeros((QH, KH, P), f16), np.zeros((QH, QG, P), f16)
    for h in range(QH):
        nsel[h, h // QG] = -1
        gmask[h, ORDER.index(h % QG)] = 1
    a["nsel"], a["gmask"] = nsel.reshape(QH, -1), gmask.reshape(QH, -1)
    t = np.arange(P)
    a["tri"] = np.concatenate([t[:, None] < t[None, :], np.ones((P, P), bool)], 1).astype(f16)
    e = np.arange(NE)
    row = np.concatenate([e, e * EROWS, np.arange(B) * P, (e[None, :] <= e[:, None]).reshape(-1), np.arange(NTILE)])
    a["mc"] = np.concatenate([np.tile(row, (P, 1)), t[:, None], t[:, None] + B * P], 1).astype(f32)
    column = np.arange(ZTILE)
    zone = np.where(column < NE * ETILE, column // ETILE, NE + np.minimum(column - NE * ETILE, NTILE - 1))
    a["empty"] = c((NR * B * P + zone[:, None] * P + t[None, :]).reshape(P, ZTILE)).astype(f32)
    return a


def kernel(**inputs):
    import numpy as np
    import concourse.bacc as bacc
    from concourse.bass_utils import run_bass_kernel_spmd

    nc = bacc.Bacc("TRN2", target_bir_lowering=False, num_devices=1)
    arrays = _layout(np, {n: np.asarray(v) for n, v in inputs.items()})
    aps = {n: nc.dram_tensor(f"in_{n}", v.shape, mybir.dt.from_np(v.dtype), kind="ExternalInput").ap()
           for n, v in arrays.items()}
    out = nc.dram_tensor("out_0", (P, B * D), F32, kind="ExternalOutput").ap()
    decoder(nc, aps, out)
    r = run_bass_kernel_spmd(nc, [{f"in_{n}": v for n, v in arrays.items()}], core_ids=[0])
    y = r.results[0]["out_0"]
    return np.ascontiguousarray(y.reshape(P, B, D).transpose(1, 0, 2))
```
